# Optimizing a Trainium2 kernel written in Bass

```python
import numpy as np
import jax
import jax.numpy as jnp

def _softmax(x, axis=-1):
    return jax.nn.softmax(x, axis=axis)

def _gelu(x):
    return jax.nn.gelu(x, approximate=True)

def _silu(x):
    return jax.nn.silu(x)

def _sigmoid(x):
    return jax.nn.sigmoid(x)

def _layernorm(x, axis=-1, eps=1e-05):
    m = jnp.mean(x, axis=axis, keepdims=True)
    v = jnp.var(x, axis=axis, keepdims=True)
    return (x - m) / jnp.sqrt(v + eps)

def _scatter_add(tgt, idx, src, axis=0):
    return tgt.at[idx].add(src)

def _segment_sum(src, seg, n):
    return jax.ops.segment_sum(src, seg, n)
kernel_name = 'mk_conv_attn_hybrid_d2_conv_nhwc256_r4_e3a4cd'

def setup_inputs(seed: int=0):
    np.random.seed(seed)
    _w = jnp.asarray

    def _rec_inputs():
        import jax
        import jax.numpy as jnp
        _gk = jax.random.key(seed)
        x = -0.0002023 + 1 * jax.random.normal(jax.random.fold_in(_gk, 1), (8, 56, 56, 64), jnp.float32)
        return x
    x = _rec_inputs()

    def _L0_conv_setup():
        import jax, jax.numpy as jnp
        import numpy as np
        P = 32
        C = 64
        D = 4
        EPS = 0.001

        def _bn(x, g, b, m, v):
            return g * (x - m) * jax.lax.rsqrt(v + EPS) + b

        def _path(x, w1, b1, g1, be1, m1, v1, w2, b2, g2, be2, m2, v2, w3, b3, g3, be3, m3, v3):
            h = jnp.einsum('nhwc,cd->nhwd', x, w1) + b1
            h = jax.nn.relu(_bn(h, g1, be1, m1, v1))
            h = jax.lax.conv_general_dilated(h, w2, window_strides=(1, 1), padding='SAME', dimension_numbers=('NHWC', 'HWIO', 'NHWC')) + b2
            h = jax.nn.relu(_bn(h, g2, be2, m2, v2))
            h = jnp.einsum('nhwd,dc->nhwc', h, w3) + b3
            h = jax.nn.relu(_bn(h, g3, be3, m3, v3))
            return h
        key = jax.random.key(seed)
        ks = jax.random.split(key, 24)

        def nrm(k, shape, s=0.05):
            return jax.random.normal(k, shape, dtype=jnp.float32) * s
        inp = {}
        inp['x'] = jax.random.normal(ks[0], (8, 56, 56, C), dtype=jnp.float32)
        inp['W1'] = nrm(ks[1], (P, C, D))
        inp['B1'] = nrm(ks[2], (P, D))
        inp['W2'] = nrm(ks[3], (P, 3, 3, D, D))
        inp['B2'] = nrm(ks[4], (P, D))
        inp['W3'] = nrm(ks[5], (P, D, C))
        inp['B3'] = nrm(ks[6], (P, C))
        inp['G1'] = 1.0 + nrm(ks[7], (P, D))
        inp['Be1'] = nrm(ks[8], (P, D))
        inp['M1'] = nrm(ks[9], (P, D))
        inp['V1'] = 1.0 + 0.1 * jax.random.uniform(ks[10], (P, D), dtype=jnp.float32)
        inp['G2'] = 1.0 + nrm(ks[11], (P, D))
        inp['Be2'] = nrm(ks[12], (P, D))
        inp['M2'] = nrm(ks[13], (P, D))
        inp['V2'] = 1.0 + 0.1 * jax.random.uniform(ks[14], (P, D), dtype=jnp.float32)
        inp['G3'] = 1.0 + nrm(ks[15], (P, C))
        inp['Be3'] = nrm(ks[16], (P, C))
        inp['M3'] = nrm(ks[17], (P, C))
        inp['V3'] = 1.0 + 0.1 * jax.random.uniform(ks[18], (P, C), dtype=jnp.float32)
        return inp
    _L0_conv_all = _L0_conv_setup()
    _L0_conv_in = {k: v for k, v in _L0_conv_all.items() if k in ('W1', 'B1', 'G1', 'Be1', 'M1', 'V1', 'W2', 'B2', 'G2', 'Be2', 'M2', 'V2', 'W3', 'B3', 'G3', 'Be3', 'M3', 'V3')}
    del _L0_conv_all

    def _L1_attn_setup():
        import jax, jax.numpy as jnp
        import numpy as np
        import math
        B, N, DIM = (2, 1024, 64)
        NUM_HEADS = 8
        HEAD_DIM = DIM // NUM_HEADS
        WINDOW = 7

        def local_mask(seq_len: int, window_size: int=WINDOW) -> jnp.ndarray:
            grid = int(math.isqrt(seq_len))
            idx = jnp.arange(seq_len)
            row, col = (idx // grid, idx % grid)
            half = window_size // 2
            ok_row = jnp.abs(row[:, None] - row[None, :]) <= half
            ok_col = jnp.abs(col[:, None] - col[None, :]) <= half
            return ok_row & ok_col
        key = jax.random.key(seed)
        k1, k2, k3, k4 = jax.random.split(key, 4)
        x = jax.random.normal(k1, (B, N, DIM), dtype=jnp.float32)
        W_qkv = jax.random.normal(k2, (3 * DIM, DIM), dtype=jnp.float32) * DIM ** (-0.5)
        W_proj = jax.random.normal(k3, (DIM, DIM), dtype=jnp.float32) * DIM ** (-0.5)
        b_proj = jax.random.normal(k4, (DIM,), dtype=jnp.float32) * 0.01
        temperature = jnp.ones((1,), dtype=jnp.float32)
        return {'x': x, 'W_qkv': W_qkv, 'W_proj': W_proj, 'b_proj': b_proj, 'temperature': temperature}
    _L1_attn_all = _L1_attn_setup()
    _L1_attn_in = {k: v for k, v in _L1_attn_all.items() if k in ('W_qkv', 'W_proj', 'b_proj', 'temperature')}
    del _L1_attn_all

    def _L1_ffn_setup():
        import jax, jax.numpy as jnp
        import numpy as np
        B, N, D = (16, 1024, 64)
        NUM_EXPERTS, TOP_K, HEADS = (4, 2, 4)
        N_EDGES = 262144
        LN_EPS = 1e-05

        def _layernorm(x, g, b):
            mu = x.mean(-1, keepdims=True)
            var = ((x - mu) ** 2).mean(-1, keepdims=True)
            return (x - mu) * jax.lax.rsqrt(var + LN_EPS) * g + b

        def _forward(x, edge_index, W_gat, att_src, att_dst, b_gat, ln_gamma, ln_beta, W1, b1, W2, b2):
            Bc, Nc, Dc = x.shape
            M = Bc * Nc
            x_flat = x.reshape(M, Dc)
            h = (x_flat @ W_gat).reshape(M, HEADS, NUM_EXPERTS)
            loops = jnp.arange(M, dtype=edge_index.dtype)
            src = jnp.concatenate([edge_index[0], loops])
            dst = jnp.concatenate([edge_index[1], loops])
            a_src = (h * att_src).sum(-1)
            a_dst = (h * att_dst).sum(-1)
            e = jax.nn.leaky_relu(a_src[src] + a_dst[dst], negative_slope=0.2)
            e_max = jax.ops.segment_max(e, dst, num_segments=M)
            ee = jnp.exp(e - e_max[dst])
            denom = jax.ops.segment_sum(ee, dst, num_segments=M)
            alpha = ee / (denom[dst] + 1e-16)
            msg = h[src] * alpha[:, :, None]
            agg = jax.ops.segment_sum(msg, dst, num_segments=M).reshape(M, HEADS * NUM_EXPERTS) + b_gat
            scores = _layernorm(agg, ln_gamma, ln_beta).reshape(M, HEADS, NUM_EXPERTS).mean(1)
            scores = scores.reshape(Bc, Nc, NUM_EXPERTS)
            topk_s, topk_i = jax.lax.top_k(scores, TOP_K)
            w = jax.nn.softmax(topk_s, axis=-1)
            out = jnp.zeros_like(x)
            for ei in range(NUM_EXPERTS):
                g = jnp.where(topk_i == ei, w, 0.0).sum(-1)
                hh = jax.nn.gelu(x @ W1[ei] + b1[ei], approximate=False)
                out = out + g[..., None] * (hh @ W2[ei] + b2[ei])
            return out
        key = jax.random.key(seed)
        ks = jax.random.split(key, 8)
        s = 0.05
        return {'x': jax.random.normal(ks[0], (B, N, D), jnp.float32), 'W_gat': jax.random.normal(ks[1], (D, HEADS * NUM_EXPERTS), jnp.float32) * s, 'att_src': jax.random.normal(ks[2], (HEADS, NUM_EXPERTS), jnp.float32) * s, 'att_dst': jax.random.normal(ks[3], (HEADS, NUM_EXPERTS), jnp.float32) * s, 'b_gat': jnp.zeros((HEADS * NUM_EXPERTS,), jnp.float32), 'ln_gamma': jnp.ones((HEADS * NUM_EXPERTS,), jnp.float32), 'ln_beta': jnp.zeros((HEADS * NUM_EXPERTS,), jnp.float32), 'W1': jax.random.normal(ks[4], (NUM_EXPERTS, D, 2 * D), jnp.float32) * s, 'b1': jnp.zeros((NUM_EXPERTS, 2 * D), jnp.float32), 'W2': jax.random.normal(ks[5], (NUM_EXPERTS, 2 * D, D), jnp.float32) * s, 'b2': jnp.zeros((NUM_EXPERTS, D), jnp.float32), 'edge_index': jax.random.randint(ks[6], (2, N_EDGES), 0, B * N, jnp.int32)}
    _L1_ffn_all = _L1_ffn_setup()
    _L1_ffn_in = {k: v for k, v in _L1_ffn_all.items() if k in ('W_gat', 'att_src', 'att_dst', 'b_gat', 'ln_gamma', 'ln_beta', 'W1', 'b1', 'W2', 'b2', 'edge_index')}
    del _L1_ffn_all
    return {'x': x, 'L0_conv_W1': _L0_conv_in['W1'], 'L0_conv_B1': _L0_conv_in['B1'], 'L0_conv_G1': _L0_conv_in['G1'], 'L0_conv_Be1': _L0_conv_in['Be1'], 'L0_conv_M1': _L0_conv_in['M1'], 'L0_conv_V1': _L0_conv_in['V1'], 'L0_conv_W2': _L0_conv_in['W2'], 'L0_conv_B2': _L0_conv_in['B2'], 'L0_conv_G2': _L0_conv_in['G2'], 'L0_conv_Be2': _L0_conv_in['Be2'], 'L0_conv_M2': _L0_conv_in['M2'], 'L0_conv_V2': _L0_conv_in['V2'], 'L0_conv_W3': _L0_conv_in['W3'], 'L0_conv_B3': _L0_conv_in['B3'], 'L0_conv_G3': _L0_conv_in['G3'], 'L0_conv_Be3': _L0_conv_in['Be3'], 'L0_conv_M3': _L0_conv_in['M3'], 'L0_conv_V3': _L0_conv_in['V3'], 'L1_attn_W_qkv': _L1_attn_in['W_qkv'], 'L1_attn_W_proj': _L1_attn_in['W_proj'], 'L1_attn_b_proj': _L1_attn_in['b_proj'], 'L1_attn_temperature': _L1_attn_in['temperature'], 'L1_ffn_W_gat': _L1_ffn_in['W_gat'], 'L1_ffn_att_src': _L1_ffn_in['att_src'], 'L1_ffn_att_dst': _L1_ffn_in['att_dst'], 'L1_ffn_b_gat': _L1_ffn_in['b_gat'], 'L1_ffn_ln_gamma': _L1_ffn_in['ln_gamma'], 'L1_ffn_ln_beta': _L1_ffn_in['ln_beta'], 'L1_ffn_W1': _L1_ffn_in['W1'], 'L1_ffn_b1': _L1_ffn_in['b1'], 'L1_ffn_W2': _L1_ffn_in['W2'], 'L1_ffn_b2': _L1_ffn_in['b2'], 'L1_ffn_edge_index': _L1_ffn_in['edge_index']}

def reference(x, L0_conv_W1, L0_conv_B1, L0_conv_G1, L0_conv_Be1, L0_conv_M1, L0_conv_V1, L0_conv_W2, L0_conv_B2, L0_conv_G2, L0_conv_Be2, L0_conv_M2, L0_conv_V2, L0_conv_W3, L0_conv_B3, L0_conv_G3, L0_conv_Be3, L0_conv_M3, L0_conv_V3, L1_attn_W_qkv, L1_attn_W_proj, L1_attn_b_proj, L1_attn_temperature, L1_ffn_W_gat, L1_ffn_att_src, L1_ffn_att_dst, L1_ffn_b_gat, L1_ffn_ln_gamma, L1_ffn_ln_beta, L1_ffn_W1, L1_ffn_b1, L1_ffn_W2, L1_ffn_b2, L1_ffn_edge_index):
    import jax
    import jax.numpy as jnp

    def _L0_conv_ref(x, W1, B1, G1, Be1, M1, V1, W2, B2, G2, Be2, M2, V2, W3, B3, G3, Be3, M3, V3):
        import jax, jax.numpy as jnp
        import numpy as np
        P = 32
        C = 64
        D = 4
        EPS = 0.001

        def _bn(x, g, b, m, v):
            return g * (x - m) * jax.lax.rsqrt(v + EPS) + b

        def _path(x, w1, b1, g1, be1, m1, v1, w2, b2, g2, be2, m2, v2, w3, b3, g3, be3, m3, v3):
            h = jnp.einsum('nhwc,cd->nhwd', x, w1) + b1
            h = jax.nn.relu(_bn(h, g1, be1, m1, v1))
            h = jax.lax.conv_general_dilated(h, w2, window_strides=(1, 1), padding='SAME', dimension_numbers=('NHWC', 'HWIO', 'NHWC')) + b2
            h = jax.nn.relu(_bn(h, g2, be2, m2, v2))
            h = jnp.einsum('nhwd,dc->nhwc', h, w3) + b3
            h = jax.nn.relu(_bn(h, g3, be3, m3, v3))
            return h
        paths = jax.vmap(_path, in_axes=(None,) + (0,) * 18)(x, W1, B1, G1, Be1, M1, V1, W2, B2, G2, Be2, M2, V2, W3, B3, G3, Be3, M3, V3)
        return jax.nn.relu(paths.sum(axis=0) + x)

    def _L1_attn_ref(x, W_qkv, W_proj, b_proj, temperature):
        import jax, jax.numpy as jnp
        import numpy as np
        import math
        B, N, DIM = (2, 1024, 64)
        NUM_HEADS = 8
        HEAD_DIM = DIM // NUM_HEADS
        WINDOW = 7

        def local_mask(seq_len: int, window_size: int=WINDOW) -> jnp.ndarray:
            grid = int(math.isqrt(seq_len))
            idx = jnp.arange(seq_len)
            row, col = (idx // grid, idx % grid)
            half = window_size // 2
            ok_row = jnp.abs(row[:, None] - row[None, :]) <= half
            ok_col = jnp.abs(col[:, None] - col[None, :]) <= half
            return ok_row & ok_col
        Bb, Nn, C = x.shape
        scale = HEAD_DIM ** (-0.5)
        qkv = (x @ W_qkv.T).reshape(Bb, Nn, 3, NUM_HEADS, HEAD_DIM)
        qkv = jnp.transpose(qkv, (2, 0, 3, 1, 4))
        q, k, v = (qkv[0], qkv[1], qkv[2])
        attn = jnp.einsum('bhqd,bhkd->bhqk', q, k) * (scale * temperature[0])
        mask = local_mask(Nn)
        attn = jnp.where(mask[None, None, :, :], attn, -jnp.inf)
        attn = jax.nn.softmax(attn, axis=-1)
        out = jnp.einsum('bhqk,bhkd->bhqd', attn, v)
        out = jnp.transpose(out, (0, 2, 1, 3)).reshape(Bb, Nn, C)
        return out @ W_proj.T + b_proj

    def _L1_ffn_ref(x, W_gat, att_src, att_dst, b_gat, ln_gamma, ln_beta, W1, b1, W2, b2, edge_index):
        import jax, jax.numpy as jnp
        import numpy as np
        B, N, D = (16, 1024, 64)
        NUM_EXPERTS, TOP_K, HEADS = (4, 2, 4)
        N_EDGES = 262144
        LN_EPS = 1e-05

        def _layernorm(x, g, b):
            mu = x.mean(-1, keepdims=True)
            var = ((x - mu) ** 2).mean(-1, keepdims=True)
            return (x - mu) * jax.lax.rsqrt(var + LN_EPS) * g + b

        def _forward(x, edge_index, W_gat, att_src, att_dst, b_gat, ln_gamma, ln_beta, W1, b1, W2, b2):
            Bc, Nc, Dc = x.shape
            M = Bc * Nc
            x_flat = x.reshape(M, Dc)
            h = (x_flat @ W_gat).reshape(M, HEADS, NUM_EXPERTS)
            loops = jnp.arange(M, dtype=edge_index.dtype)
            src = jnp.concatenate([edge_index[0], loops])
            dst = jnp.concatenate([edge_index[1], loops])
            a_src = (h * att_src).sum(-1)
            a_dst = (h * att_dst).sum(-1)
            e = jax.nn.leaky_relu(a_src[src] + a_dst[dst], negative_slope=0.2)
            e_max = jax.ops.segment_max(e, dst, num_segments=M)
            ee = jnp.exp(e - e_max[dst])
            denom = jax.ops.segment_sum(ee, dst, num_segments=M)
            alpha = ee / (denom[dst] + 1e-16)
            msg = h[src] * alpha[:, :, None]
            agg = jax.ops.segment_sum(msg, dst, num_segments=M).reshape(M, HEADS * NUM_EXPERTS) + b_gat
            scores = _layernorm(agg, ln_gamma, ln_beta).reshape(M, HEADS, NUM_EXPERTS).mean(1)
            scores = scores.reshape(Bc, Nc, NUM_EXPERTS)
            topk_s, topk_i = jax.lax.top_k(scores, TOP_K)
            w = jax.nn.softmax(topk_s, axis=-1)
            out = jnp.zeros_like(x)
            for ei in range(NUM_EXPERTS):
                g = jnp.where(topk_i == ei, w, 0.0).sum(-1)
                hh = jax.nn.gelu(x @ W1[ei] + b1[ei], approximate=False)
                out = out + g[..., None] * (hh @ W2[ei] + b2[ei])
            return out
        return _forward(x, edge_index, W_gat, att_src, att_dst, b_gat, ln_gamma, ln_beta, W1, b1, W2, b2)

    def _gn(v, G=32, eps=1e-05):
        B_, H_, W_, C_ = v.shape
        g = v.reshape(B_, H_, W_, G, C_ // G)
        m = jnp.mean(g, axis=(1, 2, 4), keepdims=True)
        s = jnp.var(g, axis=(1, 2, 4), keepdims=True)
        return ((g - m) / jnp.sqrt(s + eps)).reshape(v.shape)

    def _ln_c(v, eps=1e-06):
        m = jnp.mean(v, axis=-1, keepdims=True)
        s = jnp.var(v, axis=-1, keepdims=True)
        return (v - m) / jnp.sqrt(s + eps)

    def _ln_t(v, eps=1e-05):
        m = jnp.mean(v, axis=-1, keepdims=True)
        s = jnp.var(v, axis=-1, keepdims=True)
        return (v - m) / jnp.sqrt(s + eps)

    def _to_tokens(v):
        B_, H_, W_, C_ = v.shape
        return v.reshape(B_, H_ * W_, C_)

    def _from_tokens(t, like):
        return t.reshape(like.shape)
    x = _L0_conv_ref(x, L0_conv_W1, L0_conv_B1, L0_conv_G1, L0_conv_Be1, L0_conv_M1, L0_conv_V1, L0_conv_W2, L0_conv_B2, L0_conv_G2, L0_conv_Be2, L0_conv_M2, L0_conv_V2, L0_conv_W3, L0_conv_B3, L0_conv_G3, L0_conv_Be3, L0_conv_M3, L0_conv_V3)
    t = _to_tokens(x)
    t = t + _L1_attn_ref(_ln_t(t), L1_attn_W_qkv, L1_attn_W_proj, L1_attn_b_proj, L1_attn_temperature)
    t = t + _L1_ffn_ref(_ln_t(t), L1_ffn_W_gat, L1_ffn_att_src, L1_ffn_att_dst, L1_ffn_b_gat, L1_ffn_ln_gamma, L1_ffn_ln_beta, L1_ffn_W1, L1_ffn_b1, L1_ffn_W2, L1_ffn_b2, L1_ffn_edge_index)
    x = _from_tokens(t, x)
    return x

_drawn_inputs = setup_inputs


def setup_inputs(seed=0):
    import zlib

    import numpy as np

    out = dict(_drawn_inputs(seed))
    spreads = {'L1_ffn_b_gat': (0.0, 0.8),
     'L1_ffn_ln_gamma': (1.0, 0.6),
     'L1_ffn_ln_beta': (0.0, 2.0),
     'L1_ffn_b1': (0.0, 2.0),
     'L1_ffn_b2': (0.0, 0.8)}
    factors = {'L0_conv_W1': 4.994,
     'L0_conv_B1': 8.0,
     'L0_conv_G1': 24.097,
     'L0_conv_Be1': 8.0,
     'L0_conv_M1': 8.0,
     'L0_conv_V1': 200.0,
     'L0_conv_W2': 3.815,
     'L0_conv_B2': 15.955,
     'L0_conv_G2': 23.344,
     'L0_conv_Be2': 36.064,
     'L0_conv_M2': 5.957,
     'L0_conv_V2': 200.0,
     'L0_conv_G3': 12.385,
     'L0_conv_V3': 200.0,
     'L1_attn_b_proj': 46.592,
     'L1_ffn_att_src': 64.0,
     'L1_ffn_att_dst': 179.381,
     'L0_conv_B3': 2.913,
     'L0_conv_Be3': 3.742,
     'L0_conv_M3': 2.811,
     'L1_ffn_W_gat': 8.0,
     'L1_ffn_W1': 7.477,
     'L1_ffn_W2': 5.197}
    for name, (base, spread) in spreads.items():
        noise = np.random.default_rng([zlib.crc32(name.encode()), seed]).standard_normal(out[name].shape)
        drawn = base * np.exp(spread * noise) if base else spread * noise
        out[name] = jnp.asarray(drawn.astype(out[name].dtype))
    for name, factor in factors.items():
        out[name] = (out[name] * factor).astype(out[name].dtype)
    return out
```

```python
from contextlib import ExitStack

import numpy as np

import concourse.bass as bass
from concourse import mybir

F32 = mybir.dt.float32
BF16 = mybir.dt.bfloat16
I32 = mybir.dt.int32
U32 = mybir.dt.uint32
ALU = mybir.AluOpType
ACT = mybir.ActivationFunctionType
AX = mybir.AxisListType

N, H, W, C = 8, 56, 56, 64
PATHS, DP = 32, 4
CHUNKS = PATHS * C // 128
ROWS = 8
TILES = H // ROWS
PIX = ROWS * W
SUB = 4
TOK = PIX // SUB
TOKENS = N * H * W
BN_EPS, LN_EPS = 1e-3, 1e-5
HEADS, HD = 8, 8
HALO = 3
QROWS = QCOLS = 4
QB = QROWS * QCOLS
WIN = QROWS + 2 * HALO
KEYS = WIN * WIN
STRIPS = H // QROWS
BLOCKS = W // QCOLS
SPIX = QROWS * W
FEATURES = QROWS + 16
KROWS = C + FEATURES
PH, PW = H + 2 * HALO, W + 2 * HALO

def ahead(n, t, k):
    return n + (t + k) // TILES, (t + k) % TILES

def wait(eng, semaphore, value):
    if not isinstance(value, int) or value > 0:
        eng.wait_ge(semaphore, value)

class Link:

    def __init__(self, eng, semaphore):
        self.eng, self.semaphore, self.n = eng, semaphore, 0

    def __call__(self, instruction):
        self.n += 1
        instruction.then_inc(self.semaphore, 1)
        self.eng.wait_ge(self.semaphore, self.n)

class Strip:

    def __init__(self, turn, par):
        self.turn, self.par, self.i = turn, par, turn * 2 + par

    def step(self, k):
        return Strip(self.turn + (self.par + k) // 2, (self.par + k) % 2)

def mask_features():
    far = -float(2 ** 100)
    keys = np.zeros((STRIPS, FEATURES, WIN, PW), np.float32)
    for s in range(STRIPS):
        for ky in range(WIN):
            row = QROWS * s + ky - HALO
            for j in range(QROWS):
                if abs(ky - HALO - j) > HALO or not 0 <= row < H:
                    keys[s, j, ky, :] = far
    for x in range(PW):
        near = {c % 16 for c in range(W) if abs(c - (x - HALO)) <= HALO} if 0 <= x - HALO < W else set()
        for j in range(16):
            if j not in near:
                keys[:, QROWS + j, :, x] = far
    queries = np.zeros((FEATURES, BLOCKS, HEADS, QROWS, QCOLS), np.float32)
    for j in range(QROWS):
        queries[j, :, :, j, :] = 1
    for x in range(W):
        queries[QROWS + x % 16, x // QCOLS, :, :, x % QCOLS] = 1
    return keys.reshape(STRIPS, FEATURES, WIN * PW), queries.reshape(FEATURES, BLOCKS, HEADS, QB)

EDGES = 262144
EF = EDGES // 128
LOW = EF // 128
SRC_BITS = 15

def partition_signs():
    bits = (np.arange(128)[:, None] >> np.arange(8)) & 1
    cols = [bits[:, 0]] + [bits[:, j - 1] ^ bits[:, j] for j in range(1, 7)] + [bits[:, 6]]
    return (1 - 2 * np.stack(cols, axis=1)).astype(np.float32)

EXPERTS, GHEADS = 4, 4
GH = GHEADS * EXPERTS
NODES = 16384
ROW = GH + GHEADS
JT = TOKENS // 128
JC = 7
FAR = 3.0e38
MISS = float(1 << 20)

FC = 128
NFC = EF // FC
HOT = 8
HIDE = 1.0e30
STATE = 2 * GHEADS + GH
ZT = 512

def clear(nc, semaphores):
    with nc.Block() as block:
        @block.gpsimd
        def _(pool):
            for s in semaphores:
                pool.sem_clear(s)

class Sort:

    HALVES = 4

    def __init__(self, key, other, psign, key_dram, turned_dram, stepped, moved):
        self.buffers, self.psign, self.drams = [key, other], psign, [key_dram, turned_dram]
        self.stepped, self.moved = stepped, moved
        self.plan = []
        col_bits = EF.bit_length() - 1
        all_bits = col_bits + 7
        self.plan.append(("negate", 4, 2, 4))
        for k in range(1, all_bits + 1):
            if k > col_bits:
                self.plan.append(("turn", 0))
                self.plan += [("compare", LOW << (j - col_bits)) for j in range(k - 1, col_bits - 1, -1)]
                self.plan.append(("turn", 1))
            self.plan += [("compare", 1 << j) for j in range(min(k, col_bits) - 1, -1, -1)]
            if k < col_bits - 1:
                self.plan.append(("negate", 4 << k, 1 << k, 3 << k))
            elif k == col_bits - 1:
                self.plan += [("negate", EF, EF // 2, EF), ("sign", 0)]
            elif k < all_bits:
                self.plan.append(("sign", k - col_bits + 1))
        self.flips = sum(step[0] in ("compare", "turn") for step in self.plan)
        self.result = self.buffers[self.flips % 2]
        self.steps = sum(step[0] != "turn" for step in self.plan)

    def vector_steps(self, dve):
        now, steps, moves = 0, 0, 0
        out = []

        def one(kind, args, now, steps, moves):
            wait(dve, self.stepped, steps)
            wait(dve, self.moved, moves)
            x, y = self.buffers[now], self.buffers[1 - now]
            if kind == "negate":
                size, a, b = args
                v = x[:].rearrange("p (n q) -> p n q", q=size)[:, :, a:b]
                dve.tensor_scalar(v, v, -1.0, None, ALU.mult).then_inc(self.stepped, 1)
            elif kind == "sign":
                dve.tensor_scalar(x[:], x[:], self.psign[:, args[0]:args[0] + 1], None, ALU.mult).then_inc(self.stepped, 1)
            else:
                src = x[:].rearrange("p (n two d) -> p n two d", two=2, d=args[0])
                dst = y[:].rearrange("p (n two d) -> p n two d", two=2, d=args[0])
                dve.tensor_tensor(dst[:, :, 0, :], src[:, :, 0, :], src[:, :, 1, :], ALU.min)
                dve.tensor_tensor(dst[:, :, 1, :], src[:, :, 0, :], src[:, :, 1, :], ALU.max).then_inc(self.stepped, 1)

        for kind, *args in self.plan:
            if kind == "turn":
                moves += 16 * (1 + self.HALVES)
                now = 1 - now
                continue
            out.append(lambda a=(kind, args, now, steps, moves): one(*a))
            steps += 1
            if kind == "compare":
                now = 1 - now
        return out

    def turns(self, pool):
        now, steps, moves = 0, 0, 0
        size = 128 // self.HALVES
        for kind, *args in self.plan:
            if kind == "turn":
                dram = self.drams[args[0]]
                pool.wait_ge(self.stepped, steps)
                pool.dma_start(dram, self.buffers[now][:]).then_inc(self.moved, 16)
                moves += 16
                pool.wait_ge(self.moved, moves)
                src = dram.rearrange("p (h l) -> h p l", l=LOW)
                dst = self.buffers[1 - now][:].rearrange("h (p l) -> h p l", l=LOW)
                for k in range(self.HALVES):
                    pool.dma_start(dst[:, k * size:(k + 1) * size], src[:, k * size:(k + 1) * size]).then_inc(self.moved, 16)
                moves += 16 * self.HALVES
                now = 1 - now
                continue
            steps += 1
            if kind == "compare":
                now = 1 - now

def sort_phase(nc, io, key_dram, turned_dram, sorted_dram):
    with ExitStack() as ctx:
        sb = lambda name, shape, dt=F32: ctx.enter_context(nc.sbuf_tensor("s_" + name, shape, dt))
        sem = lambda name: ctx.enter_context(nc.semaphore(name))
        key = sb("key", [128, EF]); other = sb("other", [128, EF]); signs = sb("signs", [128, 8])
        ends = sb("ends", [128, 2, EF], I32)
        edges_in = sem("edges_in"); built = sem("built"); stepped = sem("stepped"); moved = sem("moved"); sorted_out = sem("sorted_out")
        sort = Sort(key, other, signs, key_dram, turned_dram, stepped, moved)
        with nc.Block() as block:
            @block.sync
            def _(sp):
                sp.dma_start(ends[:], io["edges"].rearrange("a (p f) -> p a f", p=128)).then_inc(edges_in, 16)
                sp.dma_start(signs[:], io["psign"]).then_inc(edges_in, 16)
                sp.wait_ge(stepped, sort.steps)
                sp.dma_start(sorted_dram, sort.result[:]).then_inc(sorted_out, 16)
                sp.wait_ge(sorted_out, 16)

            @block.vector
            def _(dve):
                dve.wait_ge(edges_in, 32)
                dve.tensor_scalar(ends[:, 1, :], ends[:, 1, :], SRC_BITS, 1 << 30, ALU.logical_shift_left, ALU.bitwise_or).then_inc(built, 1)
                dve.wait_ge(built, 1)
                dve.tensor_tensor(key[:].bitcast(I32), ends[:, 1, :], ends[:, 0, :], ALU.bitwise_or).then_inc(built, 1)
                dve.wait_ge(built, 2)
                for step in sort.vector_steps(dve):
                    step()

            @block.gpsimd
            def _(pool):
                sort.turns(pool)

def conv_phase(nc, io, t1_dram, q_dram, kpad_dram, vpad_dram):
    with ExitStack() as ctx:
        sb = lambda name, shape, dt=F32: ctx.enter_context(nc.sbuf_tensor(name, shape, dt))
        ps = lambda name, shape: ctx.enter_context(nc.psum_tensor(name, shape, F32))
        semaphores = []

        def sem(name):
            semaphores.append(ctx.enter_context(nc.semaphore(name)))
            return semaphores[-1]

        ident = sb("c_ident", [128, 128])
        pathmask = sb("c_pathmask", [128, PATHS])
        fold = sb("c_fold", [128, C])
        w1 = sb("c_w1", [C, 128])
        w2c = sb("c_w2c", [128, 9, DP])
        w2 = sb("c_w2", [128, 9, 128])
        w3c = sb("c_w3c", [128, C])
        w3 = sb("c_w3", [128, PATHS, C])
        bn1 = sb("c_bn1", [128, 5])
        bn2 = sb("c_bn2", [128, 5])
        bn3 = sb("c_bn3", [128, 5, CHUNKS])
        bn3e = sb("c_bn3e", [128, 2, C])
        s1 = sb("c_s1", [128, 2])
        s2 = sb("c_s2", [128, 2])
        s3 = sb("c_s3", [128, CHUNKS])
        b3 = sb("c_b3", [128, CHUNKS])
        sumb3 = sb("c_sumb3", [128, 1])
        s3e = sb("c_s3e", [128, C])
        wqkv = sb("c_wqkv", [C, 3 * C])
        qscale = sb("c_qscale", [128, 1])
        zero = sb("c_zero", [C, PH * PW])

        x_tok = sb("x_tok", [TOK, TILES, SUB, C])
        x_ch = sb("x_ch", [C, TILES, PIX])
        h1 = sb("h1", [128, H + 2, W + 2])
        h2 = sb("h2", [128, TILES, PIX])
        acc = sb("acc", [128, TILES, PIX])
        usum = sb("usum", [TOK, TILES, SUB, C])
        t1 = sb("t1", [TOK, TILES, SUB, C])
        cen = sb("cen", [TOK, TILES, SUB, C])
        sq = sb("sq", [TOK, TILES, SUB, C])
        z = sb("z", [TOK, TILES, SUB, C])
        stat = sb("stat", [TOK, TILES, 6, SUB])
        z_ch = sb("z_ch", [C, TILES, PIX])
        qk = sb("qk", [128, TILES, PIX])
        v = sb("v", [TOK, TILES, SUB, C])

        psT = ps("psT", [128, 512])
        psH1 = ps("psH1", [128, 512])
        psH2 = ps("psH2", [128, 512])
        psE = [ps(f"psE{i}", [128, 512]) for i in range(2)]
        psF = ps("psF", [128, 512])
        psQK = ps("psQK", [128, 512])
        psV = ps("psV", [128, 512])

        passed = sem("passed")
        const_in = sem("const_in")
        x_loaded = [sem(f"x_loaded{t}") for t in range(TILES)]
        prep = sem("prep")
        prep_sqrt = sem("prep_sqrt")
        weights = sem("weights")
        a1_ready = sem("a1_ready"); h1_done = sem("h1_done")
        c_ready = sem("c_ready"); h2_done = sem("h2_done")
        e_ready = sem("e_ready"); stt_done = sem("stt_done")
        f_ready = sem("f_ready"); u_done = sem("u_done"); t1_done = sem("t1_done")
        ln_step = sem("ln_step"); var_done = sem("var_done"); std_done = sem("std_done"); z_done = sem("z_done")
        zt_ready = sem("zt_ready"); zt_done = sem("zt_done")
        qkv_ready = sem("qkv_ready"); qk_done = sem("qk_done"); v_done = sem("v_done")
        t1_stored = [sem(f"t1_stored{t}") for t in range(TILES)]
        qkv_stored = [sem(f"qkv_stored{t}") for t in range(TILES)]
        zero_set = sem("zero_set"); pad_stored = sem("pad_stored")

        x_view = io["x"].rearrange("n (t s r) w c -> n t (r w) s c", t=TILES, s=SUB)
        t1_view = t1_dram.rearrange("(n t s p) c -> n t p s c", n=N, t=TILES, s=SUB)
        xc_view = io["x_ch"].rearrange("c n (t q) -> n t c q", t=TILES)
        N_CONST = 12

        with nc.Block() as block:
            @block.sync
            def _(sp):
                loads = [(ident[:], io["ident"]), (pathmask[:], io["pathmask"]), (fold[:], io["fold"]),
                         (w1[:], io["w1"]), (w2c[:], io["w2"]), (w3c[:], io["w3"]),
                         (bn1[:], io["bn1"]), (bn2[:], io["bn2"]), (bn3[:], io["bn3"]), (bn3e[:], io["bn3e"]),
                         (wqkv[:], io["wqkv"]),
                         (qscale[0:C, :], io["temperature"].rearrange("(a b) -> a b", a=1).to_broadcast([C, 1]))]
                def load_x(n, t):
                    sp.dma_start(x_ch[:, t], xc_view[n, t]).then_inc(x_loaded[t], 16)
                    sp.dma_start(x_tok[:, t], x_view[n, t]).then_inc(x_loaded[t], 16)

                for dst, src in loads:
                    sp.dma_start(dst, src).then_inc(const_in, 16)
                assert len(loads) == N_CONST
                for t in range(TILES):
                    load_x(0, t)

                sp.wait_ge(zero_set, 1)
                for n in range(N):
                    sp.dma_start(kpad_dram[:, n].rearrange("c y x -> c (y x)"), zero[0:C, 0:PH * PW]).then_inc(pad_stored, 16)
                    sp.dma_start(vpad_dram[n].rearrange("y x c -> (y x c)").rearrange("(p q) -> p q", p=C), zero[0:C, 0:PH * PW]).then_inc(pad_stored, 16)
                sp.wait_ge(pad_stored, 32 * N)

                def stores(n, t):
                    g = n * TILES + t
                    sp.wait_ge(t1_done, g + 1)
                    sp.dma_start(t1_view[n, t], t1[:, t]).then_inc(t1_stored[t], 16)
                    sp.wait_ge(qk_done, g + 1)
                    y0 = HALO + ROWS * t
                    sp.dma_start(q_dram[:, n, PIX * t:PIX * (t + 1)], qk[0:C, t]).then_inc(qkv_stored[t], 16)
                    sp.dma_start(kpad_dram[:, n, y0:y0 + ROWS, HALO:HALO + W],
                                 qk[C:2 * C, t].rearrange("c (y x) -> c y x", x=W)).then_inc(qkv_stored[t], 16)
                    sp.wait_ge(v_done, g + 1)
                    for r in range(2):
                        sp.dma_start(vpad_dram[n, y0 + r:y0 + ROWS:2, HALO:HALO + W, :].rearrange("s x c -> x s c"),
                                     v[r * W:(r + 1) * W, t]).then_inc(qkv_stored[t], 16)

                def image(n, last):
                    for t in range(TILES):
                        if not last:
                            sp.wait_ge(u_done, n * TILES + t + 1)
                            load_x(n + 1, t)
                        stores(n, t)

                with sp.Fori(0, N - 1) as n:
                    image(n, False)
                image(N - 1, True)
                for t in range(TILES):
                    sp.wait_ge(t1_stored[t], 16 * N)
                    sp.wait_ge(qkv_stored[t], 64 * N)

            @block.gpsimd
            def _(pool):
                pool.memset(zero[:], 0.0).then_inc(zero_set, 1)
                pool.memset(h1[:], 0.0).then_inc(zero_set, 1)

            @block.tensor
            def _(pe):
                pe.wait_ge(const_in, 16 * N_CONST)
                pe.wait_ge(weights, 1)
                pe.wait_ge(prep_sqrt, 4)
                pe.wait_ge(zero_set, 2)

                def reduce_1x1(n, t):
                    g = n * TILES + t
                    pe.wait_ge(x_loaded[t], 32 * (n + 1))
                    wait(pe, h1_done, g)
                    pe.matmul(psH1[:, 0:PIX], w1[:], x_ch[:, t], start=True, stop=True).then_inc(a1_ready, 1)

                def conv3(n, t):
                    g = n * TILES + t
                    pe.wait_ge(h1_done, g + (2 if t < TILES - 1 else 1))
                    wait(pe, h2_done, g)
                    for tap in range(9):
                        dy, dx = divmod(tap, 3)
                        m = pe.matmul(psH2[:, 0:PIX].rearrange("p (y x) -> p y x", x=W), w2[:, tap, :],
                                      h1[:, ROWS * t + dy:ROWS * (t + 1) + dy, dx:dx + W],
                                      start=(tap == 0), stop=(tap == 8))
                    m.then_inc(c_ready, 1)

                def expand(n, t):
                    g = n * TILES + t
                    pe.wait_ge(h2_done, g + 1)
                    for c in range(CHUNKS):
                        wait(pe, stt_done, g * CHUNKS + c - 1)
                        pe.matmul(psE[c % 2][:, 0:PIX], w3[:, 2 * c:2 * c + 2, :].rearrange("p j c -> p (j c)"),
                                  h2[:, t], start=True, stop=True).then_inc(e_ready, 1)

                def to_tokens(n, t):
                    g = n * TILES + t
                    pe.wait_ge(stt_done, (g + 1) * CHUNKS)
                    wait(pe, u_done, g)
                    for s in range(SUB):
                        m = pe.matmul(psF[0:TOK, s * C:(s + 1) * C], acc[:, t, s * TOK:(s + 1) * TOK], fold[:],
                                      start=True, stop=True)
                    m.then_inc(f_ready, 1)

                def z_to_channels(n, t):
                    g = n * TILES + t
                    pe.wait_ge(z_done, g + 1)
                    wait(pe, zt_done, g)
                    pe.sem_inc(passed, 1)
                    for s in range(SUB):
                        m = pe.transpose(psT[0:C, s * TOK:(s + 1) * TOK], z[:, t, s, :], ident[0:TOK, 0:TOK])
                    m.then_inc(zt_ready, 1)

                def project(n, t):
                    g = n * TILES + t
                    pe.wait_ge(zt_done, g + 1)
                    wait(pe, qk_done, g)
                    pe.matmul(psQK[:, 0:PIX], wqkv[:, 0:128], z_ch[:, t], start=True, stop=True).then_inc(qkv_ready, 1)
                    wait(pe, v_done, g)
                    for s in range(SUB):
                        m = pe.matmul(psV[0:TOK, s * C:(s + 1) * C], z_ch[:, t, s * TOK:(s + 1) * TOK], wqkv[:, 128:192],
                                      start=True, stop=True)
                    m.then_inc(qkv_ready, 1)

                def image(n, first, last):
                    for t in range(TILES):
                        if not (last and t + 2 >= TILES):
                            reduce_1x1(*ahead(n, t, 2))
                        if not (last and t + 1 >= TILES):
                            conv3(*ahead(n, t, 1))
                        expand(n, t)
                        if not (first and t == 0):
                            z_to_channels(*ahead(n, t, -1))
                        to_tokens(n, t)
                        if not (first and t == 0):
                            project(*ahead(n, t, -1))

                reduce_1x1(0, 0)
                reduce_1x1(0, 1)
                conv3(0, 0)
                image(0, True, False)
                with pe.Fori(1, N - 1) as n:
                    image(n, False, False)
                image(N - 1, False, True)
                z_to_channels(N - 1, TILES - 1)
                project(N - 1, TILES - 1)

            @block.scalar
            def _(act):
                for k, (dst, src) in enumerate([(s1[:, 0:1], bn1[:, 4:5]), (s2[:, 0:1], bn2[:, 4:5]), (s3[:], bn3[:, 4, :]), (s3e[:], bn3e[:, 1, :])]):
                    act.wait_ge(prep, 1)
                    act.activation(dst, src, ACT.Sqrt).then_inc(prep_sqrt, 1)
                act.wait_ge(weights, 1)
                act.wait_ge(zero_set, 2)

                def h1_relu(n, t):
                    g = n * TILES + t
                    act.wait_ge(a1_ready, g + 1)
                    act.activation(h1[:, ROWS * t + 1:ROWS * (t + 1) + 1, 1:W + 1],
                                   psH1[:, 0:PIX].rearrange("p (y x) -> p y x", x=W),
                                   ACT.Relu, bias=s1[:, 1:2], scale=s1[:, 0:1]).then_inc(h1_done, 1)

                def h2_relu(n, t):
                    act.wait_ge(c_ready, n * TILES + t + 1)
                    act.activation(h2[:, t], psH2[:, 0:PIX], ACT.Relu, bias=s2[:, 1:2], scale=s2[:, 0:1]).then_inc(h2_done, 1)

                def layernorm(n, t, first):
                    g = n * TILES + t
                    if not first:
                        act.wait_ge(t1_stored[t], 16 * n)
                    act.wait_ge(u_done, g + 1)
                    act.activation(t1[:, t], usum[:, t], ACT.Relu).then_inc(t1_done, 1)
                    act.wait_ge(var_done, g + 1)
                    act.activation(stat[:, t, 4], stat[:, t, 3], ACT.Sqrt).then_inc(std_done, 1)

                def qkv(n, t, first):
                    g = n * TILES + t
                    act.wait_ge(zt_ready, g + 1)
                    act.activation(z_ch[:, t], psT[0:C, 0:PIX], ACT.Copy).then_inc(zt_done, 1)
                    if not first:
                        act.wait_ge(qkv_stored[t], 64 * n)
                    act.wait_ge(qkv_ready, 2 * g + 1)
                    act.activation(qk[C:2 * C, t], psQK[C:2 * C, 0:PIX], ACT.Copy)
                    for s in range(PIX // SPIX):
                        m = act.activation(qk[0:C, t, s * SPIX:(s + 1) * SPIX].rearrange("c (b y x) -> c y b x", y=QROWS, x=QCOLS),
                                           psQK[0:C, s * SPIX:(s + 1) * SPIX].rearrange("c (y b x) -> c y b x", y=QROWS, x=QCOLS),
                                           ACT.Copy, scale=qscale[0:C, 0:1])
                    m.then_inc(qk_done, 1)
                    act.wait_ge(qkv_ready, 2 * g + 2)
                    act.activation(v[:, t], psV[0:TOK, 0:SUB * C].rearrange("p (s c) -> p s c", c=C), ACT.Copy).then_inc(v_done, 1)

                def image(n, first, last):
                    for t in range(TILES):
                        if not (last and t + 2 >= TILES):
                            h1_relu(*ahead(n, t, 2))
                        if not (last and t + 1 >= TILES):
                            h2_relu(*ahead(n, t, 1))
                        if not (first and t == 0):
                            layernorm(*ahead(n, t, -1), first)
                            qkv(*ahead(n, t, -1), first)

                h1_relu(0, 0)
                h1_relu(0, 1)
                h2_relu(0, 0)
                image(0, True, False)
                with act.Fori(1, N - 1) as n:
                    image(n, False, False)
                image(N - 1, False, True)
                layernorm(N - 1, TILES - 1, False)
                qkv(N - 1, TILES - 1, False)

            @block.vector
            def _(dve):
                dve.wait_ge(const_in, 16 * N_CONST)
                link = Link(dve, ln_step)
                for variance in (bn1[:, 4:5], bn2[:, 4:5], bn3[:, 4, :]):
                    dve.tensor_scalar(variance, variance, BN_EPS, None, ALU.add)
                dve.tensor_scalar(qscale[C:2 * C, :], pathmask[C:2 * C, 0:1], 0.0, 1.0, ALU.mult, ALU.add)
                dve.tensor_scalar(qscale[0:C, :], qscale[0:C, :], float(HD) ** -0.5, None, ALU.mult)
                dve.tensor_scalar(bn3e[:, 1, :], bn3e[:, 1, :], BN_EPS, None, ALU.add).then_inc(prep, 1)
                dve.wait_ge(prep_sqrt, 4)
                for d in (s1[:, 0:1], s2[:, 0:1], s3[:], s3e[:]):
                    m = dve.reciprocal(d, d)
                link(m)
                dve.tensor_tensor(s1[:, 0:1], s1[:, 0:1], bn1[:, 1:2], ALU.mult)
                dve.tensor_tensor(s2[:, 0:1], s2[:, 0:1], bn2[:, 1:2], ALU.mult)
                dve.tensor_tensor(s3[:], s3[:], bn3[:, 1, :], ALU.mult)
                dve.tensor_tensor(s3e[:], s3e[:], bn3e[:, 0, :], ALU.mult)
                dve.tensor_tensor(s1[:, 1:2], bn1[:, 0:1], bn1[:, 3:4], ALU.subtract)
                dve.tensor_tensor(s2[:, 1:2], bn2[:, 0:1], bn2[:, 3:4], ALU.subtract)
                link(dve.tensor_tensor(b3[:], bn3[:, 0, :], bn3[:, 3, :], ALU.subtract))
                dve.tensor_tensor(s1[:, 1:2], s1[:, 1:2], s1[:, 0:1], ALU.mult)
                dve.tensor_tensor(s2[:, 1:2], s2[:, 1:2], s2[:, 0:1], ALU.mult)
                dve.tensor_tensor(w3c[:], w3c[:], s3e[:], ALU.mult)
                link(dve.tensor_tensor(b3[:], b3[:], s3[:], ALU.mult))
                dve.tensor_tensor(s1[:, 1:2], s1[:, 1:2], bn1[:, 2:3], ALU.add)
                dve.tensor_tensor(s2[:, 1:2], s2[:, 1:2], bn2[:, 2:3], ALU.add)
                link(dve.tensor_tensor(b3[:], b3[:], bn3[:, 2, :], ALU.add))
                link(dve.tensor_reduce(sumb3[:], b3[:], AX.X, ALU.add))
                link(dve.tensor_scalar(b3[:], b3[:], -1.0, None, ALU.mult))
                for tap in range(9):
                    dve.tensor_tensor(w2[:, tap, :].rearrange("p (q d) -> p q d", d=DP),
                                      w2c[:, tap:tap + 1, :].to_broadcast([128, PATHS, DP]),
                                      pathmask[:].unsqueeze(2).to_broadcast([128, PATHS, DP]), ALU.mult)
                dve.tensor_tensor(w3[:], w3c[:].unsqueeze(1).to_broadcast([128, PATHS, C]),
                                  pathmask[:].unsqueeze(2).to_broadcast([128, PATHS, C]), ALU.mult).then_inc(weights, 1)
                base = link.n
                LN_STEPS = 6

                def layernorm_ops(n, t):
                    g = n * TILES + t
                    at = lambda k: g * LN_STEPS + base + k
                    st = lambda j: stat[:, t, j]
                    bc = lambda j: stat[:, t, j].unsqueeze(2).to_broadcast([TOK, SUB, C])

                    def residual():
                        dve.wait_ge(f_ready, g + 1)
                        dve.tensor_tensor(usum[:, t], psF[0:TOK, 0:SUB * C].rearrange("p (s c) -> p s c", c=C),
                                          x_tok[:, t], ALU.add).then_inc(u_done, 1)

                    def total():
                        dve.wait_ge(t1_done, g + 1)
                        dve.tensor_reduce(st(0), t1[:, t], AX.X, ALU.add).then_inc(ln_step, 1)

                    def minus_mean():
                        dve.wait_ge(ln_step, at(1))
                        dve.tensor_scalar(st(1), st(0), -1.0 / C, None, ALU.mult).then_inc(ln_step, 1)

                    def center():
                        dve.wait_ge(ln_step, at(2))
                        dve.tensor_tensor(cen[:, t], t1[:, t], bc(1), ALU.add).then_inc(ln_step, 1)

                    def square():
                        dve.wait_ge(ln_step, at(3))
                        dve.tensor_tensor(sq[:, t], cen[:, t], cen[:, t], ALU.mult).then_inc(ln_step, 1)

                    def squares():
                        dve.wait_ge(ln_step, at(4))
                        dve.tensor_reduce(st(2), sq[:, t], AX.X, ALU.add).then_inc(ln_step, 1)

                    def variance():
                        dve.wait_ge(ln_step, at(5))
                        dve.tensor_scalar(st(3), st(2), 1.0 / C, LN_EPS, ALU.mult, ALU.add).then_inc(var_done, 1)

                    def inverse():
                        dve.wait_ge(std_done, g + 1)
                        dve.reciprocal(st(5), st(4)).then_inc(ln_step, 1)

                    def scale():
                        dve.wait_ge(ln_step, at(6))
                        dve.tensor_tensor(z[:, t], cen[:, t], bc(5), ALU.mult).then_inc(z_done, 1)

                    return [residual, total, minus_mean, center, square, squares, variance, inverse, scale]

                def tile(n, t, pending):
                    g = n * TILES + t
                    for c in range(CHUNKS):
                        dve.wait_ge(e_ready, g * CHUNKS + c + 1)
                        if c == 0:
                            dve.tensor_scalar(acc[:, t], psE[0][:, 0:PIX], b3[:, 0:1], sumb3[:, 0:1], ALU.max, ALU.add)\
                               .then_inc(stt_done, 1)
                        else:
                            dve.wait_ge(stt_done, g * CHUNKS + c)
                            dve.scalar_tensor_tensor(acc[:, t], psE[c % 2][:, 0:PIX], b3[:, c:c + 1], acc[:, t],
                                                     ALU.max, ALU.add).then_inc(stt_done, 1)
                        if c % 2 == 0 and c >= 2 or c >= 14:
                            if pending:
                                pending.pop(0)()
                    while pending:
                        pending.pop(0)()

                def image(n, first):
                    for t in range(TILES):
                        tile(n, t, [] if first and t == 0 else layernorm_ops(*ahead(n, t, -1)))

                image(0, True)
                with dve.Fori(1, N) as n:
                    image(n, False)
                for op in layernorm_ops(N - 1, TILES - 1):
                    op()

        clear(nc, semaphores)

def attention_phase(nc, io, t1_dram, q_dram, kpad_dram, vpad_dram, t2_dram):
    with ExitStack() as ctx:
        sb = lambda name, shape, dt=F32: ctx.enter_context(nc.sbuf_tensor(name, shape, dt))
        sb2 = lambda name, shape: [sb(f"{name}{i}", shape) for i in range(2)]
        ps = lambda name, shape: ctx.enter_context(nc.psum_tensor(name, shape, F32))
        semaphores = []

        def sem(name):
            semaphores.append(ctx.enter_context(nc.semaphore(name)))
            return semaphores[-1]

        ident = sb("a_ident", [128, 128])
        headmask = sb("a_headmask", [C, HEADS])
        outmask = sb("a_outmask", [128, C])
        pick = sb("a_pick", [128, QB])
        wproj = sb("a_wproj", [C, C])
        bproj = sb("a_bproj", [TOK, C])

        keys = sb2("keys", [KROWS, WIN * PW])
        q = sb2("q", [C, SPIX])
        q_exp = sb2("q_exp", [KROWS, BLOCKS, HEADS, QB])
        val = sb2("val", [KEYS, BLOCKS, C + 1])
        t1 = sb2("t1", [TOK, 2, C])
        prob = sb2("prob", [128, BLOCKS * KEYS])
        mx = sb2("mx", [128, BLOCKS])
        prob_t = sb("prob_t", [KEYS, BLOCKS, 128])
        rden = sb2("rden", [128, BLOCKS])
        om = sb2("om", [128, BLOCKS, C])
        onorm = sb2("onorm", [128, BLOCKS, C])
        o_ch = sb2("o_ch", [C, SPIX])
        t2a = sb2("t2a", [TOK, 2, C])
        t2 = sb2("t2", [TOK, 2, C])

        psS = [ps(f"psS{i}", [128, 512]) for i in range(3)]
        psP = [ps(f"psP{i}", [128, 512]) for i in range(2)]
        psO = [ps(f"psO{i}", [128, 512]) for i in range(2)]
        psM = ps("psM", [128, 512])
        BANKS = [(0, 5), (5, 10), (10, 14)]
        GROUPS = [(0, 4), (4, 8), (8, 12), (12, 14)]
        HALVES = [(0, 7), (7, 14)]

        const_in = sem("const_in")
        ones_set = sem("ones_set")
        kq_loaded = [sem(f"kq_loaded{i}") for i in range(2)]
        v_loaded = [sem(f"v_loaded{i}") for i in range(2)]
        t1_loaded = [sem(f"t1_loaded{i}") for i in range(2)]
        t2_stored = [sem(f"t2_stored{i}") for i in range(2)]
        exp_q = sem("exp_q"); s_ready = sem("s_ready"); mx_done = sem("mx_done"); sub_done = sem("sub_done")
        exp_done = sem("exp_done"); pt_ready = sem("pt_ready"); pt_done = sem("pt_done")
        pv_ready = sem("pv_ready"); rden_done = sem("rden_done"); o_done = sem("o_done"); norm_done = sem("norm_done")
        ot_ready = sem("ot_ready"); ot_done = sem("ot_done"); pr_ready = sem("pr_ready")
        t2a_done = sem("t2a_done"); t2_done = sem("t2_done")

        t1_view = t1_dram.rearrange("(i r p) c -> i p r c", r=2, p=TOK)
        t2_view = t2_dram.rearrange("(i r p) c -> i p r c", r=2, p=TOK)
        consts = [(ident, "ident"), (headmask, "headmask"), (outmask, "outmask"), (pick, "pick"), (wproj, "wproj")]
        N_CONST = len(consts) + 1 + 2
        PAIRS = N * STRIPS // 2
        FIRST, LAST = 0, PAIRS - 1

        def windows(n, y):
            row = vpad_dram[n, bass.ds(y, 1)]
            return bass.AP(row.tensor, row.offset, [[C, WIN], [QCOLS * C, BLOCKS], [1, C]])

        def every_strip(eng, step):
            step(Strip(0, 0), True, False)
            step(Strip(0, 1), False, False)
            with eng.Fori(1, PAIRS - 1) as turn:
                step(Strip(turn, 0), False, False)
                step(Strip(turn, 1), False, False)
            step(Strip(PAIRS - 1, 0), False, False)
            step(Strip(PAIRS - 1, 1), False, True)

        with nc.Block() as block:
            @block.sync
            def _(sp):
                for dst, name in consts:
                    sp.dma_start(dst[:], io[name]).then_inc(const_in, 16)
                sp.dma_start(bproj[:], io["bproj"].rearrange("(a b) -> a b", a=1).to_broadcast([TOK, C])).then_inc(const_in, 16)
                for par in range(2):
                    sp.dma_start(q_exp[par][C:KROWS], io["qfeat"]).then_inc(const_in, 16)

                def loads(n, s, par, i):
                    wait(sp, s_ready, 3 * i - 3)
                    sp.dma_start(keys[par][0:C, :],
                                 kpad_dram[:, n, bass.ds(s * QROWS, WIN), :].rearrange("c y x -> c (y x)")).then_inc(kq_loaded[par], 16)
                    sp.dma_start(keys[par][C:KROWS, :], io["kfeat"][bass.ds(s, 1)].rearrange("o f x -> (o f) x")).then_inc(kq_loaded[par], 16)
                    wait(sp, exp_q, i - 1)
                    sp.dma_start(q[par][:], q_dram[:, n, bass.ds(s * SPIX, SPIX)]).then_inc(kq_loaded[par], 16)
                    wait(sp, pv_ready, 2 * i - 2)
                    for ky in range(WIN):
                        sp.dma_start(val[par][ky * WIN:(ky + 1) * WIN, :, 0:C], windows(n, s * QROWS + ky)).then_inc(v_loaded[par], 16)

                sp.wait_ge(ones_set, 2)
                for par in range(2):
                    loads(0, par, par, par)
                with sp.Fori(1, STRIPS // 2) as pair:
                    for par in range(2):
                        loads(0, pair * 2 + par, par, pair * 2 + par)
                with sp.Fori(1, N) as n:
                    with sp.Fori(0, STRIPS // 2) as pair:
                        for par in range(2):
                            loads(n, pair * 2 + par, par, n * STRIPS + pair * 2 + par)

            @block.gpsimd
            def _(pool):
                for par in range(2):
                    pool.memset(val[par][:], 1.0).then_inc(ones_set, 1)
                pool.wait_ge(const_in, 16 * N_CONST)

                def spread_q(st):
                    i, par = st.i, st.par
                    pool.wait_ge(kq_loaded[par], 48 * (st.turn + 1))
                    wait(pool, s_ready, 3 * i - 3)
                    pool.tensor_tensor(q_exp[par][0:C],
                                       q[par][:].rearrange("c (b m) -> c b m", m=QB).unsqueeze(2).to_broadcast([C, BLOCKS, HEADS, QB]),
                                       headmask[:].unsqueeze(1).unsqueeze(3).to_broadcast([C, BLOCKS, HEADS, QB]),
                                       ALU.mult).then_inc(exp_q, 1)

                def add_bias(st):
                    i, par = st.i, st.par
                    pool.wait_ge(t2a_done, i + 1)
                    wait(pool, t2_stored[par], 16 * (st.turn))
                    pool.tensor_tensor(t2[par][:], t2a[par][:], bproj[:].unsqueeze(1).to_broadcast([TOK, 2, C]), ALU.add)\
                        .then_inc(t2_done, 1)
                    pool.wait_ge(t2_done, i + 1)
                    pool.dma_start(t2_view[i], t2[par][:]).then_inc(t2_stored[par], 16)

                def normalise(st):
                    i, par = st.i, st.par
                    wait(pool, ot_ready, i - 1)
                    for k, (a, b) in enumerate(HALVES):
                        pool.wait_ge(o_done, 2 * i + k + 1)
                        pool.tensor_tensor(onorm[par][:, a:b, :], om[par][:, a:b, :],
                                           rden[par][:, a:b].unsqueeze(2).to_broadcast([128, b - a, C]), ALU.mult)\
                            .then_inc(norm_done, 1)

                def step(st, first, last):
                    if not last and not (isinstance(st.turn, int) and st.turn == PAIRS - 1):
                        spread_q(st.step(2))
                    if not first:
                        add_bias(st.step(-1))
                    normalise(st)

                spread_q(Strip(0, 0))
                spread_q(Strip(0, 1))
                every_strip(pool, step)
                add_bias(Strip(PAIRS - 1, 1))
                for par in range(2):
                    pool.wait_ge(t2_stored[par], 16 * PAIRS)

            @block.tensor
            def _(pe):
                pe.wait_ge(const_in, 16 * N_CONST)

                def scores(st):
                    i, par = st.i, st.par
                    pe.wait_ge(exp_q, i + 1)
                    pe.wait_ge(kq_loaded[par], 48 * (st.turn + 1))
                    for bank, (a, b) in enumerate(BANKS):
                        wait(pe, sub_done, 3 * i - 3 + bank + 1)
                        for blk in range(a, b):
                            x = blk * QCOLS
                            m = pe.matmul(psS[bank][:, (blk - a) * KEYS:(blk - a + 1) * KEYS],
                                          q_exp[par][:, blk].rearrange("k h m -> k (h m)"),
                                          keys[par][:].rearrange("k (y x) -> k y x", x=PW)[:, :, x:x + WIN],
                                          start=True, stop=True)
                        m.then_inc(s_ready, 1)

                def turn_probs(st):
                    i, par = st.i, st.par
                    for k, (a, b) in enumerate(GROUPS):
                        pe.wait_ge(exp_done, 3 * i + (1, 2, 3, 3)[k])
                        wait(pe, pt_done, 4 * i + k - 1)
                        for blk in range(a, b):
                            m = pe.transpose(psP[k % 2][0:KEYS, (blk - a) * 128:(blk - a + 1) * 128],
                                             prob[par][:, blk * KEYS:(blk + 1) * KEYS], ident[:])
                        m.then_inc(pt_ready, 1)

                def weigh_values(st):
                    i, par = st.i, st.par
                    pe.wait_ge(v_loaded[par], 16 * WIN * (st.turn + 1))
                    for k, (a, b) in enumerate(HALVES):
                        pe.wait_ge(pt_done, 4 * i + (2, 4)[k])
                        wait(pe, o_done, 2 * i - 2 + k + 1)
                        for blk in range(a, b):
                            m = pe.matmul(psO[k][:, (blk - a) * (C + 1):(blk - a + 1) * (C + 1)], prob_t[:, blk, :],
                                          val[par][:, blk, :], start=True, stop=True)
                        m.then_inc(pv_ready, 1)

                def turn_outputs(st):
                    i, par = st.i, st.par
                    pe.wait_ge(norm_done, 2 * i + 2)
                    wait(pe, ot_done, i)
                    for blk in range(BLOCKS):
                        m = pe.matmul(psM[0:C, blk * QB:(blk + 1) * QB], onorm[par][:, blk, :], pick[:], start=True, stop=True)
                    m.then_inc(ot_ready, 1)

                def project(st):
                    i, par = st.i, st.par
                    pe.wait_ge(ot_done, i + 1)
                    wait(pe, t2a_done, i)
                    for r in range(2):
                        m = pe.matmul(psM[0:TOK, SPIX + r * C:SPIX + (r + 1) * C], o_ch[par][:, r * TOK:(r + 1) * TOK], wproj[:],
                                      start=True, stop=True)
                    m.then_inc(pr_ready, 1)

                def step(st, first, last):
                    if not last:
                        scores(st.step(1))
                    if not first:
                        turn_outputs(st.step(-1))
                    turn_probs(st)
                    if not first:
                        project(st.step(-1))
                    weigh_values(st)

                scores(Strip(0, 0))
                every_strip(pe, step)
                turn_outputs(Strip(PAIRS - 1, 1))
                project(Strip(PAIRS - 1, 1))

            @block.scalar
            def _(act):
                def exponentials(st):
                    i, par = st.i, st.par
                    for bank, (a, b) in enumerate(BANKS):
                        act.wait_ge(sub_done, 3 * i + bank + 1)
                        p = prob[par][:, a * KEYS:b * KEYS]
                        act.activation(p, p, ACT.Exp).then_inc(exp_done, 1)

                def copy_probs(st):
                    i, par = st.i, st.par
                    for k, (a, b) in enumerate(GROUPS):
                        act.wait_ge(pt_ready, 4 * i + k + 1)
                        if k == 0:
                            wait(act, pv_ready, 2 * i)
                        act.activation(prob_t[:, a:b, :], psP[k % 2][0:KEYS, 0:(b - a) * 128].rearrange("k (b m) -> k b m", m=128),
                                       ACT.Copy).then_inc(pt_done, 1)

                def copy_outputs(st):
                    i, par = st.i, st.par
                    act.wait_ge(ot_ready, i + 1)
                    act.activation(o_ch[par][:].rearrange("c (y b x) -> c b y x", y=QROWS, x=QCOLS),
                                   psM[0:C, 0:SPIX].rearrange("c (b y x) -> c b y x", y=QROWS, x=QCOLS), ACT.Copy)\
                       .then_inc(ot_done, 1)

                def load_t1(st):
                    i, par = st.i, st.par
                    wait(act, t2a_done, i - 1)
                    act.dma_start(t1[par][:], t1_view[i]).then_inc(t1_loaded[par], 16)

                def step(st, first, last):
                    load_t1(st)
                    if not first:
                        copy_outputs(st.step(-1))
                    copy_probs(st)
                    if not last:
                        exponentials(st.step(1))

                exponentials(Strip(0, 0))
                every_strip(act, step)
                copy_outputs(Strip(PAIRS - 1, 1))

            @block.vector
            def _(dve):
                dve.wait_ge(const_in, 16 * N_CONST)

                def subtract_max(st):
                    i, par = st.i, st.par
                    for bank, (a, b) in enumerate(BANKS):
                        dve.wait_ge(s_ready, 3 * i + bank + 1)
                        s = psS[bank][:, 0:(b - a) * KEYS].rearrange("p (b k) -> p b k", k=KEYS)
                        dve.tensor_reduce(mx[par][:, a:b], s, AX.X, ALU.max).then_inc(mx_done, 1)
                        dve.wait_ge(mx_done, 3 * i + bank + 1)
                        dve.tensor_tensor(prob[par][:, a * KEYS:b * KEYS].rearrange("p (b k) -> p b k", k=KEYS), s,
                                          mx[par][:, a:b].unsqueeze(2).to_broadcast([128, b - a, KEYS]), ALU.subtract)\
                           .then_inc(sub_done, 1)

                def own_head(st):
                    i, par = st.i, st.par
                    wait(dve, norm_done, 2 * i - 2)
                    for k, (a, b) in enumerate(HALVES):
                        dve.wait_ge(pv_ready, 2 * i + k + 1)
                        o = psO[k][:, 0:(b - a) * (C + 1)].rearrange("p (b c) -> p b c", c=C + 1)
                        dve.reciprocal(rden[par][:, a:b], o[:, :, C])
                        dve.tensor_tensor(om[par][:, a:b, :], o[:, :, 0:C],
                                          outmask[:].unsqueeze(1).to_broadcast([128, b - a, C]), ALU.mult).then_inc(o_done, 1)

                def residual(st):
                    i, par = st.i, st.par
                    dve.wait_ge(pr_ready, i + 1)
                    dve.wait_ge(t1_loaded[par], 16 * (st.turn + 1))
                    wait(dve, t2_done, i - 1)
                    dve.tensor_tensor(t2a[par][:], psM[0:TOK, SPIX:SPIX + 2 * C].rearrange("p (r c) -> p r c", c=C), t1[par][:],
                                      ALU.add).then_inc(t2a_done, 1)

                def step(st, first, last):
                    if not last:
                        subtract_max(st.step(1))
                    if not first:
                        residual(st.step(-1))
                    own_head(st)

                subtract_max(Strip(0, 0))
                every_strip(dve, step)
                residual(Strip(PAIRS - 1, 1))

        clear(nc, semaphores)

def index_phase(nc, io, key_dram, edge_dram, node_dram, first_dram, ends_dram):
    with ExitStack() as ctx:
        sb = lambda name, shape, dt=F32: ctx.enter_context(nc.sbuf_tensor(name, shape, dt))
        sem = lambda name: ctx.enter_context(nc.semaphore(name))
        key = sb("i_key", [128, EF], I32)
        dst = sb("i_dst", [128, EF], I32)
        part_i = sb("i_part", [128, EF], I32)
        dstf = sb("i_dstf", [128, EF])
        src = sb("i_src", [128, EF], I32)
        same = sb("i_same", [128, EF])
        lim = sb("i_lim", [128, EF])
        lim2 = sb("i_lim2", [128, EF])
        digit = [sb(f"i_digit{i}", [128, EF]) for i in range(2)]
        iota = sb("i_iota", [128, 128])
        before = sb("i_before", [128, 128])
        first = sb("i_first", [128, 1], I32)
        ends = sb("i_ends", [128, 2])
        chunk = [sb(f"i_chunk{i}", [128, 2, FC]) for i in range(2)]
        hot = [[sb(f"i_hot{i}{d}", [128, HOT, 128], BF16) for d in range(2)] for i in range(2)]
        zero = sb("i_zero", [128, 128], BF16)
        cnt = sb("i_cnt", [128, 128]); inc = sb("i_inc", [128, 128]); base = sb("i_base", [128, 1])
        none = sb("i_none", [128, 128]); pos = sb("i_pos", [128, 2, 128]); posi = sb("i_posi", [128, 2, 128], I32)
        psC = ctx.enter_context(nc.psum_tensor("i_psC", [128, 128], F32))
        psB = ctx.enter_context(nc.psum_tensor("i_psB", [128, 1], F32))
        const_in = sem("const_in"); step = sem("step"); digits = sem("digits"); digits_out = sem("digits_out")
        limits = sem("limits"); limits_out = sem("limits_out"); zeroed = sem("zeroed")
        loaded = [sem(f"loaded{i}") for i in range(2)]
        hot_ready = sem("hot_ready"); hot_used = sem("hot_used"); counted = sem("counted")
        totals = sem("totals"); based = sem("based"); placed = sem("placed"); placed_out = sem("placed_out")
        digit_dram = nc.dram_tensor("scratch_digits", [NFC, 128, 2, FC], F32, kind="Internal").ap()
        GROUPS = FC // HOT

        with nc.Block() as block:
            @block.sync
            def _(sp):
                for a, b in ((key[:].bitcast(F32), key_dram), (iota[:], io["iota"]), (before[:], io["before"])):
                    sp.dma_start(a, b).then_inc(const_in, 16)
                sp.wait_ge(digits, 2)
                for d in range(2):
                    for c in range(NFC):
                        sp.dma_start(digit_dram[c, :, d, :], digit[d][:, c * FC:(c + 1) * FC]).then_inc(digits_out, 16)
                sp.wait_ge(digits_out, 32 * NFC)
                for par in range(2):
                    sp.dma_start(chunk[par][:], digit_dram[par]).then_inc(loaded[par], 16)
                with sp.Fori(0, NFC // 2 - 1) as turn:
                    for par in range(2):
                        sp.wait_ge(hot_ready, (turn * 2 + par + 1) * GROUPS)
                        sp.dma_start(chunk[par][:], digit_dram[turn * 2 + par + 2]).then_inc(loaded[par], 16)
                sp.wait_ge(limits, 1)
                for k, a in enumerate((src[:].bitcast(F32), lim[:], lim2[:], same[:])):
                    for c in range(NFC):
                        sp.dma_start(edge_dram[c, :, k, :], a[:, c * FC:(c + 1) * FC]).then_inc(limits_out, 16)
                sp.dma_start(first_dram, first[:]).then_inc(limits_out, 16)
                sp.dma_start(ends_dram, ends[:]).then_inc(limits_out, 16)
                sp.wait_ge(placed, 1)
                sp.dma_start(node_dram.rearrange("k p t -> p k t"), posi[:]).then_inc(placed_out, 16)
                sp.wait_ge(limits_out, 64 * NFC + 32)
                sp.wait_ge(placed_out, 16)

            @block.vector
            def _(dve):
                done = Link(dve, step)
                dve.wait_ge(const_in, 48)
                done(dve.tensor_scalar(dst[:], key[:], SRC_BITS, NODES - 1, ALU.logical_shift_right, ALU.bitwise_and))
                done(dve.tensor_scalar(part_i[:], dst[:], 127, None, ALU.bitwise_and))
                dve.tensor_copy(dstf[:], dst[:])
                done(dve.tensor_copy(digit[0][:], part_i[:]))
                done(dve.tensor_scalar(part_i[:], dst[:], 7, None, ALU.logical_shift_right))
                dve.tensor_copy(digit[1][:], part_i[:]).then_inc(digits, 2)
                dve.tensor_scalar(src[:], key[:], (1 << SRC_BITS) - 1, None, ALU.bitwise_and)
                dve.memset(same[:, 0:1], 0.0)
                done(dve.tensor_tensor(same[:, 1:EF], dstf[:, 1:EF], dstf[:, 0:EF - 1], ALU.is_equal))
                done(dve.tensor_scalar(lim[:], same[:], 2.0, -1.0, ALU.mult, ALU.add))
                dve.tensor_scalar(lim2[:], same[:], -1.0, HIDE, ALU.add, ALU.mult)
                dve.tensor_copy(first[:], dst[:, 0:1])
                dve.tensor_copy(ends[:, 0:1], dstf[:, 0:1])
                dve.tensor_copy(ends[:, 1:2], dstf[:, EF - 1:EF])
                dve.tensor_scalar(lim[:], lim[:], FAR, None, ALU.mult).then_inc(limits, 1)
                dve.memset(zero[:], 0.0).then_inc(zeroed, 1)
                with dve.Fori(0, NFC // 2) as turn:
                    for par in range(2):
                        dve.wait_ge(loaded[par], (turn + 1) * 16)
                        for g in range(GROUPS):
                            dve.wait_ge(hot_used, turn * (2 * GROUPS) + par * GROUPS + g)
                            for d in range(2):
                                m = dve.tensor_tensor(hot[g % 2][d][:], iota[:].unsqueeze(1).to_broadcast([128, HOT, 128]),
                                                      chunk[par][:, d, g * HOT:(g + 1) * HOT].unsqueeze(2).to_broadcast([128, HOT, 128]),
                                                      ALU.is_equal)
                            m.then_inc(hot_ready, 1)
                dve.wait_ge(counted, 1)
                dve.memset(none[:], 1.0)
                done(dve.tensor_copy(cnt[:], psC[:]))
                done(dve.tensor_tensor_scan(inc[:], none[:], cnt[:], 0.0, ALU.mult, ALU.add))
                dve.tensor_copy(base[:], inc[:, 127:128]).then_inc(totals, 1)
                dve.wait_ge(based, 1)
                done(dve.tensor_copy(base[:], psB[:]))
                dve.tensor_scalar(none[:], cnt[:], 0.0, MISS, ALU.is_equal, ALU.mult)
                done(dve.tensor_scalar(inc[:], inc[:], base[:], None, ALU.add))
                dve.tensor_tensor(pos[:, 1, :], inc[:], cnt[:], ALU.subtract)
                done(dve.tensor_scalar(pos[:, 0, :], inc[:], -1.0, None, ALU.add))
                done(dve.tensor_tensor(pos[:], pos[:], none[:].unsqueeze(1).to_broadcast([128, 2, 128]), ALU.add))
                dve.tensor_copy(posi[:], pos[:]).then_inc(placed, 1)

            @block.tensor
            def _(pe):
                pe.wait_ge(zeroed, 1)
                pe.matmul(psC[:], zero[:], zero[:], start=True, stop=False).then_inc(hot_used, 1)
                with pe.Fori(0, NFC // 2) as turn:
                    for par in range(2):
                        for g in range(GROUPS):
                            pe.wait_ge(hot_ready, turn * (2 * GROUPS) + par * GROUPS + g + 1)
                            for c in range(HOT):
                                m = pe.matmul(psC[:], hot[g % 2][1][:, c, :], hot[g % 2][0][:, c, :], start=False, stop=False)
                            m.then_inc(hot_used, 1)
                pe.matmul(psC[:], zero[:], zero[:], start=False, stop=True).then_inc(counted, 1)
                pe.wait_ge(totals, 1)
                pe.matmul(psB[:], before[:], base[:], start=True, stop=True).then_inc(based, 1)

def table_phase(nc, io, t2_dram, z_dram, table_dram, adst_dram):
    with ExitStack() as ctx:
        sb = lambda name, shape, dt=F32: ctx.enter_context(nc.sbuf_tensor(name, shape, dt))
        sb2 = lambda name, shape: [sb(f"{name}{i}", shape) for i in range(2)]
        ps = lambda name, shape: ctx.enter_context(nc.psum_tensor(name, shape, F32))
        sem = lambda name: ctx.enter_context(nc.semaphore(name))

        ident = sb("t_ident", [128, 128])
        wg = sb("t_wg", [C, GH + 2 * GHEADS])
        att = sb("t_att", [C, 2, GH])
        wa = sb("t_wa", [C, 2, GH])
        t2 = sb2("t_t2", [128, JC, C])
        cen = sb2("t_cen", [128, JC, C])
        sq = sb2("t_sq", [128, JC, C])
        z = sb2("t_z", [128, JC, C])
        stat = sb2("t_stat", [128, 6, JC])
        z_ch = sb2("t_z_ch", [C, JC * 128])
        rows = sb2("t_rows", [128, JC, ROW])
        adst = sb2("t_adst", [128, JC, GHEADS])
        psZ = [ps(f"t_psZ{i}", [128, 512]) for i in range(4)]
        psR = [ps(f"t_psR{i}", [128, 512]) for i in range(2)]
        NCH = JT // JC

        passed = sem("passed")
        const_in = sem("const_in"); weights = sem("weights")
        loaded = [sem(f"loaded{i}") for i in range(2)]
        stored = [sem(f"stored{i}") for i in range(2)]
        step = sem("step"); cen_done = sem("cen_done"); sq_done = sem("sq_done"); var_done = sem("var_done")
        std_done = sem("std_done"); inv_done = sem("inv_done"); z_done = sem("z_done")
        zt_ready = sem("zt_ready"); zt_done = sem("zt_done"); row_ready = sem("row_ready"); row_done = sem("row_done")
        t2_view = t2_dram.rearrange("(p k j) c -> k p j c", p=128, j=JC)
        z_view = z_dram.rearrange("c (k x) -> k c x", k=NCH)
        table_view = table_dram.rearrange("(p k j) c -> k p j c", p=128, j=JC)
        adst_view = adst_dram.rearrange("(p k j) c -> k p j c", p=128, j=JC)
        PARTS = [(0, 4), (4, JC)]

        def every_chunk(eng, step_of):
            with eng.Fori(0, NCH // 2) as turn:
                for par in range(2):
                    step_of(turn, par)

        with nc.Block() as block:
            @block.sync
            def _(sp):
                sp.dma_start(ident[:], io["ident"]).then_inc(const_in, 16)
                sp.dma_start(wg[:, 0:GH], io["wgat"]).then_inc(const_in, 16)
                for k, name in enumerate(("att_src", "att_dst")):
                    sp.dma_start(att[:, k, :], io[name].rearrange("(a h) e -> a (h e)", a=1).to_broadcast([C, GH])).then_inc(const_in, 16)

                sp.dma_start(t2[0][:], t2_view[0]).then_inc(loaded[0], 16)
                sp.dma_start(t2[1][:], t2_view[1]).then_inc(loaded[1], 16)

                def out(turn, par):
                    k = turn * 2 + par
                    sp.wait_ge(zt_done, k * 2 + 2)
                    sp.dma_start(z_view[k], z_ch[par][:]).then_inc(stored[par], 16)
                    sp.wait_ge(row_done, k + 1)
                    sp.dma_start(table_view[k], rows[par][:]).then_inc(stored[par], 16)
                    sp.dma_start(adst_view[k], adst[par][:]).then_inc(stored[par], 16)

                with sp.Fori(0, NCH // 2 - 1) as turn:
                    for par in range(2):
                        sp.wait_ge(cen_done, turn * 2 + par + 1)
                        sp.dma_start(t2[par][:], t2_view[turn * 2 + par + 2]).then_inc(loaded[par], 16)
                        out(turn, par)
                for par in range(2):
                    out(NCH // 2 - 1, par)
                for par in range(2):
                    sp.wait_ge(stored[par], 48 * (NCH // 2))

            @block.vector
            def _(dve):
                dve.wait_ge(const_in, 64)
                for k in range(2):
                    m = dve.tensor_tensor(wa[:, k, :], wg[:, 0:GH], att[:, k, :], ALU.mult)
                m.then_inc(weights, 1)
                dve.wait_ge(weights, 1)
                for k in range(2):
                    m = dve.tensor_reduce(wg[:, GH + k * GHEADS:GH + (k + 1) * GHEADS],
                                          wa[:, k, :].rearrange("c (h e) -> c h e", e=EXPERTS), AX.X, ALU.add)
                m.then_inc(weights, 1)

                def layernorm(turn, par):
                    k = turn * 2 + par
                    st = lambda j: stat[par][:, j, :]
                    dve.wait_ge(loaded[par], (turn + 1) * 16)
                    dve.tensor_reduce(st(0), t2[par][:], AX.X, ALU.add).then_inc(step, 1)
                    dve.wait_ge(step, k * 3 + 1)
                    dve.tensor_scalar(st(1), st(0), -1.0 / C, None, ALU.mult).then_inc(step, 1)
                    dve.wait_ge(step, k * 3 + 2)
                    dve.tensor_tensor(cen[par][:], t2[par][:], st(1).unsqueeze(2).to_broadcast([128, JC, C]), ALU.add)\
                       .then_inc(cen_done, 1)
                    dve.wait_ge(sq_done, k + 1)
                    dve.tensor_reduce(st(2), sq[par][:], AX.X, ALU.add).then_inc(step, 1)
                    dve.wait_ge(step, k * 3 + 3)
                    dve.tensor_scalar(st(3), st(2), 1.0 / C, LN_EPS, ALU.mult, ALU.add).then_inc(var_done, 1)
                    dve.wait_ge(std_done, k + 1)
                    dve.reciprocal(st(5), st(4)).then_inc(inv_done, 1)

                every_chunk(dve, layernorm)

            @block.gpsimd
            def _(pool):
                def squares_and_scale(turn, par):
                    k = turn * 2 + par
                    pool.wait_ge(cen_done, k + 1)
                    pool.tensor_tensor(sq[par][:], cen[par][:], cen[par][:], ALU.mult).then_inc(sq_done, 1)
                    pool.wait_ge(inv_done, k + 1)
                    pool.tensor_tensor(z[par][:], cen[par][:], stat[par][:, 5, :].unsqueeze(2).to_broadcast([128, JC, C]), ALU.mult)\
                        .then_inc(z_done, 1)

                every_chunk(pool, squares_and_scale)

            @block.tensor
            def _(pe):
                pe.wait_ge(weights, 2)

                def rows_of(turn, par):
                    k = turn * 2 + par
                    pe.wait_ge(z_done, k + 1)
                    pe.sem_inc(passed, 1)
                    for h, (a, b) in enumerate(PARTS):
                        for j in range(a, b):
                            m = pe.transpose(psZ[par * 2 + h][0:C, (j - a) * 128:(j - a + 1) * 128], z[par][:, j, :], ident[:])
                        m.then_inc(zt_ready, 1)
                    pe.wait_ge(zt_done, k * 2 + 2)
                    pe.wait_ge(row_done, k)
                    for j in range(JC):
                        m = pe.matmul(psR[par][:, j * 24:(j + 1) * 24], z_ch[par][:, j * 128:(j + 1) * 128], wg[:],
                                      start=True, stop=True)
                    m.then_inc(row_ready, 1)

                every_chunk(pe, rows_of)

            @block.scalar
            def _(act):
                def copies(turn, par):
                    k = turn * 2 + par
                    act.wait_ge(var_done, k + 1)
                    act.activation(stat[par][:, 4, :], stat[par][:, 3, :], ACT.Sqrt).then_inc(std_done, 1)
                    act.wait_ge(stored[par], turn * 48)
                    for h, (a, b) in enumerate(PARTS):
                        act.wait_ge(zt_ready, k * 2 + h + 1)
                        act.activation(z_ch[par][:, a * 128:b * 128], psZ[par * 2 + h][0:C, 0:(b - a) * 128], ACT.Copy).then_inc(zt_done, 1)
                    act.wait_ge(row_ready, k + 1)
                    r = psR[par][:, 0:JC * 24].rearrange("p (j c) -> p j c", c=24)
                    act.activation(rows[par][:], r[:, :, 0:ROW], ACT.Copy)
                    act.activation(adst[par][:], r[:, :, ROW:24], ACT.Copy).then_inc(row_done, 1)

                every_chunk(act, copies)

def edge_phase(nc, io, z_dram, table_dram, adst_dram, edge_dram, node_dram, first_dram, b_dram, state_dram, y_dram):
    with ExitStack() as ctx:
        sb = lambda name, shape, dt=F32: ctx.enter_context(nc.sbuf_tensor(name, shape, dt))
        sb2 = lambda name, shape, dt=F32: [sb(f"{name}{i}", shape, dt) for i in range(2)]
        sem = lambda name: ctx.enter_context(nc.semaphore(name))
        sem2 = lambda name: [sem(f"{name}{i}") for i in range(2)]

        node_dst = sb("e_node_dst", [128, 128, GHEADS])
        start_ix = sb("e_start_ix", [128, 128], I32)
        first_ix = sb("e_first_ix", [128, 1], I32)
        b_first = sb("e_b_first", [128, GHEADS])
        zeros = sb("e_zeros", [128, FC * GHEADS])
        edge = sb2("e_edge", [128, 4, FC])
        bsrc = sb2("e_bsrc", [128, FC, GHEADS])
        b = sb2("e_b", [128, FC, GHEADS])
        row = sb2("e_row", [128, FC, ROW])
        state = sb2("e_state", [128, FC, STATE])
        e0 = sb("e_e0", [128, FC, GHEADS]); e1 = sb("e_e1", [128, FC, GHEADS])
        drop = sb("e_drop", [128, 2, FC, GHEADS])
        weight = sb("e_weight", [128, 2, FC, GHEADS])
        part = sb("e_part", [128, FC, GH])

        w1 = sb("f_w1", [C, EXPERTS, 128]); b1 = sb("f_b1", [128, EXPERTS]); w2 = sb("f_w2", [128, EXPERTS, C])
        b2 = sb("f_b2", [128, EXPERTS * C])
        z = sb2("f_z", [C, ZT])
        hid = [sb(f"f_hid{e}", [128, ZT]) for e in range(EXPERTS)]
        y = sb2("f_y", [128, ZT // 128, EXPERTS * C])
        psH = [ctx.enter_context(nc.psum_tensor(f"f_psH{e}", [128, ZT], F32)) for e in range(EXPERTS)]
        psY = [ctx.enter_context(nc.psum_tensor(f"f_psY{i}", [128, ZT // 128, EXPERTS * C], F32)) for i in range(2)]

        passed = sem("passed")
        const_in = sem("const_in"); weights_in = sem("weights_in"); zeroed = sem("zeroed"); b_zeroed = sem("b_zeroed"); b_placed = sem("b_placed")
        b_gathered = sem("b_gathered")
        edge_in = sem2("edge_in"); b_in = sem2("b_in"); rows_in = sem2("rows_in"); state_out = sem2("state_out")
        b_filled = sem("b_filled"); summed = sem("summed"); leaked = sem("leaked"); maxed = sem("maxed")
        diffed = sem("diffed"); limited = sem("limited"); exped = sem("exped"); weighted = sem("weighted")
        scanned = sem("scanned")
        z_in = sem2("z_in"); hid_ready = sem("hid_ready"); gelu_done = sem("gelu_done")
        y_ready = sem2("y_ready"); y_done = sem2("y_done"); y_out = sem2("y_out")

        TILES_Z = TOKENS // ZT
        PER = TILES_Z // NFC
        z_view = z_dram.rearrange("c (k x) -> k c x", x=ZT)
        y_view = y_dram.rearrange("(p k j) c -> k p j c", p=128, j=ZT // 128)
        b_view = b_dram.rearrange("(p k f) h -> k p f h", p=128, f=FC)
        state_view = state_dram.rearrange("(p k f) c -> k p f c", p=128, f=FC)

        with nc.Block() as block:
            @block.sync
            def _(sp):
                sp.dma_start(node_dst[:], adst_dram[0:NODES].rearrange("(p t) h -> p t h", p=128)).then_inc(const_in, 16)
                sp.dma_start(start_ix[:], node_dram[1]).then_inc(const_in, 16)
                sp.dma_start(first_ix[:], first_dram).then_inc(const_in, 16)
                sp.dma_start(b2[:], io["ffn_b2"].to_broadcast([128, EXPERTS * C])).then_inc(const_in, 16)
                sp.wait_ge(zeroed, 1)
                flat = b_dram.rearrange("(p k f) h -> k p (f h)", p=128, f=FC)
                for c in range(NFC):
                    sp.dma_start(flat[c], zeros[:]).then_inc(b_zeroed, 16)
                for par in range(2):
                    sp.dma_start(edge[par][:], edge_dram[par]).then_inc(edge_in[par], 16)
                sp.wait_ge(b_placed, 16 * 129)
                for par in range(2):
                    sp.dma_start(bsrc[par][:], b_view[par]).then_inc(b_in[par], 16)

                def out(turn, par):
                    sp.wait_ge(scanned, turn * 2 + par + 2)
                    sp.dma_start(state_view[turn * 2 + par], state[par][:]).then_inc(state_out[par], 16)

                with sp.Fori(0, NFC // 2 - 1) as turn:
                    for par in range(2):
                        out(turn, par)
                        sp.dma_start(edge[par][:], edge_dram[turn * 2 + par + 2]).then_inc(edge_in[par], 16)
                        sp.dma_start(bsrc[par][:], b_view[turn * 2 + par + 2]).then_inc(b_in[par], 16)
                for par in range(2):
                    out(NFC // 2 - 1, par)
                for par in range(2):
                    sp.wait_ge(state_out[par], 16 * (NFC // 2))

            @block.gpsimd
            def _(pool):
                pool.memset(zeros[:], 0.0).then_inc(zeroed, 1)
                pool.wait_ge(const_in, 64)
                pool.wait_ge(b_zeroed, 16 * NFC)
                pool.indirect_dma_start(out=b_first[:], out_offset=None, in_=adst_dram,
                                        in_offset=bass.IndirectOffsetOnAxis(ap=first_ix[:, 0:1], axis=0)).then_inc(b_gathered, 16)
                for t in range(128):
                    pool.indirect_dma_start(out=b_dram, out_offset=bass.IndirectOffsetOnAxis(ap=start_ix[:, t:t + 1], axis=0),
                                            in_=node_dst[:, t, :], in_offset=None,
                                            bounds_check=EDGES - 1, oob_is_err=False).then_inc(b_placed, 16)
                pool.wait_ge(b_placed, 16 * 128)
                pool.wait_ge(b_gathered, 16)
                pool.dma_start(b_dram.rearrange("(p x) h -> p x h", p=128)[:, 0, :], b_first[:]).then_inc(b_placed, 16)
                with pool.Fori(0, NFC // 2) as turn:
                    for par in range(2):
                        pool.wait_ge(edge_in[par], (turn + 1) * 16)
                        pool.sem_inc(passed, 1)
                        for f in range(FC):
                            pool.indirect_dma_start(out=row[par][:, f, :], out_offset=None, in_=table_dram,
                                                    in_offset=bass.IndirectOffsetOnAxis(ap=edge[par][:, 0, f:f + 1].bitcast(I32), axis=0)
                                                    ).then_inc(rows_in[par], 16)

            @block.vector
            def _(dve):
                dve.memset(state[1][:, FC - 1, 0:GHEADS], -FAR)
                dve.memset(state[1][:, FC - 1, GHEADS:STATE], 0.0)
                dve.memset(b[1][:, FC - 1, :], 0.0).then_inc(scanned, 1)
                dve.wait_ge(scanned, 1)
                dve.wait_ge(const_in, 64)

                def outputs(t_slot, par):
                    dve.wait_ge(y_ready[par], t_slot + 1)
                    dve.wait_ge(y_out[par], t_slot * 16)
                    dve.tensor_tensor(y[par][:], psY[par][:], b2[:].unsqueeze(1).to_broadcast([128, ZT // 128, EXPERTS * C]),
                                      ALU.add).then_inc(y_done[par], 1)

                def scans(turn, par):
                    c = turn * 2 + par
                    same, lim, lim2 = edge[par][:, 3, :], edge[par][:, 1, :], edge[par][:, 2, :]
                    st, last = state[par], state[1 - par][:, FC - 1, :]
                    dve.wait_ge(edge_in[par], (turn + 1) * 16)
                    dve.wait_ge(b_in[par], (turn + 1) * 16)
                    dve.wait_ge(scanned, c + 1)
                    for h in range(GHEADS):
                        m = dve.tensor_tensor_scan(b[par][:, :, h], same, bsrc[par][:, :, h], b[1 - par][:, FC - 1, h:h + 1], ALU.mult, ALU.add)
                    m.then_inc(b_filled, 1)
                    dve.wait_ge(b_filled, c + 1)
                    dve.wait_ge(rows_in[par], (turn + 1) * (16 * FC))
                    dve.tensor_tensor(e0[:], row[par][:, :, GH:ROW], b[par][:], ALU.add).then_inc(summed, 1)
                    dve.wait_ge(summed, c + 1)
                    dve.scalar_tensor_tensor(e1[:], e0[:], 0.2, e0[:], ALU.mult, ALU.max).then_inc(leaked, 1)
                    dve.wait_ge(leaked, c + 1)
                    dve.wait_ge(state_out[par], turn * 16)
                    for h in range(GHEADS):
                        m = dve.tensor_tensor_scan(st[:, :, h], lim, e1[:, :, h], last[:, h:h + 1], ALU.min, ALU.max)
                    m.then_inc(maxed, 1)
                    dve.wait_ge(maxed, c + 1)
                    dve.tensor_tensor(drop[:, 1], e1[:], st[:, :, 0:GHEADS], ALU.subtract)
                    dve.tensor_tensor(drop[:, 0, 1:FC, :], st[:, 0:FC - 1, 0:GHEADS], st[:, 1:FC, 0:GHEADS], ALU.subtract)
                    dve.tensor_tensor(drop[:, 0, 0, :], last[:, 0:GHEADS], st[:, 0, 0:GHEADS], ALU.subtract).then_inc(diffed, 1)
                    dve.wait_ge(diffed, c + 1)
                    dve.scalar_tensor_tensor(drop[:, 0], drop[:, 0], 0.0, lim2.unsqueeze(2).to_broadcast([128, FC, GHEADS]),
                                             ALU.min, ALU.add).then_inc(limited, 1)
                    dve.wait_ge(exped, c + 1)
                    for h in range(GHEADS):
                        dve.tensor_tensor_scan(st[:, :, GHEADS + h], weight[:, 0, :, h], weight[:, 1, :, h],
                                               last[:, GHEADS + h:GHEADS + h + 1], ALU.mult, ALU.add)
                    dve.tensor_tensor(part[:].rearrange("p f (h e) -> p f h e", e=EXPERTS),
                                      row[par][:, :, 0:GH].rearrange("p f (h e) -> p f h e", e=EXPERTS),
                                      weight[:, 1].unsqueeze(3).to_broadcast([128, FC, GHEADS, EXPERTS]), ALU.mult).then_inc(weighted, 1)
                    dve.wait_ge(weighted, c + 1)
                    for k in range(GH):
                        n = 2 * GHEADS + k
                        m = dve.tensor_tensor_scan(st[:, :, n], weight[:, 0, :, k // EXPERTS], part[:, :, k], last[:, n:n + 1],
                                                   ALU.mult, ALU.add)
                    m.then_inc(scanned, 1)

                with dve.Fori(0, NFC // 2) as turn:
                    for par in range(2):
                        for q in range(par * PER, (par + 1) * PER):
                            outputs(turn * PER + q // 2, q % 2)
                        scans(turn, par)
                outputs(NFC // 2 * PER, 0)

            @block.scalar
            def _(act):
                for a, name in ((w1, "ffn_w1"), (b1, "ffn_b1"), (w2, "ffn_w2")):
                    act.dma_start(a[:], io[name]).then_inc(weights_in, 16)
                for par in range(2):
                    act.dma_start(z[par][:], z_view[par]).then_inc(z_in[par], 16)
                act.wait_ge(weights_in, 48)

                def gelus(turn, q, load):
                    t, par = turn * (2 * PER) + q, q % 2
                    for e in range(EXPERTS):
                        act.wait_ge(hid_ready, t * EXPERTS + e + 1)
                        act.activation(hid[e][:], psH[e][:], ACT.Gelu, bias=b1[:, e:e + 1]).then_inc(gelu_done, 1)
                    if load:
                        act.dma_start(z[par][:], z_view[t + 2]).then_inc(z_in[par], 16)
                    act.wait_ge(y_done[par], turn * PER + q // 2 + 1)
                    act.dma_start(y_view[t], y[par][:]).then_inc(y_out[par], 16)

                def exps(turn, par):
                    act.wait_ge(limited, turn * 2 + par + 1)
                    act.activation(weight[:], drop[:], ACT.Exp).then_inc(exped, 1)

                def both(turn, last):
                    for par in range(2):
                        for q in range(par * PER, (par + 1) * PER):
                            gelus(turn, q, not last or q < 2 * PER - 1)
                        exps(turn, par)

                with act.Fori(0, NFC // 2 - 1) as turn:
                    both(turn, False)
                both(NFC // 2 - 1, True)
                gelus(NFC // 2, 0, False)
                act.wait_ge(y_out[0], 16 * (TILES_Z // 2 + 1))
                act.wait_ge(y_out[1], 16 * (TILES_Z // 2))

            @block.tensor
            def _(pe):
                pe.wait_ge(weights_in, 48)

                def tile(turn, q):
                    t, par, k = turn * (2 * PER) + q, q % 2, turn * PER + q // 2
                    pe.wait_ge(z_in[par], (k + 1) * 16)
                    for e in range(EXPERTS):
                        pe.matmul(psH[e][:], w1[:, e, :], z[par][:], start=True, stop=True).then_inc(hid_ready, 1)
                    pe.wait_ge(y_done[par], k)
                    for e in range(EXPERTS):
                        pe.wait_ge(gelu_done, t * EXPERTS + e + 1)
                        for j in range(ZT // 128):
                            m = pe.matmul(psY[par][:, j, e * C:(e + 1) * C], hid[e][:, j * 128:(j + 1) * 128], w2[:, e, :],
                                          start=True, stop=True)
                    m.then_inc(y_ready[par], 1)

                with pe.Fori(0, NFC // 2) as turn:
                    for q in range(2 * PER):
                        tile(turn, q)
                tile(NFC // 2, 0)

def join_phase(nc, io, state_dram, node_dram, first_dram, ends_dram, sums_dram):
    with ExitStack() as ctx:
        sb = lambda name, shape, dt=F32: ctx.enter_context(nc.sbuf_tensor("j_" + name, shape, dt))
        sem = lambda name: ctx.enter_context(nc.semaphore(name))
        ident = sb("ident", [128, 128]); last_pos = sb("last_pos", [128, 1])
        ends = sb("ends", [128, 2]); first_ix = sb("first_ix", [128, 1], I32); end_ix = sb("end_ix", [128, 128], I32)
        tail = sb("tail", [128, STATE])
        wide = sb("wide", [128, 5, GH])
        wt = sb("wt", [GH, 5, 128])
        cont = sb("cont", [GH, 128])
        link = sb("link", [GH, 128])
        lims = sb("lims", [GH, 2, 128]); lim2 = sb("lim2", [GH, 128])
        run = sb("run", [GH, 3, 129])
        drop = sb("drop", [GH, 2, 128]); weight = sb("weight", [GH, 2, 128]); part = sb("part", [GH, 2, 128])
        carry_t = sb("carry_t", [GH, 3, 128]); carry = sb("carry", [128, 3, GH])
        pos = sb("pos", [128, 1], I32); posf = sb("posf", [128, 1]); missing = sb("missing", [128, 1]); fix_ix = sb("fix_ix", [128, 1], I32)
        fix = sb("fix", [128, STATE]); top = sb("top", [128, GHEADS]); fdrop = sb("fdrop", [128, 2, GHEADS]); fw = sb("fw", [128, 2, GHEADS])
        old = sb("old", [128, GHEADS + GH]); new = sb("new", [128, GHEADS + GH]); fixed = sb("fixed", [128, STATE])
        sums = sb("sums", [128, 128, STATE])
        rest = (TOKENS - NODES) // 128
        psT = ctx.enter_context(nc.psum_tensor("j_psT", [GH, 5, 128], F32))
        psC = ctx.enter_context(nc.psum_tensor("j_psC", [128, 3, GH], F32))
        const_in = sem("const_in"); ix_in = sem("ix_in"); widened = sem("widened"); turned = sem("turned"); step = sem("step")
        limited = sem("limited"); exped = sem("exped"); carried = sem("carried"); turned_back = sem("turned_back")
        pos_in = sem("pos_in"); fix_at = sem("fix_at"); blank = sem("blank"); fix_in = sem("fix_in"); fix_limited = sem("fix_limited")
        fix_exped = sem("fix_exped"); fix_ready = sem("fix_ready"); fix_out = sem("fix_out"); sums_in = sem("sums_in"); sums_out = sem("sums_out")
        heads = lambda a: a.rearrange("p (h e) -> p h e", e=EXPERTS)
        spread = lambda a: a.unsqueeze(2).to_broadcast([128, GHEADS, EXPERTS])

        with nc.Block() as block:
            @block.sync
            def _(sp):
                sp.dma_start(first_ix[:], first_dram).then_inc(ix_in, 16)
                sp.dma_start(end_ix[:], node_dram[0]).then_inc(ix_in, 16)
                sp.dma_start(tail[:], state_dram.rearrange("(p x) c -> p x c", p=128)[:, EF - 1, :]).then_inc(const_in, 16)
                for a, b in ((ends, ends_dram), (ident, io["ident"]), (last_pos, io["last_pos"])):
                    sp.dma_start(a[:], b).then_inc(const_in, 16)
                sp.wait_ge(blank, 2)
                sp.dma_start(sums_dram[NODES:TOKENS].rearrange("(p t) c -> p t c", p=128), sums[:, 0:rest, :]).then_inc(sums_out, 16)
                sp.wait_ge(sums_in, 16 * 128)
                sp.dma_start(sums_dram[0:NODES].rearrange("(p t) c -> p t c", p=128), sums[:]).then_inc(sums_out, 16)
                sp.wait_ge(sums_out, 32)

            @block.gpsimd
            def _(pool):
                pool.wait_ge(ix_in, 32)
                pool.indirect_dma_start(out=pos[:], out_offset=None, in_=node_dram[0].rearrange("p (t o) -> (p t) o", o=1),
                                        in_offset=bass.IndirectOffsetOnAxis(ap=first_ix[:, 0:1], axis=0)).then_inc(pos_in, 16)
                pool.wait_ge(fix_at, 1)
                pool.indirect_dma_start(out=fix[:], out_offset=None, in_=state_dram,
                                        in_offset=bass.IndirectOffsetOnAxis(ap=fix_ix[:, 0:1], axis=0),
                                        bounds_check=EDGES - 1, oob_is_err=False).then_inc(fix_in, 16)
                pool.wait_ge(fix_ready, 1)
                pool.indirect_dma_start(out=state_dram, out_offset=bass.IndirectOffsetOnAxis(ap=fix_ix[:, 0:1], axis=0),
                                        in_=fixed[:], in_offset=None, bounds_check=EDGES - 1, oob_is_err=False).then_inc(fix_out, 16)
                pool.wait_ge(fix_out, 16)
                pool.wait_ge(sums_out, 16)
                for t in range(128):
                    pool.indirect_dma_start(out=sums[:, t, :], out_offset=None, in_=state_dram,
                                            in_offset=bass.IndirectOffsetOnAxis(ap=end_ix[:, t:t + 1], axis=0),
                                            bounds_check=EDGES - 1, oob_is_err=False).then_inc(sums_in, 16)

            @block.vector
            def _(dve):
                done = Link(dve, step)
                dve.memset(sums[:, :, 0:GHEADS], -FAR).then_inc(blank, 1)
                dve.memset(sums[:, :, GHEADS:STATE], 0.0).then_inc(blank, 1)
                dve.memset(fix[:], 0.0)
                dve.memset(cont[:], 0.0)
                dve.memset(run[:, 0, 0:1], -FAR)
                done(dve.memset(run[:, 1:3, 0:1], 0.0))
                dve.wait_ge(const_in, 64)
                dve.tensor_copy(heads(wide[:, 0, :]), spread(tail[:, 0:GHEADS]))
                dve.tensor_copy(heads(wide[:, 1, :]), spread(tail[:, GHEADS:2 * GHEADS]))
                dve.tensor_copy(wide[:, 2, :], tail[:, 2 * GHEADS:])
                dve.tensor_copy(wide[:, 3:5, :], ends[:].unsqueeze(2).to_broadcast([128, 2, GH])).then_inc(widened, 1)
                dve.wait_ge(pos_in, 16)
                done(dve.tensor_copy(posf[:], pos[:]))
                dve.tensor_scalar(missing[:], posf[:], last_pos[:], MISS, ALU.is_gt, ALU.mult).then_inc(step, 1)
                done.n += 1
                dve.wait_ge(step, done.n)
                done(dve.tensor_tensor(posf[:], posf[:], missing[:], ALU.add))
                dve.tensor_copy(fix_ix[:], posf[:]).then_inc(fix_at, 1)
                dve.wait_ge(turned, 1)
                done(dve.tensor_copy(wt[:], psT[:]))
                dve.tensor_tensor(cont[:, 1:128], wt[:, 3, 1:128], wt[:, 4, 0:127], ALU.is_equal)
                done(dve.tensor_tensor(link[:], wt[:, 3, :], wt[:, 4, :], ALU.is_equal))
                done(dve.tensor_tensor(link[:], link[:], cont[:], ALU.mult))
                dve.tensor_scalar(lims[:, 0, :], link[:], 2.0, -1.0, ALU.mult, ALU.add)
                dve.tensor_scalar(lims[:, 1, :], cont[:], 2.0, -1.0, ALU.mult, ALU.add)
                done(dve.tensor_scalar(lim2[:], link[:], -1.0, HIDE, ALU.add, ALU.mult))
                done(dve.tensor_scalar(lims[:], lims[:], FAR, None, ALU.mult))
                done(dve.tensor_tensor_scan(run[:, 0, 1:129], lims[:, 0, :], wt[:, 0, :], -FAR, ALU.min, ALU.max))
                dve.tensor_tensor(drop[:, 0, :], run[:, 0, 0:128], run[:, 0, 1:129], ALU.subtract)
                done(dve.tensor_tensor(drop[:, 1, :], wt[:, 0, :], run[:, 0, 1:129], ALU.subtract))
                dve.scalar_tensor_tensor(drop[:, 0, :], drop[:, 0, :], 0.0, lim2[:], ALU.min, ALU.add).then_inc(limited, 1)
                dve.wait_ge(exped, 1)
                done(dve.tensor_tensor(part[:], wt[:, 1:3, :], weight[:, 1, :].unsqueeze(1).to_broadcast([GH, 2, 128]), ALU.mult))
                for k in range(2):
                    m = dve.tensor_tensor_scan(run[:, 1 + k, 1:129], weight[:, 0, :], part[:, k, :], 0.0, ALU.mult, ALU.add)
                done(m)
                dve.tensor_tensor(carry_t[:, 0, :], run[:, 0, 0:128], lims[:, 1, :], ALU.min)
                dve.tensor_tensor(carry_t[:, 1:3, :], run[:, 1:3, 0:128], cont[:].unsqueeze(1).to_broadcast([GH, 2, 128]),
                                  ALU.mult).then_inc(carried, 1)
                dve.wait_ge(turned_back, 1)
                done(dve.tensor_copy(carry[:], psC[:]))
                dve.wait_ge(fix_in, 16)
                head_of = lambda k: heads(carry[:, k, :])[:, :, 0]
                done(dve.tensor_tensor(fixed[:, 0:GHEADS], fix[:, 0:GHEADS], head_of(0), ALU.max))
                dve.tensor_tensor(fdrop[:, 0, :], fix[:, 0:GHEADS], fixed[:, 0:GHEADS], ALU.subtract)
                dve.tensor_tensor(fdrop[:, 1, :], head_of(0), fixed[:, 0:GHEADS], ALU.subtract).then_inc(fix_limited, 1)
                dve.wait_ge(fix_exped, 1)
                dve.tensor_tensor(old[:, 0:GHEADS], fix[:, GHEADS:2 * GHEADS], fw[:, 0, :], ALU.mult)
                dve.tensor_tensor(heads(old[:, GHEADS:]), heads(fix[:, 2 * GHEADS:]), spread(fw[:, 0, :]), ALU.mult)
                dve.tensor_tensor(new[:, 0:GHEADS], head_of(1), fw[:, 1, :], ALU.mult)
                done(dve.tensor_tensor(heads(new[:, GHEADS:]), heads(carry[:, 2, :]), spread(fw[:, 1, :]), ALU.mult))
                dve.tensor_tensor(fixed[:, GHEADS:], old[:], new[:], ALU.add).then_inc(fix_ready, 1)

            @block.tensor
            def _(pe):
                pe.wait_ge(const_in, 64)
                pe.wait_ge(widened, 1)
                for k in range(5):
                    m = pe.transpose(psT[:, k, :], wide[:, k, :], ident[:])
                m.then_inc(turned, 1)
                pe.wait_ge(carried, 1)
                for k in range(3):
                    m = pe.transpose(psC[:, k, :], carry_t[:, k, :], ident[0:GH, 0:GH])
                m.then_inc(turned_back, 1)

            @block.scalar
            def _(act):
                act.wait_ge(limited, 1)
                act.activation(weight[:], drop[:], ACT.Exp).then_inc(exped, 1)
                act.wait_ge(fix_limited, 1)
                act.activation(fw[:], fdrop[:], ACT.Exp).then_inc(fix_exped, 1)

def output_phase(nc, io, table_dram, adst_dram, sums_dram, y_dram, t2_dram, out_dram):
    with ExitStack() as ctx:
        sb = lambda name, shape, dt=F32: ctx.enter_context(nc.sbuf_tensor("g_" + name, shape, dt))
        sem = lambda name: ctx.enter_context(nc.semaphore(name))
        SLOTS, NCH = 4, JT // JC
        row = sb("row", [128, JT, ROW]); adst = sb("adst", [128, JT, GHEADS]); sums = sb("sums", [128, JT, STATE])
        consts = sb("consts", [128, 3, GH])
        score = sb("score", [128, JT, GHEADS]); top = sb("top", [128, JT, GHEADS])
        drop = sb("drop", [128, 2, JT, GHEADS]); weight = sb("weight", [128, 2, JT, GHEADS])
        den = sb("den", [128, JT, GHEADS]); own = sb("own", [128, JT, GH])
        stat = sb("stat", [128, 4, JT])
        best = sb("best", [128, JT, EXPERTS]); beaten = sb("beaten", [128, JT, EXPERTS]); won = sb("won", [128, JT])
        high = sb("high", [128, JT]); gate = sb("gate", [128, JT, EXPERTS]); rel = sb("rel", [128, JT, EXPERTS])
        y = [sb(f"y{i}", [128, JC, EXPERTS, C]) for i in range(SLOTS)]
        t2 = [sb(f"t2_{i}", [128, JC, C]) for i in range(SLOTS)]
        scaled = sb("scaled", [128, JC, EXPERTS, C]); mix = sb("mix", [128, JC, C])
        res = [sb(f"res{i}", [128, JC, C]) for i in range(SLOTS)]
        rows_in = sem("rows_in"); step = sem("step"); dropped = sem("dropped"); weighed = sem("weighed")
        varied = sem("varied"); rooted = sem("rooted"); related = sem("related"); exped = sem("exped")
        y_in = [sem(f"y_in{i}") for i in range(SLOTS)]; out_done = [sem(f"out_done{i}") for i in range(SLOTS)]
        scale_done = sem("scale_done"); mixed = sem("mixed"); res_ready = sem("res_ready")
        y_view = y_dram.rearrange("(p k j) (e c) -> k p j e c", p=128, j=JC, c=C)
        t2_view = t2_dram.rearrange("(p k j) c -> k p j c", p=128, j=JC)
        out_view = out_dram.rearrange("n h w c -> (n h w) c").rearrange("(p k j) c -> k p j c", p=128, j=JC)
        by_token = lambda a: a.rearrange("(p j) c -> p j c", p=128)
        heads = lambda a: a.rearrange("p j (h e) -> p j h e", e=EXPERTS)
        spread = lambda a: a.unsqueeze(3).to_broadcast([128, JT, GHEADS, EXPERTS])
        along = lambda a, n: a.unsqueeze(2).to_broadcast([128, JT, n])
        const = lambda k: consts[:, k, :].unsqueeze(1).to_broadcast([128, JT, GH])

        with nc.Block() as block:
            @block.sync
            def _(sp):
                sp.dma_start(row[:], by_token(table_dram)).then_inc(rows_in, 16)
                sp.dma_start(adst[:], by_token(adst_dram)).then_inc(rows_in, 16)
                sp.dma_start(sums[:], by_token(sums_dram)).then_inc(rows_in, 16)
                for k, name in enumerate(("b_gat", "ln_gamma", "ln_beta")):
                    sp.dma_start(consts[:, k, :], io[name].rearrange("(a h) -> a h", a=1).to_broadcast([128, GH])).then_inc(rows_in, 16)

                def load(turn, s):
                    sp.dma_start(y[s][:].rearrange("p j e c -> p j (e c)"), y_dram.rearrange("(p k j) c -> k p j c", p=128, j=JC)[turn * SLOTS + s]).then_inc(y_in[s], 16)
                    sp.dma_start(t2[s][:], t2_view[turn * SLOTS + s]).then_inc(y_in[s], 16)

                def out(turn, s):
                    sp.wait_ge(res_ready, turn * SLOTS + s + 1)
                    sp.dma_start(out_view[turn * SLOTS + s], res[s][:]).then_inc(out_done[s], 16)

                for s in range(SLOTS):
                    load(0, s)
                with sp.Fori(0, NCH // SLOTS - 1) as turn:
                    for s in range(SLOTS):
                        out(turn, s)
                        load(turn + 1, s)
                for s in range(SLOTS):
                    out(NCH // SLOTS - 1, s)
                for s in range(SLOTS):
                    sp.wait_ge(out_done[s], 16 * (NCH // SLOTS))

            @block.vector
            def _(dve):
                done = Link(dve, step)
                dve.wait_ge(rows_in, 96)
                done(dve.tensor_tensor(score[:], row[:, :, GH:ROW], adst[:], ALU.add))
                done(dve.scalar_tensor_tensor(top[:], score[:], 0.2, score[:], ALU.mult, ALU.max))
                done(dve.tensor_tensor(score[:], top[:], sums[:, :, 0:GHEADS], ALU.max))
                dve.tensor_tensor(drop[:, 0], sums[:, :, 0:GHEADS], score[:], ALU.subtract)
                dve.tensor_tensor(drop[:, 1], top[:], score[:], ALU.subtract).then_inc(dropped, 1)
                dve.wait_ge(weighed, 1)
                dve.tensor_tensor(den[:], sums[:, :, GHEADS:2 * GHEADS], weight[:, 0], ALU.mult)
                agg = sums[:, :, 2 * GHEADS:]
                dve.tensor_tensor(heads(agg), heads(agg), spread(weight[:, 0]), ALU.mult)
                done(dve.tensor_tensor(heads(own[:]), heads(row[:, :, 0:GH]), spread(weight[:, 1]), ALU.mult))
                done(dve.scalar_tensor_tensor(den[:], den[:], 1e-16, weight[:, 1], ALU.add, ALU.add))
                dve.reciprocal(den[:], den[:])
                done(dve.tensor_tensor(own[:], own[:], agg, ALU.add))
                done(dve.tensor_tensor(heads(own[:]), heads(own[:]), spread(den[:]), ALU.mult))
                done(dve.tensor_tensor(own[:], own[:], const(0), ALU.add))
                done(dve.tensor_reduce(stat[:, 0, :], own[:], AX.X, ALU.add))
                done(dve.tensor_scalar(stat[:, 0, :], stat[:, 0, :], -1.0 / GH, None, ALU.mult))
                done(dve.tensor_tensor(own[:], own[:], along(stat[:, 0, :], GH), ALU.add))
                done(dve.tensor_tensor(agg, own[:], own[:], ALU.mult))
                done(dve.tensor_reduce(stat[:, 1, :], agg, AX.X, ALU.add))
                dve.tensor_scalar(stat[:, 1, :], stat[:, 1, :], 1.0 / GH, LN_EPS, ALU.mult, ALU.add).then_inc(varied, 1)
                dve.wait_ge(rooted, 1)
                done(dve.reciprocal(stat[:, 3, :], stat[:, 2, :]))
                done(dve.tensor_tensor(own[:], own[:], along(stat[:, 3, :], GH), ALU.mult))
                done(dve.tensor_tensor(own[:], own[:], const(1), ALU.mult))
                done(dve.tensor_tensor(own[:], own[:], const(2), ALU.add))
                done(dve.tensor_reduce(best[:], own[:].rearrange("p j (h e) -> p j e h", e=EXPERTS), AX.X, ALU.add))
                dve.memset(beaten[:], 0.0)
                done(dve.tensor_scalar(best[:], best[:], 1.0 / GHEADS, None, ALU.mult))
                done(dve.tensor_reduce(high[:], best[:], AX.X, ALU.max))
                for a in range(EXPERTS):
                    for b in range(a + 1, EXPERTS):
                        done(dve.tensor_tensor(won[:], best[:, :, a], best[:, :, b], ALU.is_ge))
                        dve.tensor_tensor(beaten[:, :, b], beaten[:, :, b], won[:], ALU.add)
                        done(dve.scalar_tensor_tensor(beaten[:, :, a], beaten[:, :, a], 1.0, won[:], ALU.add, ALU.subtract))
                dve.tensor_tensor(rel[:], best[:], along(high[:], EXPERTS), ALU.subtract).then_inc(related, 1)
                done(dve.tensor_scalar(beaten[:], beaten[:], 2.0, None, ALU.is_lt))
                dve.wait_ge(exped, 1)
                done(dve.tensor_tensor(gate[:], gate[:], beaten[:], ALU.mult))
                done(dve.tensor_reduce(high[:], gate[:], AX.X, ALU.add))
                done(dve.reciprocal(high[:], high[:]))
                done(dve.tensor_tensor(gate[:], gate[:], along(high[:], EXPERTS), ALU.mult))
                with dve.Fori(0, NCH // SLOTS) as turn:
                    for s in range(SLOTS):
                        k = turn * SLOTS + s
                        dve.wait_ge(y_in[s], (turn + 1) * 32)
                        dve.tensor_tensor(scaled[:].rearrange("p j e c -> p (j e) c"), y[s][:].rearrange("p j e c -> p (j e) c"),
                                          gate[:].rearrange("p j e -> p (j e)")[:, bass.ds(k * (JC * EXPERTS), JC * EXPERTS)]
                                          .unsqueeze(2).to_broadcast([128, JC * EXPERTS, C]), ALU.mult).then_inc(scale_done, 1)
                        dve.wait_ge(scale_done, k + 1)
                        dve.tensor_reduce(mix[:], scaled[:].rearrange("p j e c -> p j c e"), AX.X, ALU.add).then_inc(mixed, 1)
                        dve.wait_ge(mixed, k + 1)
                        dve.wait_ge(out_done[s], turn * 16)
                        dve.tensor_tensor(res[s][:], mix[:], t2[s][:], ALU.add).then_inc(res_ready, 1)

            @block.scalar
            def _(act):
                act.wait_ge(dropped, 1)
                act.activation(weight[:], drop[:], ACT.Exp).then_inc(weighed, 1)
                act.wait_ge(varied, 1)
                act.activation(stat[:, 2, :], stat[:, 1, :], ACT.Sqrt).then_inc(rooted, 1)
                act.wait_ge(related, 1)
                act.activation(gate[:], rel[:], ACT.Exp).then_inc(exped, 1)

def host_layout(inputs):
    f = lambda a: np.ascontiguousarray(a)
    g = lambda name: np.asarray(inputs[name])
    conv = lambda name: g("L0_conv_" + name)
    bn = lambda j: f(np.stack([conv(k + j).reshape(128) for k in ("B", "G", "Be", "M", "V")], axis=1))
    x = g("x")
    out = {
        "x": f(x),
        "x_ch": f(x.reshape(N, H * W, C).transpose(2, 0, 1)),
        "w1": f(conv("W1").transpose(1, 0, 2).reshape(C, 128)),
        "w2": f(conv("W2").transpose(0, 3, 1, 2, 4).reshape(128, 9, DP)),
        "w3": f(conv("W3").reshape(128, C)),
        "bn1": bn("1"), "bn2": bn("2"),
        "bn3": f(np.stack([conv(k + "3").reshape(CHUNKS, 128).T for k in ("B", "G", "Be", "M", "V")], axis=1)),
        "bn3e": f(np.stack([np.repeat(conv(k + "3"), DP, axis=0) for k in ("G", "V")], axis=1)),
        "wqkv": f(g("L1_attn_W_qkv").T),
        "temperature": f(g("L1_attn_temperature")),
        "ident": np.eye(128, dtype=np.float32),
        "pathmask": np.kron(np.eye(PATHS), np.ones((DP, 1))).astype(np.float32),
        "fold": np.concatenate([np.eye(C)] * 2).astype(np.float32),
    }
    out["kfeat"], out["qfeat"] = mask_features()
    out["headmask"] = np.kron(np.eye(HEADS), np.ones((HD, 1))).astype(np.float32)
    out["outmask"] = np.kron(np.eye(HEADS), np.ones((QB, HD))).astype(np.float32)
    out["pick"] = np.tile(np.eye(QB), (HEADS, 1)).astype(np.float32)
    out["wproj"] = f(g("L1_attn_W_proj").T)
    out["bproj"] = f(g("L1_attn_b_proj"))
    ffn = lambda name: g("L1_ffn_" + name)
    out["wgat"], out["att_src"], out["att_dst"] = f(ffn("W_gat")), f(ffn("att_src")), f(ffn("att_dst"))
    for name in ("b_gat", "ln_gamma", "ln_beta"):
        out[name] = f(ffn(name))
    out["ffn_w1"] = f(ffn("W1").transpose(1, 0, 2))
    out["ffn_b1"] = f(ffn("b1").T)
    out["ffn_w2"] = f(ffn("W2").transpose(1, 0, 2))
    out["ffn_b2"] = f(ffn("b2").reshape(1, EXPERTS * C))
    out["edges"] = f(ffn("edge_index"))
    out["psign"] = partition_signs()
    out["before"] = np.triu(np.ones((128, 128)), 1).astype(np.float32)
    out["iota"] = np.tile(np.arange(128), (128, 1)).astype(np.float32)
    out["last_pos"] = (np.arange(128)[:, None] * EF + EF - 1).astype(np.float32)
    return out

def build_program(nc, io, out):
    dram = lambda name, shape, dt=F32: nc.dram_tensor("scratch_" + name, shape, dt, kind="Internal").ap()
    t1 = dram("t1", [TOKENS, C]); t2 = dram("t2", [TOKENS, C])
    q = dram("q", [C, N, H * W]); kpad = dram("kpad", [C, N, PH, PW]); vpad = dram("vpad", [N, PH, PW, C])
    key = dram("key", [128, EF]); turned = dram("turned", [128, EF]); ordered = dram("ordered", [128, EF])
    z = dram("z", [C, TOKENS]); table = dram("table", [TOKENS, ROW]); adst = dram("adst", [TOKENS, GHEADS])
    edge = dram("edge", [NFC, 128, 4, FC]); node = dram("node", [2, 128, 128], I32)
    first = dram("first", [128, 1], I32); ends = dram("ends", [128, 2])
    b = dram("b", [EDGES, GHEADS]); state = dram("state", [EDGES, STATE]); sums = dram("sums", [TOKENS, STATE])
    y = dram("y", [TOKENS, EXPERTS * C])

    conv_phase(nc, io, t1, q, kpad, vpad)
    attention_phase(nc, io, t1, q, kpad, vpad, t2)
    sort_phase(nc, io, key, turned, ordered)
    index_phase(nc, io, ordered, edge, node, first, ends)
    table_phase(nc, io, t2, z, table, adst)
    edge_phase(nc, io, z, table, adst, edge, node, first, b, state, y)
    join_phase(nc, io, state, node, first, ends, sums)
    output_phase(nc, io, table, adst, sums, y, t2, out)

def kernel(**inputs):
    from concourse import bacc
    from concourse.bass_utils import run_bass_kernel_spmd

    nc = bacc.Bacc("TRN2", target_bir_lowering=False, num_devices=1)
    arrays, io = {}, {}
    for name, a in host_layout(inputs).items():
        arrays["in_" + name] = a
        io[name] = nc.dram_tensor("in_" + name, a.shape, mybir.dt.from_np(a.dtype), kind="ExternalInput").ap()
    out = nc.dram_tensor("out", [N, H, W, C], F32, kind="ExternalOutput").ap()
    build_program(nc, io, out)
    result = run_bass_kernel_spmd(nc, [arrays], core_ids=[0])
    return result.results[0]["out"]
```

```python
from contextlib import ExitStack

import numpy as np

import concourse.bass as bass
from concourse import mybir

F32 = mybir.dt.float32
BF16 = mybir.dt.bfloat16
I32 = mybir.dt.int32
ALU = mybir.AluOpType
ACT = mybir.ActivationFunctionType
AX = mybir.AxisListType

N, H, W, C = 8, 56, 56, 64
PATHS, DP = 32, 4
CHUNKS = PATHS * C // 128
ROWS = 8
TILES = H // ROWS
PIX = ROWS * W
SUB = 4
TOK = PIX // SUB
TOKENS = N * H * W
BN_EPS, LN_EPS = 1e-3, 1e-5
HEADS, HD = 8, 8
HALO = 3
QROWS = QCOLS = 4
QB = QROWS * QCOLS
WIN = QROWS + 2 * HALO
KEYS = WIN * WIN
STRIPS = H // QROWS
BLOCKS = W // QCOLS
SPIX = QROWS * W
FEATURES = QROWS + 16
KROWS = C + FEATURES
PH, PW = H + 2 * HALO, W + 2 * HALO


def ahead(n, t, k):
    return n + (t + k) // TILES, (t + k) % TILES


def wait(eng, semaphore, value):
    if not isinstance(value, int) or value > 0:
        eng.wait_ge(semaphore, value)


class Link:

    def __init__(self, eng, semaphore):
        self.eng, self.semaphore, self.n = eng, semaphore, 0

    def __call__(self, instruction):
        self.n += 1
        instruction.then_inc(self.semaphore, 1)
        self.eng.wait_ge(self.semaphore, self.n)


class Strip:

    def __init__(self, turn, par):
        self.turn, self.par, self.i = turn, par, turn * 2 + par

    def step(self, k):
        return Strip(self.turn + (self.par + k) // 2, (self.par + k) % 2)


def mask_features():
    far = -float(2 ** 100)
    keys = np.zeros((STRIPS, FEATURES, WIN, PW), np.float32)
    for s in range(STRIPS):
        for ky in range(WIN):
            row = QROWS * s + ky - HALO
            for j in range(QROWS):
                if abs(ky - HALO - j) > HALO or not 0 <= row < H:
                    keys[s, j, ky, :] = far
    for x in range(PW):
        near = {c % 16 for c in range(W) if abs(c - (x - HALO)) <= HALO} if 0 <= x - HALO < W else set()
        for j in range(16):
            if j not in near:
                keys[:, QROWS + j, :, x] = far
    queries = np.zeros((FEATURES, BLOCKS, HEADS, QROWS, QCOLS), np.float32)
    for j in range(QROWS):
        queries[j, :, :, j, :] = 1
    for x in range(W):
        queries[QROWS + x % 16, x // QCOLS, :, :, x % QCOLS] = 1
    return keys.reshape(STRIPS, FEATURES, WIN * PW), queries.reshape(FEATURES, BLOCKS, HEADS, QB)


EDGES = 262144
EF = EDGES // 128
LOW = EF // 128
SRC_BITS = 15


def partition_signs():
    bits = (np.arange(128)[:, None] >> np.arange(8)) & 1
    cols = [bits[:, 0]] + [bits[:, j - 1] ^ bits[:, j] for j in range(1, 7)] + [bits[:, 6]]
    return (1 - 2 * np.stack(cols, axis=1)).astype(np.float32)


EXPERTS, GHEADS = 4, 4
GH = GHEADS * EXPERTS
NODES = 16384
ROW = GH + GHEADS
JT = TOKENS // 128
JC = 7
FAR = 3.0e38
MISS = float(1 << 20)
HIDE = 1.0e30

FC = 128
NFC = EF // FC
HOT = 8
AHEAD = 4
STATE = 2 * GHEADS + GH
ZT = 512

STACK = 9 * 2 * DP
REST_AT, LAST_PART_AT = 0, 3
SORT_SLOTS = (4, 5, 6, 7, 8, 9, 10, 11, 12)
TAPS_AT = (4, 5, 6, 7, 8, 9, 10, 11, 12)
FOLD_AT, TURN_AT, PROJECT_AT = 0, 2, 13
SORT_FIRST = 44


def clear(nc, semaphores):
    with nc.Block() as block:
        @block.gpsimd
        def _(pool):
            for s in semaphores:
                pool.sem_clear(s)


class Sort:

    HALVES = 4

    def __init__(self, key, other, psign, key_dram, turned_dram, stepped, moved):
        self.buffers, self.psign, self.drams = [key, other], psign, [key_dram, turned_dram]
        self.stepped, self.moved = stepped, moved
        self.plan = []
        col_bits = EF.bit_length() - 1
        all_bits = col_bits + 7
        self.plan.append(("negate", 4, 2, 4))
        for k in range(1, all_bits + 1):
            if k > col_bits:
                self.plan.append(("turn", 0))
                self.plan += [("compare", LOW << (j - col_bits)) for j in range(k - 1, col_bits - 1, -1)]
                self.plan.append(("turn", 1))
            self.plan += [("compare", 1 << j) for j in range(min(k, col_bits) - 1, -1, -1)]
            if k < col_bits - 1:
                self.plan.append(("negate", 4 << k, 1 << k, 3 << k))
            elif k == col_bits - 1:
                self.plan += [("negate", EF, EF // 2, EF), ("sign", 0)]
            elif k < all_bits:
                self.plan.append(("sign", k - col_bits + 1))
        self.flips = sum(step[0] in ("compare", "turn") for step in self.plan)
        self.result = self.buffers[self.flips % 2]
        self.steps = sum(step[0] != "turn" for step in self.plan)

    def vector_steps(self, dve):
        now, steps, moves = 0, 0, 0
        turned, out = False, []

        def one(kind, args, now, steps, moves, half):
            if half == 0:
                wait(dve, self.stepped, steps)
                wait(dve, self.moved, moves)
            x, y = self.buffers[now], self.buffers[1 - now]
            if kind == "negate":
                size, a, b = args
                v = x[:].rearrange("p (n q) -> p n q", q=size)[:, :, a:b]
                dve.tensor_scalar(v, v, -1.0, None, ALU.mult).then_inc(self.stepped, 1)
            elif kind == "sign":
                dve.tensor_scalar(x[:], x[:], self.psign[:, args[0]:args[0] + 1], None, ALU.mult).then_inc(self.stepped, 1)
            else:
                src = x[:].rearrange("p (n two d) -> p n two d", two=2, d=args[0])
                dst = y[:].rearrange("p (n two d) -> p n two d", two=2, d=args[0])
                if half == 0:
                    dve.tensor_tensor(dst[:, :, 0, :], src[:, :, 0, :], src[:, :, 1, :], ALU.min)
                else:
                    dve.tensor_tensor(dst[:, :, 1, :], src[:, :, 0, :], src[:, :, 1, :], ALU.max).then_inc(self.stepped, 1)

        for kind, *args in self.plan:
            if kind == "turn":
                moves += 16 * (1 + self.HALVES)
                now = 1 - now
                turned = True
                continue
            for half in range(2 if kind == "compare" else 1):
                out.append((lambda a=(kind, args, now, steps, moves, half): one(*a), turned))
                turned = False
            steps += 1
            if kind == "compare":
                now = 1 - now
        return out

    def turns(self, pool):
        now, steps, moves = 0, 0, 0
        size = 128 // self.HALVES
        for kind, *args in self.plan:
            if kind == "turn":
                dram = self.drams[args[0]]
                pool.wait_ge(self.stepped, steps)
                pool.dma_start(dram, self.buffers[now][:]).then_inc(self.moved, 16)
                moves += 16
                pool.wait_ge(self.moved, moves)
                src = dram.rearrange("p (h l) -> h p l", l=LOW)
                dst = self.buffers[1 - now][:].rearrange("h (p l) -> h p l", l=LOW)
                for k in range(self.HALVES):
                    pool.dma_start(dst[:, k * size:(k + 1) * size], src[:, k * size:(k + 1) * size]).then_inc(self.moved, 16)
                moves += 16 * self.HALVES
                now = 1 - now
                continue
            steps += 1
            if kind == "compare":
                now = 1 - now


def conv_phase(nc, io, t1_dram, q_dram, kpad_dram, vpad_dram, key_dram, turned_dram, sorted_dram):
    with ExitStack() as ctx:
        sb = lambda name, shape, dt=F32: ctx.enter_context(nc.sbuf_tensor(name, shape, dt))
        ps = lambda name, shape: ctx.enter_context(nc.psum_tensor(name, shape, F32))
        semaphores = []

        def sem(name):
            semaphores.append(ctx.enter_context(nc.semaphore(name)))
            return semaphores[-1]

        ident = sb("c_ident", [128, 128])
        pathmask = sb("c_pathmask", [128, PATHS])
        fold = sb("c_fold", [128, C])
        w1 = sb("c_w1", [C, 128])
        w2c = sb("c_w2c", [128, 9, DP])
        w2 = sb("c_w2", [128, 9, 128])
        w3c = sb("c_w3c", [128, C])
        pair = sb("c_pair", [128, 2])
        w3m = sb("c_w3m", [128, 2, C]); w3r = sb("c_w3r", [128, 2, C])
        w3p = sb("c_w3p", [128, 3, 2 * C], BF16)
        w3 = sb("c_w3", [STACK, CHUNKS, 2 * C], BF16)
        bn1 = sb("c_bn1", [128, 5])
        bn2 = sb("c_bn2", [128, 5])
        bn3 = sb("c_bn3", [128, 5, CHUNKS])
        bn3e = sb("c_bn3e", [128, 2, C])
        s1 = sb("c_s1", [128, 2])
        s2 = sb("c_s2", [128, 2])
        s3 = sb("c_s3", [128, CHUNKS])
        b3 = sb("c_b3", [128, CHUNKS])
        sumb3 = sb("c_sumb3", [128, 1])
        s3e = sb("c_s3e", [128, C])
        wqkv = sb("c_wqkv", [C, 3 * C])
        qscale = sb("c_qscale", [128, 1])
        zero = sb("c_zero", [C, PH * PW // 2])

        x_tok = sb("x_tok", [TOK, TILES, SUB, C])
        x_ch = sb("x_ch", [C, TILES, PIX])
        h1 = sb("h1", [128, H + 2, W + 2])
        h2 = sb("h2", [128, 3, PIX])
        h2r = sb("h2r", [128, PIX])
        h2p = sb("h2p", [128, 3, 3, PIX], BF16)
        stack = [sb(f"stack{k}", [STACK, CHUNKS, PIX], BF16) for k in range(3)]
        acc = sb("acc", [128, 3, PIX])
        usum = sb("usum", [TOK, SUB, C])
        t1 = sb("t1", [TOK, TILES, SUB, C])
        cen = sb("cen", [TOK, SUB, C])
        sq = sb("sq", [TOK, SUB, C])
        z = sb("z", [TOK, TILES, SUB, C])
        stat = sb("stat", [TOK, TILES, 6, SUB])
        z_ch = sb("z_ch", [C, TILES, PIX])
        qk = sb("qk", [128, TILES, PIX])
        v = sb("v", [TOK, TILES, SUB, C])

        sort_key = sb("sort_key", [128, EF]); sort_other = sb("sort_other", [128, EF]); signs = sb("signs", [128, 8])
        edges_in = sem("edges_in"); built = sem("built"); stepped = sem("stepped"); moved = sem("moved"); sorted_out = sem("sorted_out")
        sort = Sort(sort_key, sort_other, signs, key_dram, turned_dram, stepped, moved)

        psT = ps("psT", [128, 512])
        psH1 = ps("psH1", [128, 512])
        psH2 = ps("psH2", [128, 512])
        psE = [ps(f"psE{i}", [128, 512]) for i in range(2)]
        psF = ps("psF", [128, 512])
        psQK = ps("psQK", [128, 512])
        psV = ps("psV", [128, 512])

        passed = sem("passed")
        const_in = sem("const_in")
        x_loaded = [sem(f"x_loaded{t}") for t in range(TILES)]
        prep = sem("prep")
        prep_sqrt = sem("prep_sqrt")
        weights = sem("weights")
        a1_ready = sem("a1_ready"); h1_done = sem("h1_done")
        c_ready = sem("c_ready"); h2_done = sem("h2_done")
        e_ready = sem("e_ready"); stt_done = sem("stt_done")
        f_ready = sem("f_ready"); u_done = sem("u_done"); t1_done = sem("t1_done")
        ln_step = sem("ln_step"); var_done = sem("var_done"); std_done = sem("std_done"); z_done = sem("z_done")
        zt_ready = sem("zt_ready"); zt_done = sem("zt_done")
        qkv_ready = sem("qkv_ready"); qk_done = sem("qk_done"); v_done = sem("v_done")
        t1_stored = [sem(f"t1_stored{t}") for t in range(TILES)]
        qkv_stored = [sem(f"qkv_stored{t}") for t in range(TILES)]
        zero_set = sem("zero_set"); pad_stored = sem("pad_stored")

        x_view = io["x"].rearrange("n (t s r) w c -> n t (r w) s c", t=TILES, s=SUB)
        t1_view = t1_dram.rearrange("(n t s p) c -> n t p s c", n=N, t=TILES, s=SUB)
        xc_view = io["x_ch"].rearrange("c n (t q) -> n t c q", t=TILES)
        N_CONST = 13
        SLOT = (0, 1, 0, 1, 0, 1, 2)
        assert len(SLOT) == TILES
        stacked = [sem(f"stacked{t}") for t in range(TILES)]
        parts_out = [sem(f"parts_out{t}") for t in range(TILES)]; w3_out = sem("w3_out")
        parts_dram = nc.dram_tensor("scratch_parts", [3, 128, 3, PIX], BF16, kind="Internal").ap()
        w3_dram = nc.dram_tensor("scratch_w3", [128, 3, 2 * C], BF16, kind="Internal").ap()
        w3_in = sem("w3_in"); part_done = [sem(f"part_done{k}") for k in range(2)]; rest_done = sem("rest_done"); split_done = sem("split_done")
        by_chunk = lambda a: a.rearrange("(c k) x -> k c x", c=CHUNKS)
        HC = 2 * DP

        with nc.Block() as block:
            @block.sync
            def _(sp):
                loads = [(ident[:], io["ident"]), (pathmask[:], io["pathmask"]), (fold[:], io["fold"]),
                         (w1[:], io["w1"]), (w2c[:], io["w2"]), (w3c[:], io["w3"]),
                         (bn1[:], io["bn1"]), (bn2[:], io["bn2"]), (bn3[:], io["bn3"]), (bn3e[:], io["bn3e"]),
                         (pair[:], io["pair"]),
                         (wqkv[:], io["wqkv"]),
                         (qscale[0:C, :], io["temperature"].rearrange("(a b) -> a b", a=1).to_broadcast([C, 1]))]
                def load_x(n, t):
                    sp.dma_start(x_ch[:, t], xc_view[n, t]).then_inc(x_loaded[t], 16)
                    sp.dma_start(x_tok[:, t], x_view[n, t]).then_inc(x_loaded[t], 16)

                for dst, src in loads:
                    sp.dma_start(dst, src).then_inc(const_in, 16)
                assert len(loads) == N_CONST
                for t in range(TILES):
                    load_x(0, t)
                for k, a in enumerate((sort_key, sort_other)):
                    sp.dma_start(a[:].bitcast(I32), io["edges"][k].rearrange("(p f) -> p f", p=128)).then_inc(edges_in, 16)
                sp.dma_start(signs[:], io["psign"]).then_inc(edges_in, 16)

                sp.wait_ge(zero_set, 1)
                for n in range(N):
                    for pad in (kpad_dram[:, n].rearrange("c y x -> c (y x)"),
                                vpad_dram[n].rearrange("y x c -> (y x c)").rearrange("(p q) -> p q", p=C)):
                        for half in range(2):
                            size = PH * PW // 2
                            sp.dma_start(pad[:, half * size:(half + 1) * size], zero[:]).then_inc(pad_stored, 16)
                sp.wait_ge(pad_stored, 64 * N)

                def stores(n, t):
                    g = n * TILES + t
                    sp.wait_ge(t1_done, g + 1)
                    sp.dma_start(t1_view[n, t], t1[:, t]).then_inc(t1_stored[t], 16)
                    sp.wait_ge(qk_done, g + 1)
                    y0 = HALO + ROWS * t
                    sp.dma_start(q_dram[:, n, PIX * t:PIX * (t + 1)], qk[0:C, t]).then_inc(qkv_stored[t], 16)
                    sp.dma_start(kpad_dram[:, n, y0:y0 + ROWS, HALO:HALO + W],
                                 qk[C:2 * C, t].rearrange("c (y x) -> c y x", x=W)).then_inc(qkv_stored[t], 16)
                    sp.wait_ge(v_done, g + 1)
                    for r in range(2):
                        sp.dma_start(vpad_dram[n, y0 + r:y0 + ROWS:2, HALO:HALO + W, :].rearrange("s x c -> x s c"),
                                     v[r * W:(r + 1) * W, t]).then_inc(qkv_stored[t], 16)

                def image(n, last):
                    for t in range(TILES):
                        if not last:
                            sp.wait_ge(u_done, n * TILES + t + 1)
                            load_x(n + 1, t)
                        stores(n, t)

                with sp.Fori(0, N - 1) as n:
                    image(n, False)
                image(N - 1, True)
                sp.wait_ge(stepped, sort.steps)
                sp.dma_start(sorted_dram, sort.result[:]).then_inc(sorted_out, 16)
                sp.wait_ge(sorted_out, 16)
                for t in range(TILES):
                    sp.wait_ge(t1_stored[t], 16 * N)
                    sp.wait_ge(qkv_stored[t], 64 * N)

            @block.gpsimd
            def _(pool):
                pool.memset(zero[:], 0.0).then_inc(zero_set, 1)
                pool.memset(h1[:], 0.0).then_inc(zero_set, 1)
                sort.turns(pool)

            @block.tensor
            def _(pe):
                pe.wait_ge(const_in, 16 * N_CONST)
                pe.wait_ge(weights, 1)
                pe.wait_ge(prep_sqrt, 4)
                pe.wait_ge(zero_set, 2)
                pe.wait_ge(w3_in, 16 * 9)

                def reduce_1x1(n, t):
                    g = n * TILES + t
                    pe.wait_ge(x_loaded[t], 32 * (n + 1))
                    wait(pe, h1_done, g)
                    pe.matmul(psH1[:, 0:PIX], w1[:], x_ch[:, t], start=True, stop=True).then_inc(a1_ready, 1)

                def conv3(n, t):
                    g = n * TILES + t

                    def one(tap):
                        if tap == 0:
                            pe.wait_ge(h1_done, g + (2 if t < TILES - 1 else 1))
                            wait(pe, h2_done, g)
                        dy, dx = divmod(tap, 3)
                        m = pe.matmul(psH2[:, 0:PIX].rearrange("p (y x) -> p y x", x=W), w2[:, tap, :],
                                      h1[:, ROWS * t + dy:ROWS * (t + 1) + dy, dx:dx + W],
                                      start=(tap == 0), stop=(tap == 8))
                        if tap == 8:
                            m.then_inc(c_ready, 1)

                    return [lambda tap=tap: one(tap) for tap in range(9)]

                def expand(n, t, taps, others):
                    g = n * TILES + t
                    pe.wait_ge(stacked[t], 16 * 9 * (n + 1))
                    for c in range(CHUNKS):
                        wait(pe, stt_done, g * CHUNKS + c - 1)
                        pe.matmul(psE[c % 2][:, 0:PIX], w3[:, c, :], stack[SLOT[t]][:, c, :],
                                  start=True, stop=True).then_inc(e_ready, 1)
                        if c in TAPS_AT and taps:
                            taps.pop(0)()
                        if c in others:
                            others[c]()
                    while taps:
                        taps.pop(0)()

                def to_tokens(n, t):
                    g = n * TILES + t
                    pe.wait_ge(stt_done, (g + 1) * CHUNKS)
                    wait(pe, u_done, g)
                    for s in range(SUB):
                        m = pe.matmul(psF[0:TOK, s * C:(s + 1) * C], acc[:, SLOT[t], s * TOK:(s + 1) * TOK], fold[:],
                                      start=True, stop=True)
                    m.then_inc(f_ready, 1)

                def z_to_channels(n, t):
                    g = n * TILES + t
                    pe.wait_ge(z_done, g + 1)
                    wait(pe, zt_done, g)
                    pe.sem_inc(passed, 1)
                    for s in range(SUB):
                        m = pe.transpose(psT[0:C, s * TOK:(s + 1) * TOK], z[:, t, s, :], ident[0:TOK, 0:TOK])
                    m.then_inc(zt_ready, 1)

                def project(n, t):
                    g = n * TILES + t
                    pe.wait_ge(zt_done, g + 1)
                    wait(pe, qk_done, g)
                    pe.matmul(psQK[:, 0:PIX], wqkv[:, 0:128], z_ch[:, t], start=True, stop=True).then_inc(qkv_ready, 1)
                    wait(pe, v_done, g)
                    for s in range(SUB):
                        m = pe.matmul(psV[0:TOK, s * C:(s + 1) * C], z_ch[:, t, s * TOK:(s + 1) * TOK], wqkv[:, 128:192],
                                      start=True, stop=True)
                    m.then_inc(qkv_ready, 1)

                def image(n, first, last):
                    for t in range(TILES):
                        if not (last and t + 3 >= TILES):
                            reduce_1x1(*ahead(n, t, 3))
                        others = {}
                        if not (first and t == 0):
                            others[FOLD_AT] = lambda at=ahead(n, t, -1): to_tokens(*at)
                        if not (first and t <= 1):
                            others[TURN_AT] = lambda at=ahead(n, t, -2): z_to_channels(*at)
                            others[PROJECT_AT] = lambda at=ahead(n, t, -2): project(*at)
                        expand(n, t, [] if last and t + 2 >= TILES else conv3(*ahead(n, t, 2)), others)

                for t in range(3):
                    reduce_1x1(0, t)
                for t in range(2):
                    for tap in conv3(0, t):
                        tap()
                image(0, True, False)
                with pe.Fori(1, N - 1) as n:
                    image(n, False, False)
                image(N - 1, False, True)
                to_tokens(N - 1, TILES - 1)
                for t in range(TILES - 2, TILES):
                    z_to_channels(N - 1, t)
                    project(N - 1, t)

            @block.scalar
            def _(act):
                for k, (dst, src) in enumerate([(s1[:, 0:1], bn1[:, 4:5]), (s2[:, 0:1], bn2[:, 4:5]), (s3[:], bn3[:, 4, :]), (s3e[:], bn3e[:, 1, :])]):
                    act.wait_ge(prep, 1)
                    act.activation(dst, src, ACT.Sqrt).then_inc(prep_sqrt, 1)
                act.wait_ge(weights, 1)
                act.wait_ge(zero_set, 2)
                act.dma_start(w3_dram, w3p[:]).then_inc(w3_out, 16)
                act.wait_ge(w3_out, 16)
                for j in range(3):
                    for i in range(3):
                        at = (3 * j + i) * HC
                        act.dma_start(w3[at:at + HC], by_chunk(w3_dram[:, j])).then_inc(w3_in, 16)

                def h1_relu(n, t):
                    g = n * TILES + t
                    act.wait_ge(a1_ready, g + 1)
                    act.activation(h1[:, ROWS * t + 1:ROWS * (t + 1) + 1, 1:W + 1],
                                   psH1[:, 0:PIX].rearrange("p (y x) -> p y x", x=W),
                                   ACT.Relu, bias=s1[:, 1:2], scale=s1[:, 0:1]).then_inc(h1_done, 1)

                def h2_relu(n, t):
                    act.wait_ge(c_ready, n * TILES + t + 1)
                    act.activation(h2[:, SLOT[t]], psH2[:, 0:PIX], ACT.Relu, bias=s2[:, 1:2], scale=s2[:, 0:1]).then_inc(h2_done, 1)
                    act.wait_ge(h2_done, n * TILES + t + 1)
                    act.activation(h2p[:, SLOT[t], 0], h2[:, SLOT[t]], ACT.Copy).then_inc(part_done[0], 1)

                def second_part(n, t):
                    act.wait_ge(rest_done, n * TILES + t + 1)
                    act.activation(h2p[:, SLOT[t], 1], h2r[:], ACT.Copy).then_inc(part_done[1], 1)

                def store_parts(n, t):
                    act.wait_ge(split_done, n * TILES + t + 1)
                    act.dma_start(parts_dram[SLOT[t]], h2p[:, SLOT[t]]).then_inc(parts_out[t], 16)

                def stack_parts(n, t):
                    act.wait_ge(parts_out[t], 16 * (n + 1))
                    for j in range(3):
                        for i in range(3):
                            at = (3 * j + i) * HC
                            act.dma_start(stack[SLOT[t]][at:at + HC], by_chunk(parts_dram[SLOT[t], :, i])).then_inc(stacked[t], 16)

                def relu(n, t, first):
                    if not first:
                        act.wait_ge(t1_stored[t], 16 * n)
                    act.wait_ge(u_done, n * TILES + t + 1)
                    act.activation(t1[:, t], usum[:], ACT.Relu).then_inc(t1_done, 1)

                def layernorm(n, t):
                    g = n * TILES + t
                    act.wait_ge(var_done, g + 1)
                    act.activation(stat[:, t, 4], stat[:, t, 3], ACT.Sqrt).then_inc(std_done, 1)

                def turned(n, t):
                    act.wait_ge(zt_ready, n * TILES + t + 1)
                    act.activation(z_ch[:, t], psT[0:C, 0:PIX], ACT.Copy).then_inc(zt_done, 1)

                def qkv(n, t, first):
                    g = n * TILES + t
                    if not first:
                        act.wait_ge(qkv_stored[t], 64 * n)
                    act.wait_ge(qkv_ready, 2 * g + 1)
                    act.activation(qk[C:2 * C, t], psQK[C:2 * C, 0:PIX], ACT.Copy)
                    for s in range(PIX // SPIX):
                        m = act.activation(qk[0:C, t, s * SPIX:(s + 1) * SPIX].rearrange("c (b y x) -> c y b x", y=QROWS, x=QCOLS),
                                           psQK[0:C, s * SPIX:(s + 1) * SPIX].rearrange("c (y b x) -> c y b x", y=QROWS, x=QCOLS),
                                           ACT.Copy, scale=qscale[0:C, 0:1])
                    m.then_inc(qk_done, 1)
                    act.wait_ge(qkv_ready, 2 * g + 2)
                    act.activation(v[:, t], psV[0:TOK, 0:SUB * C].rearrange("p (s c) -> p s c", c=C), ACT.Copy).then_inc(v_done, 1)

                def image(n, first, last):
                    for t in range(TILES):
                        if not (last and t + 3 >= TILES):
                            h1_relu(*ahead(n, t, 3))
                        if not (last and t + 1 >= TILES):
                            second_part(*ahead(n, t, 1))
                            store_parts(*ahead(n, t, 1))
                        if not (first and t == 0):
                            relu(*ahead(n, t, -1), first)
                        if not (first and t <= 1):
                            turned(*ahead(n, t, -2))
                        if not (last and t + 1 >= TILES):
                            stack_parts(*ahead(n, t, 1))
                        if not (first and t <= 1):
                            qkv(*ahead(n, t, -2), first)
                        if not (last and t + 2 >= TILES):
                            h2_relu(*ahead(n, t, 2))
                        if not (first and t == 0):
                            layernorm(*ahead(n, t, -1))

                for t in range(3):
                    h1_relu(0, t)
                h2_relu(0, 0)
                h2_relu(0, 1)
                second_part(0, 0)
                store_parts(0, 0)
                stack_parts(0, 0)
                image(0, True, False)
                with act.Fori(1, N - 1) as n:
                    image(n, False, False)
                image(N - 1, False, True)
                turned(N - 1, TILES - 2)
                relu(N - 1, TILES - 1, False)
                qkv(N - 1, TILES - 2, False)
                layernorm(N - 1, TILES - 1)
                turned(N - 1, TILES - 1)
                qkv(N - 1, TILES - 1, False)

            @block.vector
            def _(dve):
                dve.wait_ge(const_in, 16 * N_CONST)
                link = Link(dve, ln_step)
                for variance in (bn1[:, 4:5], bn2[:, 4:5], bn3[:, 4, :]):
                    dve.tensor_scalar(variance, variance, BN_EPS, None, ALU.add)
                dve.tensor_scalar(qscale[C:2 * C, :], pathmask[C:2 * C, 0:1], 0.0, 1.0, ALU.mult, ALU.add)
                dve.tensor_scalar(qscale[0:C, :], qscale[0:C, :], float(HD) ** -0.5, None, ALU.mult)
                dve.tensor_scalar(bn3e[:, 1, :], bn3e[:, 1, :], BN_EPS, None, ALU.add).then_inc(prep, 1)
                dve.wait_ge(prep_sqrt, 4)
                for d in (s1[:, 0:1], s2[:, 0:1], s3[:], s3e[:]):
                    m = dve.reciprocal(d, d)
                link(m)
                dve.tensor_tensor(s1[:, 0:1], s1[:, 0:1], bn1[:, 1:2], ALU.mult)
                dve.tensor_tensor(s2[:, 0:1], s2[:, 0:1], bn2[:, 1:2], ALU.mult)
                dve.tensor_tensor(s3[:], s3[:], bn3[:, 1, :], ALU.mult)
                dve.tensor_tensor(s3e[:], s3e[:], bn3e[:, 0, :], ALU.mult)
                dve.tensor_tensor(s1[:, 1:2], bn1[:, 0:1], bn1[:, 3:4], ALU.subtract)
                dve.tensor_tensor(s2[:, 1:2], bn2[:, 0:1], bn2[:, 3:4], ALU.subtract)
                link(dve.tensor_tensor(b3[:], bn3[:, 0, :], bn3[:, 3, :], ALU.subtract))
                dve.tensor_tensor(s1[:, 1:2], s1[:, 1:2], s1[:, 0:1], ALU.mult)
                dve.tensor_tensor(s2[:, 1:2], s2[:, 1:2], s2[:, 0:1], ALU.mult)
                dve.tensor_tensor(w3c[:], w3c[:], s3e[:], ALU.mult)
                link(dve.tensor_tensor(b3[:], b3[:], s3[:], ALU.mult))
                dve.tensor_tensor(s1[:, 1:2], s1[:, 1:2], bn1[:, 2:3], ALU.add)
                dve.tensor_tensor(s2[:, 1:2], s2[:, 1:2], bn2[:, 2:3], ALU.add)
                link(dve.tensor_tensor(b3[:], b3[:], bn3[:, 2, :], ALU.add))
                link(dve.tensor_reduce(sumb3[:], b3[:], AX.X, ALU.add))
                link(dve.tensor_scalar(b3[:], b3[:], -1.0, None, ALU.mult))
                for tap in range(9):
                    dve.tensor_tensor(w2[:, tap, :].rearrange("p (q d) -> p q d", d=DP),
                                      w2c[:, tap:tap + 1, :].to_broadcast([128, PATHS, DP]),
                                      pathmask[:].unsqueeze(2).to_broadcast([128, PATHS, DP]), ALU.mult)
                link(dve.tensor_tensor(w3m[:], w3c[:].unsqueeze(1).to_broadcast([128, 2, C]),
                                       pair[:].unsqueeze(2).to_broadcast([128, 2, C]), ALU.mult))
                link(dve.tensor_copy(w3p[:, 0, :].rearrange("p (a c) -> p a c", a=2), w3m[:]))
                link(dve.tensor_tensor(w3r[:], w3m[:], w3p[:, 0, :].rearrange("p (a c) -> p a c", a=2), ALU.subtract))
                link(dve.tensor_copy(w3p[:, 1, :].rearrange("p (a c) -> p a c", a=2), w3r[:]))
                dve.tensor_tensor(w3p[:, 2, :].rearrange("p (a c) -> p a c", a=2), w3r[:], w3p[:, 1, :].rearrange("p (a c) -> p a c", a=2), ALU.subtract).then_inc(weights, 1)
                base = link.n
                LN_STEPS = 6

                def layernorm_ops(n, t):
                    g = n * TILES + t
                    at = lambda k: g * LN_STEPS + base + k
                    st = lambda j: stat[:, t, j]
                    bc = lambda j: stat[:, t, j].unsqueeze(2).to_broadcast([TOK, SUB, C])

                    def residual():
                        dve.wait_ge(f_ready, g + 1)
                        dve.tensor_tensor(usum[:], psF[0:TOK, 0:SUB * C].rearrange("p (s c) -> p s c", c=C),
                                          x_tok[:, t], ALU.add).then_inc(u_done, 1)

                    def total():
                        dve.wait_ge(t1_done, g + 1)
                        dve.tensor_reduce(st(0), t1[:, t], AX.X, ALU.add).then_inc(ln_step, 1)

                    def minus_mean():
                        dve.wait_ge(ln_step, at(1))
                        dve.tensor_scalar(st(1), st(0), -1.0 / C, None, ALU.mult).then_inc(ln_step, 1)

                    def center():
                        dve.wait_ge(ln_step, at(2))
                        dve.tensor_tensor(cen[:], t1[:, t], bc(1), ALU.add).then_inc(ln_step, 1)

                    def square():
                        dve.wait_ge(ln_step, at(3))
                        dve.tensor_tensor(sq[:], cen[:], cen[:], ALU.mult).then_inc(ln_step, 1)

                    def squares():
                        dve.wait_ge(ln_step, at(4))
                        dve.tensor_reduce(st(2), sq[:], AX.X, ALU.add).then_inc(ln_step, 1)

                    def variance():
                        dve.wait_ge(ln_step, at(5))
                        dve.tensor_scalar(st(3), st(2), 1.0 / C, LN_EPS, ALU.mult, ALU.add).then_inc(var_done, 1)

                    def inverse():
                        dve.wait_ge(std_done, g + 1)
                        dve.reciprocal(st(5), st(4)).then_inc(ln_step, 1)

                    def scale():
                        dve.wait_ge(ln_step, at(6))
                        dve.tensor_tensor(z[:, t], cen[:], bc(5), ALU.mult).then_inc(z_done, 1)

                    return [residual, total, minus_mean, center, square, squares, variance, inverse, scale]

                dve.wait_ge(edges_in, 48)
                dst = sort_other[:].bitcast(I32)
                dve.tensor_scalar(dst, dst, SRC_BITS, 1 << 30, ALU.logical_shift_left, ALU.bitwise_or).then_inc(built, 1)
                dve.wait_ge(built, 1)
                dve.tensor_tensor(sort_key[:].bitcast(I32), dst, sort_key[:].bitcast(I32), ALU.bitwise_or).then_inc(built, 1)
                dve.wait_ge(built, 2)
                sort_at = {}
                slot = 0
                steps = sort.vector_steps(dve)
                for step, _ in steps[:SORT_FIRST]:
                    step()
                for step, turned in steps[SORT_FIRST:]:
                    slot += len(SORT_SLOTS) if turned else 1
                    sort_at[slot] = step

                def rest(n, t):
                    g = n * TILES + t
                    dve.wait_ge(part_done[0], g + 1)
                    wait(dve, split_done, g)
                    dve.tensor_tensor(h2r[:], h2[:, SLOT[t]], h2p[:, SLOT[t], 0], ALU.subtract).then_inc(rest_done, 1)

                def last_part(n, t):
                    g = n * TILES + t
                    dve.wait_ge(part_done[1], g + 1)
                    dve.tensor_tensor(h2p[:, SLOT[t], 2], h2r[:], h2p[:, SLOT[t], 1], ALU.subtract).then_inc(split_done, 1)

                def tile(n, t, pending):
                    g = n * TILES + t
                    for c in range(CHUNKS):
                        for k, at in enumerate(SORT_SLOTS):
                            if at == c and g * len(SORT_SLOTS) + k in sort_at:
                                sort_at.pop(g * len(SORT_SLOTS) + k)()
                        if g + 1 < N * TILES:
                            if c == REST_AT:
                                rest(*ahead(n, t, 1))
                            if c == LAST_PART_AT:
                                last_part(*ahead(n, t, 1))
                        dve.wait_ge(e_ready, g * CHUNKS + c + 1)
                        if c == 0:
                            dve.tensor_scalar(acc[:, SLOT[t]], psE[0][:, 0:PIX], b3[:, 0:1], sumb3[:, 0:1], ALU.max, ALU.add)\
                               .then_inc(stt_done, 1)
                        else:
                            dve.wait_ge(stt_done, g * CHUNKS + c)
                            dve.scalar_tensor_tensor(acc[:, SLOT[t]], psE[c % 2][:, 0:PIX], b3[:, c:c + 1], acc[:, SLOT[t]],
                                                     ALU.max, ALU.add).then_inc(stt_done, 1)
                        if c % 2 == 0 and c >= 2 or c >= 14:
                            if pending:
                                pending.pop(0)()
                    while pending:
                        pending.pop(0)()

                rest(0, 0)
                last_part(0, 0)
                for n in range(N):
                    for t in range(TILES):
                        tile(n, t, [] if n == 0 and t == 0 else layernorm_ops(*ahead(n, t, -1)))
                for op in layernorm_ops(N - 1, TILES - 1):
                    op()
                for at in sorted(sort_at):
                    sort_at[at]()

        clear(nc, semaphores)


def attention_phase(nc, io, t1_dram, q_dram, kpad_dram, vpad_dram, t2_dram):
    with ExitStack() as ctx:
        sb = lambda name, shape, dt=F32: ctx.enter_context(nc.sbuf_tensor(name, shape, dt))
        sb2 = lambda name, shape: [sb(f"{name}{i}", shape) for i in range(2)]
        ps = lambda name, shape: ctx.enter_context(nc.psum_tensor(name, shape, F32))
        semaphores = []

        def sem(name):
            semaphores.append(ctx.enter_context(nc.semaphore(name)))
            return semaphores[-1]

        ident = sb("a_ident", [128, 128])
        headmask = sb("a_headmask", [2 * C, HEADS])
        wproj = sb("a_wproj", [C, C])
        bproj = sb("a_bproj", [TOK, C])

        keys = sb2("keys", [KROWS, WIN * PW])
        q = sb2("q", [C, SPIX])
        q_exp = sb2("q_exp", [KROWS, BLOCKS, HEADS, QB])
        val = sb2("val", [KEYS, BLOCKS, 2 * C])
        t1 = sb2("t1", [TOK, 2, C])
        prob = sb2("prob", [128, BLOCKS * KEYS])
        mx = sb2("mx", [128, BLOCKS])
        prob_t = sb("prob_t", [KEYS, BLOCKS, 128])
        own = sb2("own", [2 * C, 4, HEADS, QB])
        sums = sb("sums", [2 * C, BLOCKS, QB])
        inv = sb("inv", [C, BLOCKS, QB])
        o_ch = sb2("o_ch", [C, SPIX])
        t2a = sb2("t2a", [TOK, 2, C])
        t2 = sb2("t2", [TOK, 2, C])

        psS = [ps(f"psS{i}", [128, 512]) for i in range(3)]
        psP = [ps(f"psP{i}", [128, 512]) for i in range(2)]
        psO = [ps(f"psO{i}", [128, 512]) for i in range(2)]
        psM = ps("psM", [128, 512])
        BANKS = [(0, 5), (5, 10), (10, 14)]
        GROUPS = [(0, 4), (4, 8), (8, 12), (12, 14)]

        const_in = sem("const_in")
        ones_set = sem("ones_set")
        kq_loaded = [sem(f"kq_loaded{i}") for i in range(2)]
        v_loaded = [sem(f"v_loaded{i}") for i in range(2)]
        t1_loaded = [sem(f"t1_loaded{i}") for i in range(2)]
        t2_stored = [sem(f"t2_stored{i}") for i in range(2)]
        exp_q = sem("exp_q"); s_ready = sem("s_ready"); mx_done = sem("mx_done"); sub_done = sem("sub_done")
        exp_done = sem("exp_done"); pt_ready = sem("pt_ready"); pt_done = sem("pt_done")
        pv_ready = sem("pv_ready"); own_done = sem("own_done"); summed = sem("summed"); inv_done = sem("inv_done")
        o_done = sem("o_done"); pr_ready = sem("pr_ready")
        t2a_done = sem("t2a_done"); t2_done = sem("t2_done")

        t1_view = t1_dram.rearrange("(i r p) c -> i p r c", r=2, p=TOK)
        t2_view = t2_dram.rearrange("(i r p) c -> i p r c", r=2, p=TOK)
        consts = [(ident[:], "ident"), (headmask[0:C], "headmask"), (headmask[C:2 * C], "headmask"), (wproj[:], "wproj")]
        N_CONST = len(consts) + 1 + 2
        PAIRS = N * STRIPS // 2

        def windows(n, y):
            row = vpad_dram[n, bass.ds(y, 1)]
            return bass.AP(row.tensor, row.offset, [[C, WIN], [QCOLS * C, BLOCKS], [1, C]])

        def every_strip(eng, step):
            step(Strip(0, 0), True, False)
            step(Strip(0, 1), False, False)
            with eng.Fori(1, PAIRS - 1) as turn:
                step(Strip(turn, 0), False, False)
                step(Strip(turn, 1), False, False)
            step(Strip(PAIRS - 1, 0), False, False)
            step(Strip(PAIRS - 1, 1), False, True)

        with nc.Block() as block:
            @block.sync
            def _(sp):
                for dst, name in consts:
                    sp.dma_start(dst, io[name]).then_inc(const_in, 16)
                sp.dma_start(bproj[:], io["bproj"].rearrange("(a b) -> a b", a=1).to_broadcast([TOK, C])).then_inc(const_in, 16)
                for par in range(2):
                    sp.dma_start(q_exp[par][C:KROWS], io["qfeat"]).then_inc(const_in, 16)

                def loads(n, s, par, i):
                    wait(sp, s_ready, 3 * i - 3)
                    sp.dma_start(keys[par][0:C, :],
                                 kpad_dram[:, n, bass.ds(s * QROWS, WIN), :].rearrange("c y x -> c (y x)")).then_inc(kq_loaded[par], 16)
                    sp.dma_start(keys[par][C:KROWS, :], io["kfeat"][bass.ds(s, 1)].rearrange("o f x -> (o f) x")).then_inc(kq_loaded[par], 16)
                    wait(sp, exp_q, i - 1)
                    sp.dma_start(q[par][:], q_dram[:, n, bass.ds(s * SPIX, SPIX)]).then_inc(kq_loaded[par], 16)
                    wait(sp, pv_ready, 4 * i - 4)
                    for ky in range(WIN):
                        sp.dma_start(val[par][ky * WIN:(ky + 1) * WIN, :, 0:C], windows(n, s * QROWS + ky)).then_inc(v_loaded[par], 16)

                sp.wait_ge(ones_set, 2)
                for par in range(2):
                    loads(0, par, par, par)
                with sp.Fori(1, STRIPS // 2) as pair:
                    for par in range(2):
                        loads(0, pair * 2 + par, par, pair * 2 + par)
                with sp.Fori(1, N) as n:
                    with sp.Fori(0, STRIPS // 2) as pair:
                        for par in range(2):
                            loads(n, pair * 2 + par, par, n * STRIPS + pair * 2 + par)

            @block.gpsimd
            def _(pool):
                for par in range(2):
                    pool.memset(val[par][:], 1.0).then_inc(ones_set, 1)
                pool.wait_ge(const_in, 16 * N_CONST)

                def spread_q(st):
                    i, par = st.i, st.par
                    pool.wait_ge(kq_loaded[par], 48 * (st.turn + 1))
                    wait(pool, s_ready, 3 * i - 3)
                    pool.tensor_tensor(q_exp[par][0:C],
                                       q[par][:].rearrange("c (b m) -> c b m", m=QB).unsqueeze(2).to_broadcast([C, BLOCKS, HEADS, QB]),
                                       headmask[0:C].unsqueeze(1).unsqueeze(3).to_broadcast([C, BLOCKS, HEADS, QB]),
                                       ALU.mult).then_inc(exp_q, 1)

                def add_bias(st):
                    i, par = st.i, st.par
                    pool.wait_ge(t2a_done, i + 1)
                    wait(pool, t2_stored[par], 16 * (st.turn))
                    pool.tensor_tensor(t2[par][:], t2a[par][:], bproj[:].unsqueeze(1).to_broadcast([TOK, 2, C]), ALU.add)\
                        .then_inc(t2_done, 1)
                    pool.wait_ge(t2_done, i + 1)
                    pool.dma_start(t2_view[i], t2[par][:]).then_inc(t2_stored[par], 16)

                def step(st, first, last):
                    if not last and not (isinstance(st.turn, int) and st.turn == PAIRS - 1):
                        spread_q(st.step(2))
                    if not first:
                        add_bias(st.step(-1))

                spread_q(Strip(0, 0))
                spread_q(Strip(0, 1))
                every_strip(pool, step)
                add_bias(Strip(PAIRS - 1, 1))
                for par in range(2):
                    pool.wait_ge(t2_stored[par], 16 * PAIRS)

            @block.tensor
            def _(pe):
                pe.wait_ge(const_in, 16 * N_CONST)

                def scores(st):
                    i, par = st.i, st.par
                    pe.wait_ge(exp_q, i + 1)
                    pe.wait_ge(kq_loaded[par], 48 * (st.turn + 1))
                    for bank, (a, b) in enumerate(BANKS):
                        wait(pe, sub_done, 3 * i - 3 + bank + 1)
                        for blk in range(a, b):
                            x = blk * QCOLS
                            m = pe.matmul(psS[bank][:, (blk - a) * KEYS:(blk - a + 1) * KEYS],
                                          q_exp[par][:, blk].rearrange("k h m -> k (h m)"),
                                          keys[par][:].rearrange("k (y x) -> k y x", x=PW)[:, :, x:x + WIN],
                                          start=True, stop=True)
                        m.then_inc(s_ready, 1)

                def turn_probs(st):
                    i, par = st.i, st.par
                    for k, (a, b) in enumerate(GROUPS):
                        pe.wait_ge(exp_done, 3 * i + (1, 2, 3, 3)[k])
                        wait(pe, pt_done, 4 * i + k - 1)
                        for blk in range(a, b):
                            m = pe.transpose(psP[k % 2][0:KEYS, (blk - a) * 128:(blk - a + 1) * 128],
                                             prob[par][:, blk * KEYS:(blk + 1) * KEYS], ident[:])
                        m.then_inc(pt_ready, 1)

                def weigh_values(st):
                    i, par = st.i, st.par
                    pe.wait_ge(v_loaded[par], 16 * WIN * (st.turn + 1))
                    for k, (a, b) in enumerate(GROUPS):
                        pe.wait_ge(pt_done, 4 * i + k + 1)
                        wait(pe, own_done, 4 * i + k - 1)
                        for blk in range(a, b):
                            m = pe.matmul(psO[k % 2][:, (blk - a) * 128:(blk - a + 1) * 128], val[par][:, blk, :],
                                          prob_t[:, blk, :], start=True, stop=True)
                        m.then_inc(pv_ready, 1)

                def project(st):
                    i, par = st.i, st.par
                    pe.wait_ge(o_done, i + 1)
                    wait(pe, t2a_done, i)
                    for r in range(2):
                        m = pe.matmul(psM[0:TOK, SPIX + r * C:SPIX + (r + 1) * C], o_ch[par][:, r * TOK:(r + 1) * TOK], wproj[:],
                                      start=True, stop=True)
                    m.then_inc(pr_ready, 1)

                def step(st, first, last):
                    turn_probs(st)
                    if not last:
                        scores(st.step(1))
                    if not first:
                        project(st.step(-1))
                    weigh_values(st)

                scores(Strip(0, 0))
                every_strip(pe, step)
                project(Strip(PAIRS - 1, 1))

            @block.scalar
            def _(act):
                def exponentials(st):
                    i, par = st.i, st.par
                    for bank, (a, b) in enumerate(BANKS):
                        act.wait_ge(sub_done, 3 * i + bank + 1)
                        p = prob[par][:, a * KEYS:b * KEYS]
                        act.activation(p, p, ACT.Exp).then_inc(exp_done, 1)

                def copy_probs(st):
                    i, par = st.i, st.par
                    for k, (a, b) in enumerate(GROUPS):
                        act.wait_ge(pt_ready, 4 * i + k + 1)
                        if k == 0:
                            wait(act, pv_ready, 4 * i)
                        act.activation(prob_t[:, a:b, :], psP[k % 2][0:KEYS, 0:(b - a) * 128].rearrange("k (b m) -> k b m", m=128),
                                       ACT.Copy).then_inc(pt_done, 1)

                def load_t1(st):
                    i, par = st.i, st.par
                    wait(act, t2a_done, i - 1)
                    act.dma_start(t1[par][:], t1_view[i]).then_inc(t1_loaded[par], 16)

                def step(st, first, last):
                    load_t1(st)
                    copy_probs(st)
                    if not last:
                        exponentials(st.step(1))

                exponentials(Strip(0, 0))
                every_strip(act, step)

            @block.vector
            def _(dve):
                dve.wait_ge(const_in, 16 * N_CONST)

                def subtract_max(st):
                    i, par = st.i, st.par
                    for bank, (a, b) in enumerate(BANKS):
                        dve.wait_ge(s_ready, 3 * i + bank + 1)
                        s = psS[bank][:, 0:(b - a) * KEYS].rearrange("p (b k) -> p b k", k=KEYS)
                        dve.tensor_reduce(mx[par][:, a:b], s, AX.X, ALU.max).then_inc(mx_done, 1)
                        dve.wait_ge(mx_done, 3 * i + bank + 1)
                        dve.tensor_tensor(prob[par][:, a * KEYS:b * KEYS].rearrange("p (b k) -> p b k", k=KEYS), s,
                                          mx[par][:, a:b].unsqueeze(2).to_broadcast([128, b - a, KEYS]), ALU.subtract)\
                           .then_inc(sub_done, 1)

                def own_head(st):
                    i, par = st.i, st.par
                    for k, (a, b) in enumerate(GROUPS):
                        n = b - a
                        dve.wait_ge(pv_ready, 4 * i + k + 1)
                        dve.tensor_tensor(own[k % 2][:, 0:n], psO[k % 2][:, 0:n * 128].rearrange("p (b h m) -> p b h m", h=HEADS, m=QB),
                                          headmask[:].unsqueeze(1).unsqueeze(3).to_broadcast([2 * C, n, HEADS, QB]),
                                          ALU.mult).then_inc(own_done, 1)
                        dve.wait_ge(own_done, 4 * i + k + 1)
                        dve.tensor_reduce(sums[:, a:b, :], own[k % 2][:, 0:n].rearrange("p b h m -> p b m h"), AX.X, ALU.add)\
                           .then_inc(summed, 1)
                    dve.wait_ge(summed, 4 * i + 4)
                    dve.reciprocal(inv[:], sums[C:2 * C]).then_inc(inv_done, 1)
                    dve.wait_ge(inv_done, i + 1)
                    wait(dve, pr_ready, i - 1)
                    dve.tensor_tensor(o_ch[par][:].rearrange("c (y b x) -> c b y x", y=QROWS, x=QCOLS),
                                      sums[0:C].rearrange("c b (y x) -> c b y x", x=QCOLS),
                                      inv[:].rearrange("c b (y x) -> c b y x", x=QCOLS), ALU.mult).then_inc(o_done, 1)

                def residual(st):
                    i, par = st.i, st.par
                    dve.wait_ge(pr_ready, i + 1)
                    dve.wait_ge(t1_loaded[par], 16 * (st.turn + 1))
                    wait(dve, t2_done, i - 1)
                    dve.tensor_tensor(t2a[par][:], psM[0:TOK, SPIX:SPIX + 2 * C].rearrange("p (r c) -> p r c", c=C), t1[par][:],
                                      ALU.add).then_inc(t2a_done, 1)

                def step(st, first, last):
                    if not last:
                        subtract_max(st.step(1))
                    if not first:
                        residual(st.step(-1))
                    own_head(st)

                subtract_max(Strip(0, 0))
                every_strip(dve, step)
                residual(Strip(PAIRS - 1, 1))

        clear(nc, semaphores)


def index_phase(nc, io, key_dram, digit_dram, edge_dram, first_dram, ends_dram):
    with ExitStack() as ctx:
        sb = lambda name, shape, dt=F32: ctx.enter_context(nc.sbuf_tensor(name, shape, dt))
        sem = lambda name: ctx.enter_context(nc.semaphore(name))
        key = sb("i_key", [128, EF], I32)
        dst = sb("i_dst", [128, EF], I32)
        part_i = sb("i_part", [128, EF], I32)
        dstf = sb("i_dstf", [128, EF])
        out = sb("i_out", [128, NFC, 6, FC])
        first = sb("i_first", [128, 1], I32)
        ends = sb("i_ends", [128, 2])
        const_in = sem("const_in"); step = sem("step"); digits = sem("digits"); limits = sem("limits"); stored = sem("stored")
        chunks = lambda a: a[:].rearrange("p (k f) -> p k f", f=FC)

        with nc.Block() as block:
            @block.sync
            def _(sp):
                sp.dma_start(key[:].bitcast(F32), key_dram).then_inc(const_in, 16)
                sp.wait_ge(digits, 1)
                sp.dma_start(digit_dram.rearrange("k p d f -> p k d f"), out[:, :, 4:6, :]).then_inc(stored, 16)
                sp.dma_start(first_dram, first[:]).then_inc(stored, 16)
                sp.dma_start(ends_dram, ends[:]).then_inc(stored, 16)
                sp.wait_ge(limits, 1)
                sp.dma_start(edge_dram.rearrange("k p d f -> p k d f"), out[:, :, 0:4, :]).then_inc(stored, 16)
                sp.wait_ge(stored, 64)

            @block.vector
            def _(dve):
                done = Link(dve, step)
                dve.wait_ge(const_in, 16)
                done(dve.tensor_scalar(dst[:], key[:], SRC_BITS, NODES - 1, ALU.logical_shift_right, ALU.bitwise_and))
                done(dve.tensor_scalar(part_i[:], dst[:], 127, None, ALU.bitwise_and))
                dve.tensor_copy(dstf[:], dst[:])
                done(dve.tensor_copy(out[:, :, 4, :], chunks(part_i)))
                done(dve.tensor_scalar(part_i[:], dst[:], 7, None, ALU.logical_shift_right))
                dve.tensor_copy(first[:], dst[:, 0:1])
                dve.tensor_copy(ends[:, 0:1], dstf[:, 0:1])
                dve.tensor_copy(ends[:, 1:2], dstf[:, EF - 1:EF])
                dve.tensor_copy(out[:, :, 5, :], chunks(part_i)).then_inc(digits, 1)
                dve.tensor_scalar(out[:, :, 0, :].bitcast(I32), chunks(key), (1 << SRC_BITS) - 1, None, ALU.bitwise_and)
                same = out[:, :, 3, :]
                dve.memset(same[:, 0, 0:1], 0.0)
                dve.tensor_tensor(same[:, 1:NFC, 0], chunks(dstf)[:, 1:NFC, 0], chunks(dstf)[:, 0:NFC - 1, FC - 1], ALU.is_equal)
                done(dve.tensor_tensor(same[:, :, 1:FC], chunks(dstf)[:, :, 1:FC], chunks(dstf)[:, :, 0:FC - 1], ALU.is_equal))
                done(dve.tensor_scalar(out[:, :, 1, :], same, 2.0, -1.0, ALU.mult, ALU.add))
                dve.tensor_scalar(out[:, :, 2, :], same, -1.0, HIDE, ALU.add, ALU.mult)
                dve.tensor_scalar(out[:, :, 1, :], out[:, :, 1, :], FAR, None, ALU.mult).then_inc(limits, 1)


def table_phase(nc, io, t2_dram, z_dram, table_dram, adst_dram):
    with ExitStack() as ctx:
        sb = lambda name, shape, dt=F32: ctx.enter_context(nc.sbuf_tensor(name, shape, dt))
        sb2 = lambda name, shape: [sb(f"{name}{i}", shape) for i in range(2)]
        ps = lambda name, shape: ctx.enter_context(nc.psum_tensor(name, shape, F32))
        sem = lambda name: ctx.enter_context(nc.semaphore(name))

        ident = sb("t_ident", [128, 128])
        wg = sb("t_wg", [C, GH + 2 * GHEADS])
        att = sb("t_att", [C, 2, GH])
        wa = sb("t_wa", [C, 2, GH])
        t2 = sb2("t_t2", [128, JC, C])
        cen = sb2("t_cen", [128, JC, C])
        sq = sb2("t_sq", [128, JC, C])
        z = sb2("t_z", [128, JC, C])
        stat = sb2("t_stat", [128, 6, JC])
        z_ch = sb2("t_z_ch", [C, JC * 128])
        rows = sb2("t_rows", [128, JC, ROW])
        adst = sb2("t_adst", [128, JC, GHEADS])
        psZ = [ps(f"t_psZ{i}", [128, 512]) for i in range(4)]
        psR = [ps(f"t_psR{i}", [128, 512]) for i in range(2)]
        NCH = JT // JC

        passed = sem("passed")
        const_in = sem("const_in"); weights = sem("weights")
        loaded = [sem(f"loaded{i}") for i in range(2)]
        stored = [sem(f"stored{i}") for i in range(2)]
        step = sem("step"); cen_done = sem("cen_done"); sq_done = sem("sq_done"); var_done = sem("var_done")
        std_done = sem("std_done"); inv_done = sem("inv_done"); z_done = sem("z_done")
        zt_ready = sem("zt_ready"); zt_done = sem("zt_done"); row_ready = sem("row_ready"); row_done = sem("row_done")
        t2_view = t2_dram.rearrange("(p k j) c -> k p j c", p=128, j=JC)
        z_view = z_dram.rearrange("c (k x) -> k c x", k=NCH)
        table_view = table_dram.rearrange("(p k j) c -> k p j c", p=128, j=JC)
        adst_view = adst_dram.rearrange("(p k j) c -> k p j c", p=128, j=JC)
        PARTS = [(0, 4), (4, JC)]

        def every_chunk(eng, step_of):
            with eng.Fori(0, NCH // 2) as turn:
                for par in range(2):
                    step_of(turn, par)

        with nc.Block() as block:
            @block.sync
            def _(sp):
                sp.dma_start(ident[:], io["ident"]).then_inc(const_in, 16)
                sp.dma_start(wg[:, 0:GH], io["wgat"]).then_inc(const_in, 16)
                for k, name in enumerate(("att_src", "att_dst")):
                    sp.dma_start(att[:, k, :], io[name].rearrange("(a h) e -> a (h e)", a=1).to_broadcast([C, GH])).then_inc(const_in, 16)

                sp.dma_start(t2[0][:], t2_view[0]).then_inc(loaded[0], 16)
                sp.dma_start(t2[1][:], t2_view[1]).then_inc(loaded[1], 16)

                def out(turn, par):
                    k = turn * 2 + par
                    sp.wait_ge(zt_done, k * 2 + 2)
                    sp.dma_start(z_view[k], z_ch[par][:]).then_inc(stored[par], 16)
                    sp.wait_ge(row_done, k + 1)
                    sp.dma_start(table_view[k], rows[par][:]).then_inc(stored[par], 16)
                    sp.dma_start(adst_view[k], adst[par][:]).then_inc(stored[par], 16)

                with sp.Fori(0, NCH // 2 - 1) as turn:
                    for par in range(2):
                        sp.wait_ge(cen_done, turn * 2 + par + 1)
                        sp.dma_start(t2[par][:], t2_view[turn * 2 + par + 2]).then_inc(loaded[par], 16)
                        out(turn, par)
                for par in range(2):
                    out(NCH // 2 - 1, par)
                for par in range(2):
                    sp.wait_ge(stored[par], 48 * (NCH // 2))

            @block.vector
            def _(dve):
                dve.wait_ge(const_in, 64)
                for k in range(2):
                    m = dve.tensor_tensor(wa[:, k, :], wg[:, 0:GH], att[:, k, :], ALU.mult)
                m.then_inc(weights, 1)
                dve.wait_ge(weights, 1)
                for k in range(2):
                    m = dve.tensor_reduce(wg[:, GH + k * GHEADS:GH + (k + 1) * GHEADS],
                                          wa[:, k, :].rearrange("c (h e) -> c h e", e=EXPERTS), AX.X, ALU.add)
                m.then_inc(weights, 1)

                def layernorm(turn, par):
                    k = turn * 2 + par
                    st = lambda j: stat[par][:, j, :]
                    dve.wait_ge(loaded[par], (turn + 1) * 16)
                    dve.tensor_reduce(st(0), t2[par][:], AX.X, ALU.add).then_inc(step, 1)
                    dve.wait_ge(step, k * 3 + 1)
                    dve.tensor_scalar(st(1), st(0), -1.0 / C, None, ALU.mult).then_inc(step, 1)
                    dve.wait_ge(step, k * 3 + 2)
                    dve.tensor_tensor(cen[par][:], t2[par][:], st(1).unsqueeze(2).to_broadcast([128, JC, C]), ALU.add)\
                       .then_inc(cen_done, 1)
                    dve.wait_ge(sq_done, k + 1)
                    dve.tensor_reduce(st(2), sq[par][:], AX.X, ALU.add).then_inc(step, 1)
                    dve.wait_ge(step, k * 3 + 3)
                    dve.tensor_scalar(st(3), st(2), 1.0 / C, LN_EPS, ALU.mult, ALU.add).then_inc(var_done, 1)
                    dve.wait_ge(std_done, k + 1)
                    dve.reciprocal(st(5), st(4)).then_inc(inv_done, 1)

                every_chunk(dve, layernorm)

            @block.gpsimd
            def _(pool):
                def squares_and_scale(turn, par):
                    k = turn * 2 + par
                    pool.wait_ge(cen_done, k + 1)
                    pool.tensor_tensor(sq[par][:], cen[par][:], cen[par][:], ALU.mult).then_inc(sq_done, 1)
                    pool.wait_ge(inv_done, k + 1)
                    pool.tensor_tensor(z[par][:], cen[par][:], stat[par][:, 5, :].unsqueeze(2).to_broadcast([128, JC, C]), ALU.mult)\
                        .then_inc(z_done, 1)

                every_chunk(pool, squares_and_scale)

            @block.tensor
            def _(pe):
                pe.wait_ge(weights, 2)

                def rows_of(turn, par):
                    k = turn * 2 + par
                    pe.wait_ge(z_done, k + 1)
                    pe.sem_inc(passed, 1)
                    for h, (a, b) in enumerate(PARTS):
                        for j in range(a, b):
                            m = pe.transpose(psZ[par * 2 + h][0:C, (j - a) * 128:(j - a + 1) * 128], z[par][:, j, :], ident[:])
                        m.then_inc(zt_ready, 1)
                    pe.wait_ge(zt_done, k * 2 + 2)
                    pe.wait_ge(row_done, k)
                    for j in range(JC):
                        m = pe.matmul(psR[par][:, j * 24:(j + 1) * 24], z_ch[par][:, j * 128:(j + 1) * 128], wg[:],
                                      start=True, stop=True)
                    m.then_inc(row_ready, 1)

                every_chunk(pe, rows_of)

            @block.scalar
            def _(act):
                def copies(turn, par):
                    k = turn * 2 + par
                    act.wait_ge(var_done, k + 1)
                    act.activation(stat[par][:, 4, :], stat[par][:, 3, :], ACT.Sqrt).then_inc(std_done, 1)
                    act.wait_ge(stored[par], turn * 48)
                    for h, (a, b) in enumerate(PARTS):
                        act.wait_ge(zt_ready, k * 2 + h + 1)
                        act.activation(z_ch[par][:, a * 128:b * 128], psZ[par * 2 + h][0:C, 0:(b - a) * 128], ACT.Copy).then_inc(zt_done, 1)
                    act.wait_ge(row_ready, k + 1)
                    r = psR[par][:, 0:JC * 24].rearrange("p (j c) -> p j c", c=24)
                    act.activation(rows[par][:], r[:, :, 0:ROW], ACT.Copy)
                    act.activation(adst[par][:], r[:, :, ROW:24], ACT.Copy).then_inc(row_done, 1)

                every_chunk(act, copies)


def edge_phase(nc, io, z_dram, table_dram, adst_dram, digit_dram, edge_dram, node_dram, first_dram, b_dram, state_dram, y_dram):
    with ExitStack() as ctx:
        sb = lambda name, shape, dt=F32: ctx.enter_context(nc.sbuf_tensor(name, shape, dt))
        sb2 = lambda name, shape, dt=F32: [sb(f"{name}{i}", shape, dt) for i in range(2)]
        sem = lambda name: ctx.enter_context(nc.semaphore(name))
        sem2 = lambda name: [sem(f"{name}{i}") for i in range(2)]

        node_dst = sb("e_node_dst", [128, 128, GHEADS])
        first_ix = sb("e_first_ix", [128, 1], I32)
        b_first = sb("e_b_first", [128, GHEADS])
        zeros = sb("e_zeros", [128, FC * GHEADS])
        iota = sb("i_iota", [128, 128]); before = sb("i_before", [128, 128])
        digit = [sb(f"i_digit{i}", [128, 2, FC]) for i in range(2)]
        hot = [[sb(f"i_hot{i}{d}", [128, HOT, 128], BF16) for d in range(2)] for i in range(2)]
        zero = sb("i_zero", [128, 128], BF16)
        cnt = sb("i_cnt", [128, 128]); inc = sb("i_inc", [128, 128]); base = sb("i_base", [128, 1])
        none = sb("i_none", [128, 128]); pos = sb("i_pos", [128, 2, 128]); posi = sb("i_posi", [128, 2, 128], I32)
        edge = [sb(f"e_edge{i}", [128, 4, FC]) for i in range(AHEAD)]
        bsrc = sb2("e_bsrc", [128, FC, GHEADS])
        b = sb2("e_b", [128, FC, GHEADS])
        row = [sb(f"e_row{i}", [128, FC, ROW]) for i in range(AHEAD)]
        state = sb2("e_state", [128, FC, STATE])
        e0 = sb("e_e0", [128, FC, GHEADS]); e1 = sb("e_e1", [128, FC, GHEADS])
        drop = sb("e_drop", [128, 2, FC, GHEADS])
        weight = sb("e_weight", [128, 2, FC, GHEADS])
        part = sb("e_part", [128, FC, GH])

        w1 = sb("f_w1", [C, EXPERTS, 128]); b1 = sb("f_b1", [128, EXPERTS]); w2 = sb("f_w2", [128, EXPERTS, C])
        b2 = sb("f_b2", [128, EXPERTS * C])
        z = sb2("f_z", [C, ZT])
        hid = [sb(f"f_hid{e}", [128, ZT]) for e in range(EXPERTS)]
        y = sb2("f_y", [128, ZT // 128, EXPERTS * C])
        psH = [ctx.enter_context(nc.psum_tensor(f"f_psH{e}", [128, ZT], F32)) for e in range(EXPERTS)]
        psY = [ctx.enter_context(nc.psum_tensor(f"f_psY{i}", [128, ZT // 128, EXPERTS * C], F32)) for i in range(2)]

        psC, psB = psH[0][:, 0:128], psH[1][:, 0:1]
        passed = sem("passed")
        const_in = sem("const_in"); weights_in = sem("weights_in"); zeroed = sem("zeroed"); b_zeroed = sem("b_zeroed"); b_placed = sem("b_placed")
        b_gathered = sem("b_gathered")
        b_in = sem2("b_in"); state_out = sem2("state_out")
        edge_in = [sem(f"edge_in{i}") for i in range(AHEAD)]; rows_in = [sem(f"rows_in{i}") for i in range(AHEAD)]
        hist_in = sem("hist_in"); zeroed_hot = sem("zeroed_hot"); digit_in = sem2("digit_in")
        hot_ready = sem("hot_ready"); hot_used = sem("hot_used"); counted = sem("counted"); step = sem("step")
        totals = sem("totals"); based = sem("based"); placed = sem("placed"); placed_out = sem("placed_out")
        GROUPS = FC // HOT
        b_filled = sem("b_filled"); summed = sem("summed"); leaked = sem("leaked"); maxed = sem("maxed")
        diffed = sem("diffed"); limited = sem("limited"); exped = sem("exped"); weighted = sem("weighted")
        scanned = sem("scanned")
        z_in = sem2("z_in"); hid_ready = sem("hid_ready"); gelu_done = sem("gelu_done")
        y_ready = sem2("y_ready"); y_done = sem2("y_done"); y_out = sem2("y_out")

        TILES_Z = TOKENS // ZT
        PER = TILES_Z // NFC
        z_view = z_dram.rearrange("c (k x) -> k c x", x=ZT)
        y_view = y_dram.rearrange("(p k j) c -> k p j c", p=128, j=ZT // 128)
        b_view = b_dram.rearrange("(p k f) h -> k p f h", p=128, f=FC)
        state_view = state_dram.rearrange("(p k f) c -> k p f c", p=128, f=FC)

        with nc.Block() as block:
            @block.sync
            def _(sp):
                for s in range(AHEAD):
                    sp.dma_start(edge[s][:], edge_dram[s]).then_inc(edge_in[s], 16)
                for par in range(2):
                    sp.dma_start(digit[par][:], digit_dram[par]).then_inc(digit_in[par], 16)
                sp.dma_start(iota[:], io["iota"]).then_inc(hist_in, 16)
                sp.dma_start(before[:], io["before"]).then_inc(hist_in, 16)
                sp.dma_start(node_dst[:], adst_dram[0:NODES].rearrange("(p t) h -> p t h", p=128)).then_inc(const_in, 16)
                sp.dma_start(first_ix[:], first_dram).then_inc(const_in, 16)
                sp.dma_start(b2[:], io["ffn_b2"].to_broadcast([128, EXPERTS * C])).then_inc(const_in, 16)
                sp.wait_ge(zeroed, 1)
                flat = b_dram.rearrange("(p k f) h -> k p (f h)", p=128, f=FC)
                for c in range(NFC):
                    sp.dma_start(flat[c], zeros[:]).then_inc(b_zeroed, 16)
                with sp.Fori(0, NFC // 2 - 1) as turn:
                    for par in range(2):
                        sp.wait_ge(hot_ready, (turn * 2 + par + 1) * GROUPS)
                        sp.dma_start(digit[par][:], digit_dram[turn * 2 + par + 2]).then_inc(digit_in[par], 16)
                sp.wait_ge(placed, 1)
                sp.dma_start(node_dram.rearrange("k p t -> p k t"), posi[:]).then_inc(placed_out, 16)
                sp.wait_ge(placed_out, 16)
                sp.wait_ge(b_placed, 16 * 129)
                for par in range(2):
                    sp.dma_start(bsrc[par][:], b_view[par]).then_inc(b_in[par], 16)

                def out(turn, par):
                    sp.wait_ge(scanned, turn * 2 + par + 2)
                    sp.dma_start(state_view[turn * 2 + par], state[par][:]).then_inc(state_out[par], 16)

                def chunk(turn, s, load_edge, load_b):
                    out(turn * (AHEAD // 2) + s // 2, s % 2)
                    if load_edge:
                        sp.dma_start(edge[s][:], edge_dram[(turn + 1) * AHEAD + s]).then_inc(edge_in[s], 16)
                    if load_b:
                        sp.dma_start(bsrc[s % 2][:], b_view[turn * AHEAD + s + 2]).then_inc(b_in[s % 2], 16)

                with sp.Fori(0, NFC // AHEAD - 1) as turn:
                    for s in range(AHEAD):
                        chunk(turn, s, True, True)
                for s in range(AHEAD):
                    chunk(NFC // AHEAD - 1, s, False, s < AHEAD - 2)
                for par in range(2):
                    sp.wait_ge(state_out[par], 16 * (NFC // 2))

            @block.gpsimd
            def _(pool):
                pool.memset(zeros[:], 0.0).then_inc(zeroed, 1)

                def gather(turn, s):
                    pool.wait_ge(edge_in[s], (turn + 1) * 16)
                    pool.sem_inc(passed, 1)
                    for f in range(FC):
                        pool.indirect_dma_start(out=row[s][:, f, :], out_offset=None, in_=table_dram,
                                                in_offset=bass.IndirectOffsetOnAxis(ap=edge[s][:, 0, f:f + 1].bitcast(I32), axis=0)
                                                ).then_inc(rows_in[s], 16)

                for s in range(AHEAD):
                    gather(0, s)
                pool.wait_ge(const_in, 48)
                pool.indirect_dma_start(out=b_first[:], out_offset=None, in_=adst_dram,
                                        in_offset=bass.IndirectOffsetOnAxis(ap=first_ix[:, 0:1], axis=0)).then_inc(b_gathered, 16)
                pool.wait_ge(b_zeroed, 16 * NFC)
                pool.wait_ge(placed, 1)
                for t in range(128):
                    pool.indirect_dma_start(out=b_dram, out_offset=bass.IndirectOffsetOnAxis(ap=posi[:, 1, t:t + 1], axis=0),
                                            in_=node_dst[:, t, :], in_offset=None,
                                            bounds_check=EDGES - 1, oob_is_err=False).then_inc(b_placed, 16)
                pool.wait_ge(b_placed, 16 * 128)
                pool.wait_ge(b_gathered, 16)
                pool.dma_start(b_dram.rearrange("(p x) h -> p x h", p=128)[:, 0, :], b_first[:]).then_inc(b_placed, 16)
                with pool.Fori(1, NFC // AHEAD) as turn:
                    for s in range(AHEAD):
                        gather(turn, s)

            @block.vector
            def _(dve):
                dve.memset(state[1][:, FC - 1, 0:GHEADS], -FAR)
                dve.memset(state[1][:, FC - 1, GHEADS:STATE], 0.0)
                dve.memset(b[1][:, FC - 1, :], 0.0).then_inc(scanned, 1)
                dve.wait_ge(scanned, 1)

                dve.memset(zero[:], 0.0).then_inc(zeroed_hot, 1)
                dve.wait_ge(hist_in, 32)
                with dve.Fori(0, NFC // 2) as turn:
                    for par in range(2):
                        dve.wait_ge(digit_in[par], (turn + 1) * 16)
                        for g in range(GROUPS):
                            dve.wait_ge(hot_used, turn * (2 * GROUPS) + par * GROUPS + g)
                            for d in range(2):
                                m = dve.tensor_tensor(hot[g % 2][d][:], iota[:].unsqueeze(1).to_broadcast([128, HOT, 128]),
                                                      digit[par][:, d, g * HOT:(g + 1) * HOT].unsqueeze(2).to_broadcast([128, HOT, 128]),
                                                      ALU.is_equal)
                            m.then_inc(hot_ready, 1)
                done = Link(dve, step)
                dve.wait_ge(counted, 1)
                dve.memset(none[:], 1.0)
                done(dve.tensor_copy(cnt[:], psC))
                done(dve.tensor_tensor_scan(inc[:], none[:], cnt[:], 0.0, ALU.mult, ALU.add))
                dve.tensor_copy(base[:], inc[:, 127:128]).then_inc(totals, 1)
                dve.wait_ge(based, 1)
                done(dve.tensor_copy(base[:], psB))
                dve.tensor_scalar(none[:], cnt[:], 0.0, MISS, ALU.is_equal, ALU.mult)
                done(dve.tensor_scalar(inc[:], inc[:], base[:], None, ALU.add))
                dve.tensor_tensor(pos[:, 1, :], inc[:], cnt[:], ALU.subtract)
                done(dve.tensor_scalar(pos[:, 0, :], inc[:], -1.0, None, ALU.add))
                done(dve.tensor_tensor(pos[:], pos[:], none[:].unsqueeze(1).to_broadcast([128, 2, 128]), ALU.add))
                dve.tensor_copy(posi[:], pos[:]).then_inc(placed, 1)
                dve.wait_ge(const_in, 48)

                def outputs(t_slot, par):
                    dve.wait_ge(y_ready[par], t_slot + 1)
                    dve.wait_ge(y_out[par], t_slot * 16)
                    dve.tensor_tensor(y[par][:], psY[par][:], b2[:].unsqueeze(1).to_broadcast([128, ZT // 128, EXPERTS * C]),
                                      ALU.add).then_inc(y_done[par], 1)

                def scans(turn, s):
                    c, par = turn * AHEAD + s, s % 2
                    used = turn * (AHEAD // 2) + s // 2
                    same, lim, lim2 = edge[s][:, 3, :], edge[s][:, 1, :], edge[s][:, 2, :]
                    st, last = state[par], state[1 - par][:, FC - 1, :]
                    dve.wait_ge(edge_in[s], (turn + 1) * 16)
                    dve.wait_ge(b_in[par], (used + 1) * 16)
                    dve.wait_ge(scanned, c + 1)
                    for h in range(GHEADS):
                        m = dve.tensor_tensor_scan(b[par][:, :, h], same, bsrc[par][:, :, h], b[1 - par][:, FC - 1, h:h + 1], ALU.mult, ALU.add)
                    m.then_inc(b_filled, 1)
                    dve.wait_ge(b_filled, c + 1)
                    dve.wait_ge(rows_in[s], (turn + 1) * (16 * FC))
                    dve.tensor_tensor(e0[:], row[s][:, :, GH:ROW], b[par][:], ALU.add).then_inc(summed, 1)
                    dve.wait_ge(summed, c + 1)
                    dve.scalar_tensor_tensor(e1[:], e0[:], 0.2, e0[:], ALU.mult, ALU.max).then_inc(leaked, 1)
                    dve.wait_ge(leaked, c + 1)
                    dve.wait_ge(state_out[par], used * 16)
                    for h in range(GHEADS):
                        m = dve.tensor_tensor_scan(st[:, :, h], lim, e1[:, :, h], last[:, h:h + 1], ALU.min, ALU.max)
                    m.then_inc(maxed, 1)
                    dve.wait_ge(maxed, c + 1)
                    dve.tensor_tensor(drop[:, 1], e1[:], st[:, :, 0:GHEADS], ALU.subtract)
                    dve.tensor_tensor(drop[:, 0, 1:FC, :], st[:, 0:FC - 1, 0:GHEADS], st[:, 1:FC, 0:GHEADS], ALU.subtract)
                    dve.tensor_tensor(drop[:, 0, 0, :], last[:, 0:GHEADS], st[:, 0, 0:GHEADS], ALU.subtract).then_inc(diffed, 1)
                    dve.wait_ge(diffed, c + 1)
                    dve.scalar_tensor_tensor(drop[:, 0], drop[:, 0], 0.0, lim2.unsqueeze(2).to_broadcast([128, FC, GHEADS]),
                                             ALU.min, ALU.add).then_inc(limited, 1)
                    dve.wait_ge(exped, c + 1)
                    for h in range(GHEADS):
                        dve.tensor_tensor_scan(st[:, :, GHEADS + h], weight[:, 0, :, h], weight[:, 1, :, h],
                                               last[:, GHEADS + h:GHEADS + h + 1], ALU.mult, ALU.add)
                    dve.tensor_tensor(part[:].rearrange("p f (h e) -> p f h e", e=EXPERTS),
                                      row[s][:, :, 0:GH].rearrange("p f (h e) -> p f h e", e=EXPERTS),
                                      weight[:, 1].unsqueeze(3).to_broadcast([128, FC, GHEADS, EXPERTS]), ALU.mult).then_inc(weighted, 1)
                    dve.wait_ge(weighted, c + 1)
                    for k in range(GH):
                        n = 2 * GHEADS + k
                        m = dve.tensor_tensor_scan(st[:, :, n], weight[:, 0, :, k // EXPERTS], part[:, :, k], last[:, n:n + 1],
                                                   ALU.mult, ALU.add)
                    m.then_inc(scanned, 1)

                with dve.Fori(0, NFC // AHEAD) as turn:
                    for s in range(AHEAD):
                        for q in range(s * PER, (s + 1) * PER):
                            outputs(turn * (AHEAD // 2 * PER) + q // 2, q % 2)
                        scans(turn, s)
                outputs(NFC // 2 * PER, 0)

            @block.scalar
            def _(act):
                for a, name in ((w1, "ffn_w1"), (b1, "ffn_b1"), (w2, "ffn_w2")):
                    act.dma_start(a[:], io[name]).then_inc(weights_in, 16)
                for par in range(2):
                    act.dma_start(z[par][:], z_view[par]).then_inc(z_in[par], 16)
                act.wait_ge(weights_in, 48)

                def gelus(turn, q, load):
                    t, par = turn * (2 * PER) + q, q % 2
                    for e in range(EXPERTS):
                        act.wait_ge(hid_ready, t * EXPERTS + e + 1)
                        act.activation(hid[e][:], psH[e][:], ACT.Gelu, bias=b1[:, e:e + 1]).then_inc(gelu_done, 1)
                    if load:
                        act.dma_start(z[par][:], z_view[t + 2]).then_inc(z_in[par], 16)
                    act.wait_ge(y_done[par], turn * PER + q // 2 + 1)
                    act.dma_start(y_view[t], y[par][:]).then_inc(y_out[par], 16)

                def exps(turn, par):
                    act.wait_ge(limited, turn * 2 + par + 1)
                    act.activation(weight[:], drop[:], ACT.Exp).then_inc(exped, 1)

                def both(turn, last):
                    for par in range(2):
                        for q in range(par * PER, (par + 1) * PER):
                            gelus(turn, q, not last or q < 2 * PER - 1)
                        exps(turn, par)

                with act.Fori(0, NFC // 2 - 1) as turn:
                    both(turn, False)
                both(NFC // 2 - 1, True)
                gelus(NFC // 2, 0, False)
                act.wait_ge(y_out[0], 16 * (TILES_Z // 2 + 1))
                act.wait_ge(y_out[1], 16 * (TILES_Z // 2))

            @block.tensor
            def _(pe):
                pe.wait_ge(zeroed_hot, 1)
                pe.matmul(psC, zero[:], zero[:], start=True, stop=False).then_inc(hot_used, 1)
                with pe.Fori(0, NFC // 2) as turn:
                    for par in range(2):
                        for g in range(GROUPS):
                            pe.wait_ge(hot_ready, turn * (2 * GROUPS) + par * GROUPS + g + 1)
                            for c in range(HOT):
                                m = pe.matmul(psC, hot[g % 2][1][:, c, :], hot[g % 2][0][:, c, :], start=False, stop=False)
                            m.then_inc(hot_used, 1)
                pe.matmul(psC, zero[:], zero[:], start=False, stop=True).then_inc(counted, 1)
                pe.wait_ge(totals, 1)
                pe.matmul(psB, before[:], base[:], start=True, stop=True).then_inc(based, 1)
                pe.wait_ge(weights_in, 48)
                pe.wait_ge(placed, 1)

                def tile(turn, q):
                    t, par, k = turn * (2 * PER) + q, q % 2, turn * PER + q // 2
                    pe.wait_ge(z_in[par], (k + 1) * 16)
                    for e in range(EXPERTS):
                        pe.matmul(psH[e][:], w1[:, e, :], z[par][:], start=True, stop=True).then_inc(hid_ready, 1)
                    pe.wait_ge(y_done[par], k)
                    for e in range(EXPERTS):
                        pe.wait_ge(gelu_done, t * EXPERTS + e + 1)
                        for j in range(ZT // 128):
                            m = pe.matmul(psY[par][:, j, e * C:(e + 1) * C], hid[e][:, j * 128:(j + 1) * 128], w2[:, e, :],
                                          start=True, stop=True)
                    m.then_inc(y_ready[par], 1)

                with pe.Fori(0, NFC // 2) as turn:
                    for q in range(2 * PER):
                        tile(turn, q)
                tile(NFC // 2, 0)


def join_phase(nc, io, state_dram, node_dram, first_dram, ends_dram, sums_dram):
    with ExitStack() as ctx:
        sb = lambda name, shape, dt=F32: ctx.enter_context(nc.sbuf_tensor("j_" + name, shape, dt))
        sem = lambda name: ctx.enter_context(nc.semaphore(name))
        ident = sb("ident", [128, 128]); last_pos = sb("last_pos", [128, 1])
        ends = sb("ends", [128, 2]); first_ix = sb("first_ix", [128, 1], I32); end_ix = sb("end_ix", [128, 128], I32)
        tail = sb("tail", [128, STATE])
        wide = sb("wide", [128, 5, GH])
        wt = sb("wt", [GH, 5, 128])
        cont = sb("cont", [GH, 128])
        link = sb("link", [GH, 128])
        lims = sb("lims", [GH, 2, 128]); lim2 = sb("lim2", [GH, 128])
        run = sb("run", [GH, 3, 129])
        drop = sb("drop", [GH, 2, 128]); weight = sb("weight", [GH, 2, 128]); part = sb("part", [GH, 2, 128])
        carry_t = sb("carry_t", [GH, 3, 128]); carry = sb("carry", [128, 3, GH])
        pos = sb("pos", [128, 1], I32); posf = sb("posf", [128, 1]); missing = sb("missing", [128, 1]); fix_ix = sb("fix_ix", [128, 1], I32)
        fix = sb("fix", [128, STATE]); top = sb("top", [128, GHEADS]); fdrop = sb("fdrop", [128, 2, GHEADS]); fw = sb("fw", [128, 2, GHEADS])
        old = sb("old", [128, GHEADS + GH]); new = sb("new", [128, GHEADS + GH]); fixed = sb("fixed", [128, STATE])
        sums = sb("sums", [128, 128, STATE])
        rest = (TOKENS - NODES) // 128
        psT = ctx.enter_context(nc.psum_tensor("j_psT", [GH, 5, 128], F32))
        psC = ctx.enter_context(nc.psum_tensor("j_psC", [128, 3, GH], F32))
        const_in = sem("const_in"); ix_in = sem("ix_in"); widened = sem("widened"); turned = sem("turned"); step = sem("step")
        limited = sem("limited"); exped = sem("exped"); carried = sem("carried"); turned_back = sem("turned_back")
        pos_in = sem("pos_in"); fix_at = sem("fix_at"); blank = sem("blank"); fix_in = sem("fix_in"); fix_limited = sem("fix_limited")
        fix_exped = sem("fix_exped"); fix_ready = sem("fix_ready"); fix_out = sem("fix_out"); sums_in = sem("sums_in"); sums_out = sem("sums_out")
        heads = lambda a: a.rearrange("p (h e) -> p h e", e=EXPERTS)
        spread = lambda a: a.unsqueeze(2).to_broadcast([128, GHEADS, EXPERTS])

        with nc.Block() as block:
            @block.sync
            def _(sp):
                sp.dma_start(first_ix[:], first_dram).then_inc(ix_in, 16)
                sp.dma_start(end_ix[:], node_dram[0]).then_inc(ix_in, 16)
                sp.dma_start(tail[:], state_dram.rearrange("(p x) c -> p x c", p=128)[:, EF - 1, :]).then_inc(const_in, 16)
                for a, b in ((ends, ends_dram), (ident, io["ident"]), (last_pos, io["last_pos"])):
                    sp.dma_start(a[:], b).then_inc(const_in, 16)
                sp.wait_ge(blank, 2)
                sp.dma_start(sums_dram[NODES:TOKENS].rearrange("(p t) c -> p t c", p=128), sums[:, 0:rest, :]).then_inc(sums_out, 16)
                sp.wait_ge(sums_in, 16 * 128)
                sp.dma_start(sums_dram[0:NODES].rearrange("(p t) c -> p t c", p=128), sums[:]).then_inc(sums_out, 16)
                sp.wait_ge(sums_out, 32)

            @block.gpsimd
            def _(pool):
                pool.wait_ge(ix_in, 32)
                pool.indirect_dma_start(out=pos[:], out_offset=None, in_=node_dram[0].rearrange("p (t o) -> (p t) o", o=1),
                                        in_offset=bass.IndirectOffsetOnAxis(ap=first_ix[:, 0:1], axis=0)).then_inc(pos_in, 16)
                pool.wait_ge(fix_at, 1)
                pool.indirect_dma_start(out=fix[:], out_offset=None, in_=state_dram,
                                        in_offset=bass.IndirectOffsetOnAxis(ap=fix_ix[:, 0:1], axis=0),
                                        bounds_check=EDGES - 1, oob_is_err=False).then_inc(fix_in, 16)
                pool.wait_ge(fix_ready, 1)
                pool.indirect_dma_start(out=state_dram, out_offset=bass.IndirectOffsetOnAxis(ap=fix_ix[:, 0:1], axis=0),
                                        in_=fixed[:], in_offset=None, bounds_check=EDGES - 1, oob_is_err=False).then_inc(fix_out, 16)
                pool.wait_ge(fix_out, 16)
                pool.wait_ge(sums_out, 16)
                for t in range(128):
                    pool.indirect_dma_start(out=sums[:, t, :], out_offset=None, in_=state_dram,
                                            in_offset=bass.IndirectOffsetOnAxis(ap=end_ix[:, t:t + 1], axis=0),
                                            bounds_check=EDGES - 1, oob_is_err=False).then_inc(sums_in, 16)

            @block.vector
            def _(dve):
                done = Link(dve, step)
                dve.memset(sums[:, :, 0:GHEADS], -FAR).then_inc(blank, 1)
                dve.memset(sums[:, :, GHEADS:STATE], 0.0).then_inc(blank, 1)
                dve.memset(fix[:], 0.0)
                dve.memset(cont[:], 0.0)
                dve.memset(run[:, 0, 0:1], -FAR)
                done(dve.memset(run[:, 1:3, 0:1], 0.0))
                dve.wait_ge(const_in, 64)
                dve.tensor_copy(heads(wide[:, 0, :]), spread(tail[:, 0:GHEADS]))
                dve.tensor_copy(heads(wide[:, 1, :]), spread(tail[:, GHEADS:2 * GHEADS]))
                dve.tensor_copy(wide[:, 2, :], tail[:, 2 * GHEADS:])
                dve.tensor_copy(wide[:, 3:5, :], ends[:].unsqueeze(2).to_broadcast([128, 2, GH])).then_inc(widened, 1)
                dve.wait_ge(pos_in, 16)
                done(dve.tensor_copy(posf[:], pos[:]))
                dve.tensor_scalar(missing[:], posf[:], last_pos[:], MISS, ALU.is_gt, ALU.mult).then_inc(step, 1)
                done.n += 1
                dve.wait_ge(step, done.n)
                done(dve.tensor_tensor(posf[:], posf[:], missing[:], ALU.add))
                dve.tensor_copy(fix_ix[:], posf[:]).then_inc(fix_at, 1)
                dve.wait_ge(turned, 1)
                done(dve.tensor_copy(wt[:], psT[:]))
                dve.tensor_tensor(cont[:, 1:128], wt[:, 3, 1:128], wt[:, 4, 0:127], ALU.is_equal)
                done(dve.tensor_tensor(link[:], wt[:, 3, :], wt[:, 4, :], ALU.is_equal))
                done(dve.tensor_tensor(link[:], link[:], cont[:], ALU.mult))
                dve.tensor_scalar(lims[:, 0, :], link[:], 2.0, -1.0, ALU.mult, ALU.add)
                dve.tensor_scalar(lims[:, 1, :], cont[:], 2.0, -1.0, ALU.mult, ALU.add)
                done(dve.tensor_scalar(lim2[:], link[:], -1.0, HIDE, ALU.add, ALU.mult))
                done(dve.tensor_scalar(lims[:], lims[:], FAR, None, ALU.mult))
                done(dve.tensor_tensor_scan(run[:, 0, 1:129], lims[:, 0, :], wt[:, 0, :], -FAR, ALU.min, ALU.max))
                dve.tensor_tensor(drop[:, 0, :], run[:, 0, 0:128], run[:, 0, 1:129], ALU.subtract)
                done(dve.tensor_tensor(drop[:, 1, :], wt[:, 0, :], run[:, 0, 1:129], ALU.subtract))
                dve.scalar_tensor_tensor(drop[:, 0, :], drop[:, 0, :], 0.0, lim2[:], ALU.min, ALU.add).then_inc(limited, 1)
                dve.wait_ge(exped, 1)
                done(dve.tensor_tensor(part[:], wt[:, 1:3, :], weight[:, 1, :].unsqueeze(1).to_broadcast([GH, 2, 128]), ALU.mult))
                for k in range(2):
                    m = dve.tensor_tensor_scan(run[:, 1 + k, 1:129], weight[:, 0, :], part[:, k, :], 0.0, ALU.mult, ALU.add)
                done(m)
                dve.tensor_tensor(carry_t[:, 0, :], run[:, 0, 0:128], lims[:, 1, :], ALU.min)
                dve.tensor_tensor(carry_t[:, 1:3, :], run[:, 1:3, 0:128], cont[:].unsqueeze(1).to_broadcast([GH, 2, 128]),
                                  ALU.mult).then_inc(carried, 1)
                dve.wait_ge(turned_back, 1)
                done(dve.tensor_copy(carry[:], psC[:]))
                dve.wait_ge(fix_in, 16)
                head_of = lambda k: heads(carry[:, k, :])[:, :, 0]
                done(dve.tensor_tensor(fixed[:, 0:GHEADS], fix[:, 0:GHEADS], head_of(0), ALU.max))
                dve.tensor_tensor(fdrop[:, 0, :], fix[:, 0:GHEADS], fixed[:, 0:GHEADS], ALU.subtract)
                dve.tensor_tensor(fdrop[:, 1, :], head_of(0), fixed[:, 0:GHEADS], ALU.subtract).then_inc(fix_limited, 1)
                dve.wait_ge(fix_exped, 1)
                dve.tensor_tensor(old[:, 0:GHEADS], fix[:, GHEADS:2 * GHEADS], fw[:, 0, :], ALU.mult)
                dve.tensor_tensor(heads(old[:, GHEADS:]), heads(fix[:, 2 * GHEADS:]), spread(fw[:, 0, :]), ALU.mult)
                dve.tensor_tensor(new[:, 0:GHEADS], head_of(1), fw[:, 1, :], ALU.mult)
                done(dve.tensor_tensor(heads(new[:, GHEADS:]), heads(carry[:, 2, :]), spread(fw[:, 1, :]), ALU.mult))
                dve.tensor_tensor(fixed[:, GHEADS:], old[:], new[:], ALU.add).then_inc(fix_ready, 1)

            @block.tensor
            def _(pe):
                pe.wait_ge(const_in, 64)
                pe.wait_ge(widened, 1)
                for k in range(5):
                    m = pe.transpose(psT[:, k, :], wide[:, k, :], ident[:])
                m.then_inc(turned, 1)
                pe.wait_ge(carried, 1)
                for k in range(3):
                    m = pe.transpose(psC[:, k, :], carry_t[:, k, :], ident[0:GH, 0:GH])
                m.then_inc(turned_back, 1)

            @block.scalar
            def _(act):
                act.wait_ge(limited, 1)
                act.activation(weight[:], drop[:], ACT.Exp).then_inc(exped, 1)
                act.wait_ge(fix_limited, 1)
                act.activation(fw[:], fdrop[:], ACT.Exp).then_inc(fix_exped, 1)


def output_phase(nc, io, table_dram, adst_dram, sums_dram, y_dram, t2_dram, out_dram):
    with ExitStack() as ctx:
        sb = lambda name, shape, dt=F32: ctx.enter_context(nc.sbuf_tensor("g_" + name, shape, dt))
        sem = lambda name: ctx.enter_context(nc.semaphore(name))
        SLOTS, NCH = 4, JT // JC
        row = sb("row", [128, JT, ROW]); adst = sb("adst", [128, JT, GHEADS]); sums = sb("sums", [128, JT, STATE])
        consts = sb("consts", [128, 3, GH])
        score = sb("score", [128, JT, GHEADS]); top = sb("top", [128, JT, GHEADS])
        drop = sb("drop", [128, 2, JT, GHEADS]); weight = sb("weight", [128, 2, JT, GHEADS])
        den = sb("den", [128, JT, GHEADS]); own = sb("own", [128, JT, GH])
        stat = sb("stat", [128, 4, JT])
        best = sb("best", [128, JT, EXPERTS]); beaten = sb("beaten", [128, JT, EXPERTS]); won = sb("won", [128, JT])
        high = sb("high", [128, JT]); gate = sb("gate", [128, JT, EXPERTS]); rel = sb("rel", [128, JT, EXPERTS])
        y = [sb(f"y{i}", [128, JC, EXPERTS, C]) for i in range(SLOTS)]
        t2 = [sb(f"t2_{i}", [128, JC, C]) for i in range(SLOTS)]
        scaled = [sb(f"scaled{i}", [128, JC, EXPERTS, C]) for i in range(2)]
        mix = [sb(f"mix{i}", [128, JC, C]) for i in range(2)]
        res = [sb(f"res{i}", [128, JC, C]) for i in range(SLOTS)]
        rows_in = sem("rows_in"); step = sem("step"); dropped = sem("dropped"); weighed = sem("weighed")
        varied = sem("varied"); rooted = sem("rooted"); related = sem("related"); exped = sem("exped")
        y_in = [sem(f"y_in{i}") for i in range(SLOTS)]; out_done = [sem(f"out_done{i}") for i in range(SLOTS)]
        scale_done = [sem(f"scale_done{i}") for i in range(2)]; mixed = sem("mixed")
        res_ready = [sem(f"res_ready{i}") for i in range(2)]; gated = sem("gated"); passed = sem("passed")
        y_view = y_dram.rearrange("(p k j) c -> k p j c", p=128, j=JC)
        t2_view = t2_dram.rearrange("(p k j) c -> k p j c", p=128, j=JC)
        out_view = out_dram.rearrange("n h w c -> (n h w) c").rearrange("(p k j) c -> k p j c", p=128, j=JC)
        by_token = lambda a: a.rearrange("(p j) c -> p j c", p=128)
        heads = lambda a: a.rearrange("p j (h e) -> p j h e", e=EXPERTS)
        spread = lambda a: a.unsqueeze(3).to_broadcast([128, JT, GHEADS, EXPERTS])
        along = lambda a, n: a.unsqueeze(2).to_broadcast([128, JT, n])
        const = lambda k: consts[:, k, :].unsqueeze(1).to_broadcast([128, JT, GH])

        def scale(eng, turn, s):
            k = turn * SLOTS + s
            return eng.tensor_tensor(scaled[s % 2][:].rearrange("p j e c -> p (j e) c"), y[s][:].rearrange("p j e c -> p (j e) c"),
                                     gate[:].rearrange("p j e -> p (j e)")[:, bass.ds(k * (JC * EXPERTS), JC * EXPERTS)]
                                     .unsqueeze(2).to_broadcast([128, JC * EXPERTS, C]), ALU.mult).then_inc(scale_done[s % 2], 1)

        with nc.Block() as block:
            @block.sync
            def _(sp):
                sp.dma_start(row[:], by_token(table_dram)).then_inc(rows_in, 16)
                sp.dma_start(adst[:], by_token(adst_dram)).then_inc(rows_in, 16)
                sp.dma_start(sums[:], by_token(sums_dram)).then_inc(rows_in, 16)
                for k, name in enumerate(("b_gat", "ln_gamma", "ln_beta")):
                    sp.dma_start(consts[:, k, :], io[name].rearrange("(a h) -> a h", a=1).to_broadcast([128, GH])).then_inc(rows_in, 16)

                def load(turn, s):
                    sp.dma_start(y[s][:].rearrange("p j e c -> p j (e c)"), y_view[turn * SLOTS + s]).then_inc(y_in[s], 16)
                    sp.dma_start(t2[s][:], t2_view[turn * SLOTS + s]).then_inc(y_in[s], 16)

                def out(turn, s):
                    sp.wait_ge(res_ready[s % 2], turn * (SLOTS // 2) + s // 2 + 1)
                    sp.dma_start(out_view[turn * SLOTS + s], res[s][:]).then_inc(out_done[s], 16)

                for s in range(SLOTS):
                    load(0, s)
                with sp.Fori(0, NCH // SLOTS - 1) as turn:
                    for s in range(SLOTS):
                        out(turn, s)
                        load(turn + 1, s)
                for s in range(SLOTS):
                    out(NCH // SLOTS - 1, s)
                for s in range(SLOTS):
                    sp.wait_ge(out_done[s], 16 * (NCH // SLOTS))

            @block.vector
            def _(dve):
                done = Link(dve, step)
                dve.wait_ge(rows_in, 96)
                done(dve.tensor_tensor(score[:], row[:, :, GH:ROW], adst[:], ALU.add))
                done(dve.scalar_tensor_tensor(top[:], score[:], 0.2, score[:], ALU.mult, ALU.max))
                done(dve.tensor_tensor(score[:], top[:], sums[:, :, 0:GHEADS], ALU.max))
                dve.tensor_tensor(drop[:, 0], sums[:, :, 0:GHEADS], score[:], ALU.subtract)
                dve.tensor_tensor(drop[:, 1], top[:], score[:], ALU.subtract).then_inc(dropped, 1)
                dve.wait_ge(weighed, 1)
                dve.tensor_tensor(den[:], sums[:, :, GHEADS:2 * GHEADS], weight[:, 0], ALU.mult)
                agg = sums[:, :, 2 * GHEADS:]
                dve.tensor_tensor(heads(agg), heads(agg), spread(weight[:, 0]), ALU.mult)
                done(dve.tensor_tensor(heads(own[:]), heads(row[:, :, 0:GH]), spread(weight[:, 1]), ALU.mult))
                done(dve.scalar_tensor_tensor(den[:], den[:], 1e-16, weight[:, 1], ALU.add, ALU.add))
                dve.reciprocal(den[:], den[:])
                done(dve.tensor_tensor(own[:], own[:], agg, ALU.add))
                done(dve.tensor_tensor(heads(own[:]), heads(own[:]), spread(den[:]), ALU.mult))
                done(dve.tensor_tensor(own[:], own[:], const(0), ALU.add))
                done(dve.tensor_reduce(stat[:, 0, :], own[:], AX.X, ALU.add))
                done(dve.tensor_scalar(stat[:, 0, :], stat[:, 0, :], -1.0 / GH, None, ALU.mult))
                done(dve.tensor_tensor(own[:], own[:], along(stat[:, 0, :], GH), ALU.add))
                done(dve.tensor_tensor(agg, own[:], own[:], ALU.mult))
                done(dve.tensor_reduce(stat[:, 1, :], agg, AX.X, ALU.add))
                dve.tensor_scalar(stat[:, 1, :], stat[:, 1, :], 1.0 / GH, LN_EPS, ALU.mult, ALU.add).then_inc(varied, 1)
                dve.wait_ge(rooted, 1)
                done(dve.reciprocal(stat[:, 3, :], stat[:, 2, :]))
                done(dve.tensor_tensor(own[:], own[:], along(stat[:, 3, :], GH), ALU.mult))
                done(dve.tensor_tensor(own[:], own[:], const(1), ALU.mult))
                done(dve.tensor_tensor(own[:], own[:], const(2), ALU.add))
                done(dve.tensor_reduce(best[:], own[:].rearrange("p j (h e) -> p j e h", e=EXPERTS), AX.X, ALU.add))
                dve.memset(beaten[:], 0.0)
                done(dve.tensor_scalar(best[:], best[:], 1.0 / GHEADS, None, ALU.mult))
                done(dve.tensor_reduce(high[:], best[:], AX.X, ALU.max))
                for a in range(EXPERTS):
                    for b in range(a + 1, EXPERTS):
                        done(dve.tensor_tensor(won[:], best[:, :, a], best[:, :, b], ALU.is_ge))
                        dve.tensor_tensor(beaten[:, :, b], beaten[:, :, b], won[:], ALU.add)
                        done(dve.scalar_tensor_tensor(beaten[:, :, a], beaten[:, :, a], 1.0, won[:], ALU.add, ALU.subtract))
                dve.tensor_tensor(rel[:], best[:], along(high[:], EXPERTS), ALU.subtract).then_inc(related, 1)
                done(dve.tensor_scalar(beaten[:], beaten[:], 2.0, None, ALU.is_lt))
                dve.wait_ge(exped, 1)
                done(dve.tensor_tensor(gate[:], gate[:], beaten[:], ALU.mult))
                done(dve.tensor_reduce(high[:], gate[:], AX.X, ALU.add))
                done(dve.reciprocal(high[:], high[:]))
                dve.tensor_tensor(gate[:], gate[:], along(high[:], EXPERTS), ALU.mult).then_inc(gated, 1)
                dve.wait_ge(gated, 1)
                with dve.Fori(0, NCH // SLOTS) as turn:
                    for s in range(SLOTS):
                        use = turn * (SLOTS // 2) + s // 2
                        if s % 2 == 0:
                            dve.wait_ge(y_in[s], (turn + 1) * 32)
                            dve.wait_ge(mixed, turn * SLOTS + s)
                            scale(dve, turn, s)
                        dve.wait_ge(scale_done[s % 2], use + 1)
                        dve.wait_ge(res_ready[s % 2], use)
                        dve.tensor_reduce(mix[s % 2][:], scaled[s % 2][:].rearrange("p j e c -> p j c e"), AX.X, ALU.add)\
                           .then_inc(mixed, 1)

            @block.gpsimd
            def _(pool):
                pool.wait_ge(gated, 1)

                def add(turn, s):
                    pool.wait_ge(y_in[s], (turn + 1) * 32)
                    pool.wait_ge(mixed, turn * SLOTS + s + 1)
                    pool.wait_ge(out_done[s], turn * 16)
                    pool.tensor_tensor(res[s][:], mix[s % 2][:], t2[s][:], ALU.add).then_inc(res_ready[s % 2], 1)

                with pool.Fori(0, NCH // SLOTS) as turn:
                    for s in range(0, SLOTS, 2):
                        pool.wait_ge(y_in[s + 1], (turn + 1) * 32)
                        pool.wait_ge(mixed, turn * SLOTS + s)
                        pool.sem_inc(passed, 1)
                        scale(pool, turn, s + 1)
                        add(turn, s)
                        add(turn, s + 1)

            @block.scalar
            def _(act):
                act.wait_ge(dropped, 1)
                act.activation(weight[:], drop[:], ACT.Exp).then_inc(weighed, 1)
                act.wait_ge(varied, 1)
                act.activation(stat[:, 2, :], stat[:, 1, :], ACT.Sqrt).then_inc(rooted, 1)
                act.wait_ge(related, 1)
                act.activation(gate[:], rel[:], ACT.Exp).then_inc(exped, 1)


def host_layout(inputs):
    f = lambda a: np.ascontiguousarray(a)
    g = lambda name: np.asarray(inputs[name])
    conv = lambda name: g("L0_conv_" + name)
    bn = lambda j: f(np.stack([conv(k + j).reshape(128) for k in ("B", "G", "Be", "M", "V")], axis=1))
    x = g("x")
    out = {
        "x": f(x),
        "x_ch": f(x.reshape(N, H * W, C).transpose(2, 0, 1)),
        "w1": f(conv("W1").transpose(1, 0, 2).reshape(C, 128)),
        "w2": f(conv("W2").transpose(0, 3, 1, 2, 4).reshape(128, 9, DP)),
        "w3": f(conv("W3").reshape(128, C)),
        "bn1": bn("1"), "bn2": bn("2"),
        "bn3": f(np.stack([conv(k + "3").reshape(CHUNKS, 128).T for k in ("B", "G", "Be", "M", "V")], axis=1)),
        "bn3e": f(np.stack([np.repeat(conv(k + "3"), DP, axis=0) for k in ("G", "V")], axis=1)),
        "wqkv": f(g("L1_attn_W_qkv").T),
        "temperature": f(g("L1_attn_temperature")),
        "ident": np.eye(128, dtype=np.float32),
        "pathmask": np.kron(np.eye(PATHS), np.ones((DP, 1))).astype(np.float32),
        "pair": np.tile(np.kron(np.eye(2), np.ones((DP, 1))), (CHUNKS, 1)).astype(np.float32),
        "fold": np.concatenate([np.eye(C)] * 2).astype(np.float32),
    }
    out["kfeat"], out["qfeat"] = mask_features()
    out["headmask"] = np.kron(np.eye(HEADS), np.ones((HD, 1))).astype(np.float32)
    out["wproj"] = f(g("L1_attn_W_proj").T)
    out["bproj"] = f(g("L1_attn_b_proj"))
    ffn = lambda name: g("L1_ffn_" + name)
    out["wgat"], out["att_src"], out["att_dst"] = f(ffn("W_gat")), f(ffn("att_src")), f(ffn("att_dst"))
    for name in ("b_gat", "ln_gamma", "ln_beta"):
        out[name] = f(ffn(name))
    out["ffn_w1"] = f(ffn("W1").transpose(1, 0, 2))
    out["ffn_b1"] = f(ffn("b1").T)
    out["ffn_w2"] = f(ffn("W2").transpose(1, 0, 2))
    out["ffn_b2"] = f(ffn("b2").reshape(1, EXPERTS * C))
    out["edges"] = f(ffn("edge_index"))
    out["psign"] = partition_signs()
    out["before"] = np.triu(np.ones((128, 128)), 1).astype(np.float32)
    out["iota"] = np.tile(np.arange(128), (128, 1)).astype(np.float32)
    out["last_pos"] = (np.arange(128)[:, None] * EF + EF - 1).astype(np.float32)
    return out


def build_program(nc, io, out):
    dram = lambda name, shape, dt=F32: nc.dram_tensor("scratch_" + name, shape, dt, kind="Internal").ap()
    t1 = dram("t1", [TOKENS, C]); t2 = dram("t2", [TOKENS, C])
    q = dram("q", [C, N, H * W]); kpad = dram("kpad", [C, N, PH, PW]); vpad = dram("vpad", [N, PH, PW, C])
    key = dram("key", [128, EF]); turned = dram("turned", [128, EF]); ordered = dram("ordered", [128, EF])
    z = dram("z", [C, TOKENS]); table = dram("table", [TOKENS, ROW]); adst = dram("adst", [TOKENS, GHEADS])
    digit = dram("digit", [NFC, 128, 2, FC]); edge = dram("edge", [NFC, 128, 4, FC]); node = dram("node", [2, 128, 128], I32)
    first = dram("first", [128, 1], I32); ends = dram("ends", [128, 2])
    b = dram("b", [EDGES, GHEADS]); state = dram("state", [EDGES, STATE]); sums = dram("sums", [TOKENS, STATE])
    y = dram("y", [TOKENS, EXPERTS * C])

    conv_phase(nc, io, t1, q, kpad, vpad, key, turned, ordered)
    attention_phase(nc, io, t1, q, kpad, vpad, t2)
    index_phase(nc, io, ordered, digit, edge, first, ends)
    table_phase(nc, io, t2, z, table, adst)
    edge_phase(nc, io, z, table, adst, digit, edge, node, first, b, state, y)
    join_phase(nc, io, state, node, first, ends, sums)
    output_phase(nc, io, table, adst, sums, y, t2, out)


def kernel(**inputs):
    from concourse import bacc
    from concourse.bass_utils import run_bass_kernel_spmd

    nc = bacc.Bacc("TRN2", target_bir_lowering=False, num_devices=1)
    arrays, io = {}, {}
    for name, a in host_layout(inputs).items():
        arrays["in_" + name] = a
        io[name] = nc.dram_tensor("in_" + name, a.shape, mybir.dt.from_np(a.dtype), kind="ExternalInput").ap()
    out = nc.dram_tensor("out", [N, H, W, C], F32, kind="ExternalOutput").ap()
    build_program(nc, io, out)
    result = run_bass_kernel_spmd(nc, [arrays], core_ids=[0])
    return result.results[0]["out"]
```
